# Optimizing a Trainium2 kernel written in Bass

```python
import numpy as np
import jax
import jax.numpy as jnp

def _softmax(x, axis=-1):
    return jax.nn.softmax(x, axis=axis)

def _gelu(x):
    return jax.nn.gelu(x, approximate=True)

def _silu(x):
    return jax.nn.silu(x)

def _sigmoid(x):
    return jax.nn.sigmoid(x)

def _layernorm(x, axis=-1, eps=1e-05):
    m = jnp.mean(x, axis=axis, keepdims=True)
    v = jnp.var(x, axis=axis, keepdims=True)
    return (x - m) / jnp.sqrt(v + eps)

def _scatter_add(tgt, idx, src, axis=0):
    return tgt.at[idx].add(src)

def _segment_sum(src, seg, n):
    return jax.ops.segment_sum(src, seg, n)
kernel_name = 'mk_recurrent_d1_jaxref_r8_fcbeb9'

def setup_inputs(seed: int=0):
    np.random.seed(seed)
    _w = jnp.asarray

    def _L0_attn_setup():
        import jax, jax.numpy as jnp
        import numpy as np
        import math
        D_MODEL = 128
        D_INNER = 256
        D_HALF = D_INNER // 2
        D_STATE = 16
        D_CONV = 4
        DT_RANK = 64
        B_SZ = 4
        L = 256

        def _dw_conv(x, w, b):
            y = jax.lax.conv_general_dilated(x, w, window_strides=(1,), padding='SAME', feature_group_count=x.shape[-1], dimension_numbers=('NWC', 'WIO', 'NWC'))
            return y + b

        def _selective_scan(u, delta, A, Bc, Cc, D):
            b, l, d = u.shape
            n = A.shape[1]

            def step(h, inp):
                d_t, u_t, B_t, C_t = inp
                dA = jnp.exp(d_t[..., None] * A)
                h = dA * h + (d_t * u_t)[..., None] * B_t[:, None, :]
                y = jnp.einsum('bdn,bn->bd', h, C_t)
                return (h, y)
            h0 = jnp.zeros((b, d, n), u.dtype)
            xs = (jnp.moveaxis(delta, 1, 0), jnp.moveaxis(u, 1, 0), jnp.moveaxis(Bc, 1, 0), jnp.moveaxis(Cc, 1, 0))
            _, ys = jax.lax.scan(step, h0, xs)
            return jnp.moveaxis(ys, 0, 1) + u * D
        key = jax.random.key(seed)
        ks = jax.random.split(key, 12)
        x = jax.random.normal(ks[0], (B_SZ, L, D_MODEL), jnp.float32)
        W_in = jax.random.normal(ks[1], (D_MODEL, D_INNER), jnp.float32) * D_MODEL ** (-0.5)
        conv_x_w = jax.random.normal(ks[2], (D_CONV, 1, D_HALF), jnp.float32) * D_CONV ** (-0.5)
        conv_x_b = jnp.zeros((D_HALF,), jnp.float32)
        conv_z_w = jax.random.normal(ks[3], (D_CONV, 1, D_HALF), jnp.float32) * D_CONV ** (-0.5)
        conv_z_b = jnp.zeros((D_HALF,), jnp.float32)
        W_xdbl = jax.random.normal(ks[4], (D_HALF, DT_RANK + 2 * D_STATE), jnp.float32) * D_HALF ** (-0.5)
        dt_init_std = DT_RANK ** (-0.5)
        W_dt = jax.random.uniform(ks[5], (DT_RANK, D_HALF), jnp.float32, -dt_init_std, dt_init_std)
        rand_vals = jax.random.uniform(ks[6], (D_HALF,))
        dt_bias = jnp.exp(rand_vals * (math.log(0.1) - math.log(0.001)) + math.log(0.001))
        dt_bias = jnp.clip(dt_bias, 0.0001)
        inv_dt = dt_bias + jnp.log(-jnp.expm1(-dt_bias))
        D = jnp.ones((D_HALF,), jnp.float32)
        W_out = jax.random.normal(ks[7], (D_INNER, D_MODEL), jnp.float32) * D_INNER ** (-0.5)
        b_out = jnp.zeros((D_MODEL,), jnp.float32)
        return dict(x=x, W_in=W_in, conv_x_w=conv_x_w, conv_x_b=conv_x_b, conv_z_w=conv_z_w, conv_z_b=conv_z_b, W_xdbl=W_xdbl, W_dt=W_dt, inv_dt=inv_dt, D=D, W_out=W_out, b_out=b_out)
    _L0_attn_in = _L0_attn_setup()

    def _L0_ffn_setup():
        import jax, jax.numpy as jnp
        import numpy as np
        DIM = 128
        DEPTH = 6
        HEADS = 16
        DIM_HEAD = 64
        WINDOW = 32
        INNER = HEADS * DIM_HEAD
        DIM_INNER = int(DIM * 4 * 2 / 3)
        QK_SCALE = 8.0

        def shift_tokens(t):
            a, s = jnp.split(t, 2, -1)
            s = jnp.pad(s, ((0, 0), (1, 0), (0, 0)))[:, :-1]
            return jnp.concatenate([a, s], -1)

        def l2norm(t):
            return t / jnp.maximum(jnp.linalg.norm(t, axis=-1, keepdims=True), 1e-12)

        def rotate_half(x):
            x1, x2 = jnp.split(x, 2, -1)
            return jnp.concatenate([-x2, x1], -1)

        def rotary_tables(n):
            half = jnp.arange(0, DIM_HEAD, 2, dtype=jnp.float32)
            inv_freq = 1.0 / 10000.0 ** (half / DIM_HEAD)
            t = jnp.arange(n, dtype=jnp.float32)
            freqs = t[:, None] * inv_freq[None, :]
            freqs = jnp.concatenate([freqs, freqs], -1)
            base_scale = (half + 0.4 * DIM_HEAD) / (1.4 * DIM_HEAD)
            power = (t - n // 2) / (WINDOW // 2)
            scale = base_scale[None, :] ** power[:, None]
            scale = jnp.concatenate([scale, scale], -1)
            return (freqs, scale)

        def local_attention(q, k, v):
            b, h, n, d = q.shape
            w = WINDOW
            nw = n // w
            bq = q.reshape(b, h, nw, w, d)
            bk = k.reshape(b, h, nw, w, d)
            bv = v.reshape(b, h, nw, w, d)

            def look(t):
                p = jnp.pad(t, ((0, 0), (0, 0), (1, 0), (0, 0), (0, 0)))
                return jnp.concatenate([p[:, :, :nw], p[:, :, 1:]], axis=3)
            bk2, bv2 = (look(bk), look(bv))
            seq = jnp.arange(n).reshape(nw, w)
            seq_p = jnp.pad(seq, ((1, 0), (0, 0)), constant_values=-1)
            jt = jnp.concatenate([seq_p[:nw], seq_p[1:]], axis=1)
            it = seq[:, :, None]
            jb = jt[:, None, :]
            mask = (it < jb) | (it > jb + w) | (jb == -1)
            sim = jnp.einsum('bhwie,bhwje->bhwij', bq, bk2) * QK_SCALE
            sim = jnp.where(mask, -jnp.finfo(sim.dtype).max, sim)
            attn = jax.nn.softmax(sim, -1)
            out = jnp.einsum('bhwij,bhwje->bhwie', attn, bv2)
            return out.reshape(b, h, n, d)

        def attn_layer(x, Wqkv, qs, ksc, Wo):
            b, n, _ = x.shape
            qkv = x @ Wqkv
            q, k, v = jnp.split(qkv, 3, -1)
            sh = lambda t: t.reshape(b, n, HEADS, DIM_HEAD).transpose(0, 2, 1, 3)
            q, k, v = (sh(q), sh(k), sh(v))
            q = l2norm(q) * qs
            k = l2norm(k) * ksc
            freqs, scale = rotary_tables(n)
            cos, sin = (jnp.cos(freqs), jnp.sin(freqs))
            q = q * cos * scale + rotate_half(q) * sin * scale
            inv = 1.0 / scale
            k = k * cos * inv + rotate_half(k) * sin * inv
            out = local_attention(q, k, v)
            out = out.transpose(0, 2, 1, 3).reshape(b, n, INNER)
            return out @ Wo

        def ffn_layer(x, g, bln, W1, b1, W2, b2):
            mu = x.mean(-1, keepdims=True)
            var = ((x - mu) ** 2).mean(-1, keepdims=True)
            xn = (x - mu) / jnp.sqrt(var + 1e-05) * g + bln
            hg = xn @ W1 + b1
            a, gate = jnp.split(hg, 2, -1)
            return a * jax.nn.gelu(gate, approximate=False) @ W2 + b2
        key = jax.random.key(seed)
        ks = jax.random.split(key, 8)
        B, N = (2, 256)
        init = lambda k, shape: jax.random.normal(k, shape, jnp.float32) * 0.02
        return {'x': jax.random.normal(ks[0], (B, N, DIM), jnp.float32), 'Wqkv': init(ks[1], (DEPTH, DIM, 3 * INNER)), 'q_scale': jnp.ones((DEPTH, DIM_HEAD), jnp.float32), 'k_scale': jnp.ones((DEPTH, DIM_HEAD), jnp.float32), 'Wo': init(ks[2], (DEPTH, INNER, DIM)), 'ln_g': jnp.ones((DEPTH, DIM), jnp.float32), 'ln_b': jnp.zeros((DEPTH, DIM), jnp.float32), 'W1': init(ks[3], (DEPTH, DIM, 2 * DIM_INNER)), 'b1': jnp.zeros((DEPTH, 2 * DIM_INNER), jnp.float32), 'W2': init(ks[4], (DEPTH, DIM_INNER, DIM)), 'b2': jnp.zeros((DEPTH, DIM), jnp.float32)}
    _L0_ffn_in = _L0_ffn_setup()
    _d = {'L0_attn_x': _L0_attn_in['x'], 'L0_attn_W_in': _L0_attn_in['W_in'], 'L0_attn_conv_x_w': _L0_attn_in['conv_x_w'], 'L0_attn_conv_x_b': _L0_attn_in['conv_x_b'], 'L0_attn_conv_z_w': _L0_attn_in['conv_z_w'], 'L0_attn_conv_z_b': _L0_attn_in['conv_z_b'], 'L0_attn_W_xdbl': _L0_attn_in['W_xdbl'], 'L0_attn_W_dt': _L0_attn_in['W_dt'], 'L0_attn_inv_dt': _L0_attn_in['inv_dt'], 'L0_attn_D': _L0_attn_in['D'], 'L0_attn_W_out': _L0_attn_in['W_out'], 'L0_attn_b_out': _L0_attn_in['b_out'], 'L0_ffn_Wqkv': _L0_ffn_in['Wqkv'], 'L0_ffn_q_scale': _L0_ffn_in['q_scale'], 'L0_ffn_k_scale': _L0_ffn_in['k_scale'], 'L0_ffn_Wo': _L0_ffn_in['Wo'], 'L0_ffn_ln_g': _L0_ffn_in['ln_g'], 'L0_ffn_ln_b': _L0_ffn_in['ln_b'], 'L0_ffn_W1': _L0_ffn_in['W1'], 'L0_ffn_b1': _L0_ffn_in['b1'], 'L0_ffn_W2': _L0_ffn_in['W2'], 'L0_ffn_b2': _L0_ffn_in['b2']}
    _x0 = _d['L0_attn_x']
    _d['L0_attn_x'] = jax.random.normal(jax.random.fold_in(jax.random.key(seed), 1), (16, 256, 128), dtype=_x0.dtype)
    del _x0
    return _d

def reference(L0_attn_x, L0_attn_W_in, L0_attn_conv_x_w, L0_attn_conv_x_b, L0_attn_conv_z_w, L0_attn_conv_z_b, L0_attn_W_xdbl, L0_attn_W_dt, L0_attn_inv_dt, L0_attn_D, L0_attn_W_out, L0_attn_b_out, L0_ffn_Wqkv, L0_ffn_q_scale, L0_ffn_k_scale, L0_ffn_Wo, L0_ffn_ln_g, L0_ffn_ln_b, L0_ffn_W1, L0_ffn_b1, L0_ffn_W2, L0_ffn_b2):

    def _L0_attn_ref(x, W_in, conv_x_w, conv_x_b, conv_z_w, conv_z_b, W_xdbl, W_dt, inv_dt, D, W_out, b_out):
        import jax, jax.numpy as jnp
        import numpy as np
        import math
        D_MODEL = 128
        D_INNER = 256
        D_HALF = D_INNER // 2
        D_STATE = 16
        D_CONV = 4
        DT_RANK = 64
        B_SZ = 4
        L = 256

        def _dw_conv(x, w, b):
            y = jax.lax.conv_general_dilated(x, w, window_strides=(1,), padding='SAME', feature_group_count=x.shape[-1], dimension_numbers=('NWC', 'WIO', 'NWC'))
            return y + b

        def _selective_scan(u, delta, A, Bc, Cc, D):
            b, l, d = u.shape
            n = A.shape[1]

            def step(h, inp):
                d_t, u_t, B_t, C_t = inp
                dA = jnp.exp(d_t[..., None] * A)
                h = dA * h + (d_t * u_t)[..., None] * B_t[:, None, :]
                y = jnp.einsum('bdn,bn->bd', h, C_t)
                return (h, y)
            h0 = jnp.zeros((b, d, n), u.dtype)
            xs = (jnp.moveaxis(delta, 1, 0), jnp.moveaxis(u, 1, 0), jnp.moveaxis(Bc, 1, 0), jnp.moveaxis(Cc, 1, 0))
            _, ys = jax.lax.scan(step, h0, xs)
            return jnp.moveaxis(ys, 0, 1) + u * D
        xz = x @ W_in
        xs, z = jnp.split(xz, 2, axis=-1)
        A = -jnp.tile(jnp.arange(1, D_STATE + 1, dtype=jnp.float32), (D_HALF, 1))
        xs = jax.nn.silu(_dw_conv(xs, conv_x_w, conv_x_b))
        z = jax.nn.silu(_dw_conv(z, conv_z_w, conv_z_b))
        x_dbl = xs @ W_xdbl
        dt_low, Bc, Cc = jnp.split(x_dbl, [DT_RANK, DT_RANK + D_STATE], axis=-1)
        dt = dt_low @ W_dt + inv_dt
        delta = jax.nn.softplus(dt + inv_dt)
        y = _selective_scan(xs, delta, A, Bc, Cc, D)
        y = jnp.concatenate([y, z], axis=-1)
        return y @ W_out + b_out

    def _L0_ffn_ref(x, Wqkv, q_scale, k_scale, Wo, ln_g, ln_b, W1, b1, W2, b2):
        import jax, jax.numpy as jnp
        import numpy as np
        DIM = 128
        DEPTH = 6
        HEADS = 16
        DIM_HEAD = 64
        WINDOW = 32
        INNER = HEADS * DIM_HEAD
        DIM_INNER = int(DIM * 4 * 2 / 3)
        QK_SCALE = 8.0

        def shift_tokens(t):
            a, s = jnp.split(t, 2, -1)
            s = jnp.pad(s, ((0, 0), (1, 0), (0, 0)))[:, :-1]
            return jnp.concatenate([a, s], -1)

        def l2norm(t):
            return t / jnp.maximum(jnp.linalg.norm(t, axis=-1, keepdims=True), 1e-12)

        def rotate_half(x):
            x1, x2 = jnp.split(x, 2, -1)
            return jnp.concatenate([-x2, x1], -1)

        def rotary_tables(n):
            half = jnp.arange(0, DIM_HEAD, 2, dtype=jnp.float32)
            inv_freq = 1.0 / 10000.0 ** (half / DIM_HEAD)
            t = jnp.arange(n, dtype=jnp.float32)
            freqs = t[:, None] * inv_freq[None, :]
            freqs = jnp.concatenate([freqs, freqs], -1)
            base_scale = (half + 0.4 * DIM_HEAD) / (1.4 * DIM_HEAD)
            power = (t - n // 2) / (WINDOW // 2)
            scale = base_scale[None, :] ** power[:, None]
            scale = jnp.concatenate([scale, scale], -1)
            return (freqs, scale)

        def local_attention(q, k, v):
            b, h, n, d = q.shape
            w = WINDOW
            nw = n // w
            bq = q.reshape(b, h, nw, w, d)
            bk = k.reshape(b, h, nw, w, d)
            bv = v.reshape(b, h, nw, w, d)

            def look(t):
                p = jnp.pad(t, ((0, 0), (0, 0), (1, 0), (0, 0), (0, 0)))
                return jnp.concatenate([p[:, :, :nw], p[:, :, 1:]], axis=3)
            bk2, bv2 = (look(bk), look(bv))
            seq = jnp.arange(n).reshape(nw, w)
            seq_p = jnp.pad(seq, ((1, 0), (0, 0)), constant_values=-1)
            jt = jnp.concatenate([seq_p[:nw], seq_p[1:]], axis=1)
            it = seq[:, :, None]
            jb = jt[:, None, :]
            mask = (it < jb) | (it > jb + w) | (jb == -1)
            sim = jnp.einsum('bhwie,bhwje->bhwij', bq, bk2) * QK_SCALE
            sim = jnp.where(mask, -jnp.finfo(sim.dtype).max, sim)
            attn = jax.nn.softmax(sim, -1)
            out = jnp.einsum('bhwij,bhwje->bhwie', attn, bv2)
            return out.reshape(b, h, n, d)

        def attn_layer(x, Wqkv, qs, ksc, Wo):
            b, n, _ = x.shape
            qkv = x @ Wqkv
            q, k, v = jnp.split(qkv, 3, -1)
            sh = lambda t: t.reshape(b, n, HEADS, DIM_HEAD).transpose(0, 2, 1, 3)
            q, k, v = (sh(q), sh(k), sh(v))
            q = l2norm(q) * qs
            k = l2norm(k) * ksc
            freqs, scale = rotary_tables(n)
            cos, sin = (jnp.cos(freqs), jnp.sin(freqs))
            q = q * cos * scale + rotate_half(q) * sin * scale
            inv = 1.0 / scale
            k = k * cos * inv + rotate_half(k) * sin * inv
            out = local_attention(q, k, v)
            out = out.transpose(0, 2, 1, 3).reshape(b, n, INNER)
            return out @ Wo

        def ffn_layer(x, g, bln, W1, b1, W2, b2):
            mu = x.mean(-1, keepdims=True)
            var = ((x - mu) ** 2).mean(-1, keepdims=True)
            xn = (x - mu) / jnp.sqrt(var + 1e-05) * g + bln
            hg = xn @ W1 + b1
            a, gate = jnp.split(hg, 2, -1)
            return a * jax.nn.gelu(gate, approximate=False) @ W2 + b2
        for i in range(DEPTH):
            x = attn_layer(shift_tokens(x), Wqkv[i], q_scale[i], k_scale[i], Wo[i]) + x
            x = ffn_layer(shift_tokens(x), ln_g[i], ln_b[i], W1[i], b1[i], W2[i], b2[i]) + x
        return x
    x = L0_attn_x
    xn = _layernorm(x, axis=-1)
    s = _L0_attn_ref(xn, L0_attn_W_in, L0_attn_conv_x_w, L0_attn_conv_x_b, L0_attn_conv_z_w, L0_attn_conv_z_b, L0_attn_W_xdbl, L0_attn_W_dt, L0_attn_inv_dt, L0_attn_D, L0_attn_W_out, L0_attn_b_out)
    g = _silu(_L0_ffn_ref(xn, L0_ffn_Wqkv, L0_ffn_q_scale, L0_ffn_k_scale, L0_ffn_Wo, L0_ffn_ln_g, L0_ffn_ln_b, L0_ffn_W1, L0_ffn_b1, L0_ffn_W2, L0_ffn_b2))
    x = x + s * g
    return x

_drawn_inputs = setup_inputs


def setup_inputs(seed=0):
    import zlib

    import numpy as np

    out = dict(_drawn_inputs(seed))
    spreads = {'L0_attn_conv_x_b': (0.0, 0.325),
     'L0_attn_conv_z_b': (0.0, 2.0),
     'L0_attn_D': (1.0, 0.6),
     'L0_attn_b_out': (0.0, 2.0),
     'L0_ffn_q_scale': (1.0, 0.6),
     'L0_ffn_k_scale': (1.0, 0.6),
     'L0_ffn_ln_g': (1.0, 0.6),
     'L0_ffn_ln_b': (0.0, 0.8),
     'L0_ffn_b1': (0.0, 0.8),
     'L0_ffn_b2': (0.0, 0.1)}
    factors = {'L0_attn_W_xdbl': 5.262,
     'L0_attn_W_dt': 8.0,
     'L0_attn_inv_dt': 7.51,
     'L0_ffn_W1': 5.052,
     'L0_ffn_W2': 4.97,
     'L0_attn_conv_z_w': 8.0}
    for name, (base, spread) in spreads.items():
        noise = np.random.default_rng([zlib.crc32(name.encode()), seed]).standard_normal(out[name].shape)
        drawn = base * np.exp(spread * noise) if base else spread * noise
        out[name] = jnp.asarray(drawn.astype(out[name].dtype))
    for name, factor in factors.items():
        out[name] = (out[name] * factor).astype(out[name].dtype)
    return out
```

```python
from contextlib import ExitStack

import numpy as np

import concourse.bass as bass
from concourse import mybir

ALU = mybir.AluOpType
ACT = mybir.ActivationFunctionType
AX_X = mybir.AxisListType.X
F32 = mybir.dt.float32
F32R = mybir.dt.float32r

P = 128
BATCH, SEQ, DIM = 16, 256, 128
TOKENS = BATCH * SEQ
GB = 2
GT = GB * SEQ
GROUPS = TOKENS // GT
TILES = TOKENS // P
DEPTH, HEADS, DH, WINDOW = 6, 16, 64, 32
INNER = HEADS * DH
PAIRS = HEADS // 2
FF = int(DIM * 4 * 2 / 3)
FCH = [(0, 128), (128, 128), (256, FF - 256)]
D_STATE, DT_RANK, D_CONV = 16, 64, 4
QK_SCALE = 8.0
MASKED = -1e30
R_LOG2 = 24
NBLK = 4 * PAIRS
STEPS = PAIRS * GB
UW = 2 * P + WINDOW
V_QS, V_QSW, V_KS, V_KSW, V_G, V_B, V_B2, V_B1A, V_B1G, NVEC = 0, 1, 2, 3, 4, 5, 6, 7, 10, 13
M_CXW, M_CZW, M_CXB, M_CZB, M_DT2, M_D, M_BO, NMV = 0, 4, 8, 9, 10, 11, 12, 13
ORDER = [0, 4, 1, 5, 2, 6, 3, 7]


def head_row(h):
    return h if h < 8 else 24 + h


def build(nc, x_in, W_in, W_xdbl, W_dt, W_out, mvec, Wqkv, Wo, W1, W2, lvec, tabs_c, mask_c, ident_c,
          headsum_c, headpick_c, statepick_c, out):
    ctx = ExitStack()
    with ctx:
        def sb(name, shape, dt=F32):
            return ctx.enter_context(nc.sbuf_tensor(name, shape, dt))

        def sem(name):
            return ctx.enter_context(nc.semaphore(name))

        xT = sb("xT", [P, TOKENS + GT])
        rot = sb("rot", [P, 2 * PAIRS, GT])
        wide = sb("wide", [P, PAIRS, GT])
        vtok = sb("vtok", [P, 4, INNER])
        wqk_h = sb("wqk_h", [P, NBLK, P], F32R)
        wqk_l = sb("wqk_l", [P, NBLK, P], F32R)
        wv_h = sb("wv_h", [P, INNER], F32R)
        wv_l = sb("wv_l", [P, INNER], F32R)
        w1_h = sb("w1_h", [P, 2 * FF], F32R)
        w1_l = sb("w1_l", [P, 2 * FF], F32R)
        w2_h = sb("w2_h", [P, 3, P], F32R)
        w2_l = sb("w2_l", [P, 3, P], F32R)
        wo = sb("wo", [P, PAIRS, P])
        xh = sb("xh", [P, GB, SEQ], F32R)
        xl = sb("xl", [P, GB, SEQ], F32R)
        ab = sb("ab", [P, 2, 2, GT])
        hh = sb("hh", [P, 2, GT], F32R)
        hl = sb("hl", [P, 2, GT], F32R)
        sm = sb("sm", [P, 2, 2, UW])
        pr = sb("pr", [P, 4, 2, UW])
        pt = sb("pt", [P, 3, 2, 2 * P])
        pp = sb("pp", [P, 3, 2, WINDOW])
        tab = sb("tab", [P, 4, SEQ])
        ltab = sb("ltab", [P, 4, SEQ])
        mask = sb("mask", [P, UW])
        ident = sb("ident", [P, P])
        headsum = sb("headsum", [P, 4, 32])
        headpick = sb("headpick", [P, PAIRS, P], F32R)
        mean_w = sb("mean_w", [P, P])
        rsum = sb("rsum", [P, GT])
        rq = sb("rq", [P, 4, 64])
        nrq = sb("nrq", [P, 4, 64])
        mx = sb("mx", [P, STEPS, 2, 2])
        nb = sb("nb", [P, STEPS, 2, 2])
        den = sb("den", [P, STEPS, 2, 2])
        rden = sb("rden", [P, STEPS, 2, 2])
        lv_all = sb("lv_all", [P, DEPTH * NVEC])
        lv = sb("lv", [P, NVEC])
        mv = sb("mv", [P, NMV])
        st = sb("st", [P, 4, TILES])
        eps = sb("eps", [P, 1])
        bank = [ctx.enter_context(nc.psum_tensor(f"bank{i}", [P, GT], F32)) for i in range(8)]
        s_dram = nc.dram_tensor("s_scratch", (P, TOKENS), F32, kind="Internal").ap()

        rotw = rot[:, :, :].rearrange("p a n -> p (a n)")
        wide_f = wide[:, :, :].rearrange("p a n -> p (a n)")
        vt_f = vtok[:, :, :].rearrange("p a n -> p (a n)")
        xtok = rotw[:, 0:TOKENS].rearrange("p (t c) -> p t c", c=DIM)
        xsq = rotw[:, TOKENS:2 * TOKENS].rearrange("p (t c) -> p t c", c=DIM)
        statepick = vt_f[:, 0:32 * P].rearrange("p (n c) -> p n c", c=P)
        w_in = ab[:, 0, 0, 0:2 * P]
        w_xdbl = ab[:, 0, 1, 0:DT_RANK + 2 * D_STATE]
        w_dt = ab[:, 1, 0, 0:P]
        w_out = ab[:, 1, 1, 0:2 * P]
        PADW = SEQ + D_CONV - 1
        pad_x = sm[:, 0, :, 0:PADW]
        pad_z = sm[:, 1, :, 0:PADW]
        ct = [rot[:, i, :] for i in range(4)]
        u, z_act, xd, delta, du, acc, yy, dtmp = (rot[:, 4 + i, :] for i in range(8))
        dA = [rot[:, 12 + i, :] for i in range(2)]
        dBu = [rot[:, 14 + i, :] for i in range(2)]
        hst = [wide[:, i, :] for i in range(2)]
        hC = [wide[:, 2 + i, :] for i in range(2)]
        sp = [wide[:, 4 + i, :] for i in range(2)]
        s_out = wide[:, 6, :]
        raw_qkv = rotw[:, 0:3 * INNER]
        raw_wo = rotw[:, 3 * INNER:4 * INNER].rearrange("p (t c) -> p t c", c=P)
        raw_w1 = rotw[:, 4 * INNER:4 * INNER + 2 * FF]
        raw_w2 = rotw[:, 4 * INNER + 2 * FF:4 * INNER + 2 * FF + 3 * P].rearrange("p (t c) -> p t c", c=P)

        consts_in = sem("consts_in")
        xtok_in = sem("xtok_in")
        link = {e: sem(f"{e}_link") for e in ("dve", "act")}
        ln0_mean = sem("ln0_mean")
        ln0_sq = sem("ln0_sq")
        ln0_var = sem("ln0_var")
        ln0_rstd = sem("ln0_rstd")
        ln0_xn = sem("ln0_xn")
        ln0_tr = sem("ln0_tr")
        ln0_xT = sem("ln0_xT")
        consts_made = sem("consts_made")
        m_proj, m_pad, m_conv, m_silu, m_xdbl, m_xd = (sem(f"m_{n}") for n in ("proj", "pad", "conv", "silu", "xdbl", "xd"))
        m_dt, m_soft, m_soft2, m_softl, m_delta, m_B, m_C = (
            sem(f"m_{n}") for n in ("dt", "soft", "soft2", "softl", "delta", "B", "C"))
        m_dA, m_dBu, m_scan, m_hC, m_acc, m_y, m_s, m_sout, m_sdma = (
            sem(f"m_{n}") for n in ("dA", "dBu", "scan", "hC", "acc", "y", "s", "sout", "sdma"))
        m_x, m_cv, m_rl, m_du = (sem(f"m_{n}") for n in ("x", "cv", "rl", "du"))
        w_in_sem = sem("w_loaded")
        w_hi, w_lo = sem("w_hi"), sem("w_lo")
        lvec_ok = sem("lvec_ok")
        x_hi, x_split = sem("x_hi"), sem("x_split")
        qk_proj, qk_sq, qk_mul, qk_rot = sem("qk_proj"), sem("qk_sq"), sem("qk_mul"), sem("qk_rot")
        sq_part, sq_clamp, r_ln, r_exp, r_hi, r_split = (
            sem(n) for n in ("sq_part", "sq_clamp", "r_ln", "r_exp", "r_hi", "r_split"))
        v_proj, v_sb = sem("v_proj"), sem("v_sb")
        rq_T, rq_sb = sem("rq_T"), sem("rq_sb")
        rk_bc, k_norm = sem("rk_bc"), sem("k_norm")
        sc_ps, sc_max, sc_bias, p_exp, p_rden, p_norm, p_T, p_Tsb, o_ps, o_sb = (
            sem(n) for n in ("sc_ps", "sc_max", "sc_bias", "p_exp", "p_rden", "p_norm", "p_T", "p_Tsb", "o_ps", "o_sb"))
        at_out, at_add = sem("at_out"), sem("at_add")
        l_sh, l_mean, l_xc, l_sq, l_var, l_ln, l_rstd, l_mul, l_xn = (
            sem(n) for n in ("l_sh", "l_mean", "l_xc", "l_sq", "l_var", "l_ln", "l_rstd", "l_mul", "l_xn"))
        f_hi, f_split, f_up, f_gelu, f_h, f_hhi, f_hlo, f_dn, f_add = (
            sem(n) for n in ("f_hi", "f_split", "f_up", "f_gelu", "f_h", "f_hhi", "f_hlo", "f_dn", "f_add"))
        s_in = sem("s_in")
        g_silu, g_mul, g_T, g_out, out_dma = (sem(n) for n in ("g_silu", "g_mul", "g_T", "g_out", "out_dma"))

        NCONST = 12
        FFS = 2 * len(FCH)
        block = ctx.enter_context(nc.Block())

        def three_pass(eng, o, wh, wl, ah, al):
            eng.matmul(o, wh, ah, start=True, stop=False)
            eng.matmul(o, wl, ah, start=False, stop=False)
            return eng.matmul(o, wh, al, start=False, stop=True)

        def settle(eng):
            eng.wait_ge(consts_made, 1)

        def seqs(ap):
            return ap.rearrange("p (b t) -> p b t", b=GB)

        @block.sync
        def _(sp_e):
            sp_e.dma_start(xtok, x_in.rearrange("b (t p) c -> p (b t) c", p=P)).then_inc(xtok_in, 16)
            for dst, src in ((ident[:, :], ident_c), (w_in, W_in), (mv[:, :], mvec),
                             (w_xdbl, W_xdbl), (w_dt[0:DT_RANK, :], W_dt),
                             (w_out[:, :].rearrange("p (t c) -> p t c", t=2), W_out.rearrange("(t p) c -> p t c", p=P)),
                             (statepick[64:96, :, :], statepick_c), (lv_all[:, :], lvec),
                             (tab[:, :, :], tabs_c), (mask[:, :], mask_c), (headsum[:, :, :], headsum_c),
                             (wide[:, 0:2, :].rearrange("p a n -> p (a n)").rearrange("p (t c) -> p t c", c=P), headpick_c)):
                sp_e.dma_start(dst, src).then_inc(consts_in, 16)
            with sp_e.Fori(0, GROUPS) as g:
                sp_e.wait_ge(m_sout, g + 1)
                sp_e.dma_start(s_dram[:, bass.ds(g * GT, GT)], s_out).then_inc(m_sdma, 16)
            sp_e.wait_ge(m_sdma, 16 * GROUPS)
            with sp_e.Fori(0, DEPTH) as l:
                sp_e.wait_ge(at_out, l * GROUPS)
                sp_e.dma_start(raw_qkv, Wqkv[bass.ds(l, 1), :, :].rearrange("l p n -> p (l n)")).then_inc(w_in_sem, 16)
                sp_e.dma_start(raw_wo, Wo[bass.ds(l, 1), :, :].rearrange("l (t p) c -> p (l t) c", p=P)).then_inc(w_in_sem, 16)
                sp_e.dma_start(raw_w1, W1[bass.ds(l, 1), :, :].rearrange("l p n -> p (l n)")).then_inc(w_in_sem, 16)
                sp_e.dma_start(raw_w2[:, 0:2, :], W2[bass.ds(l, 1), 0:256, :].rearrange("l (t p) c -> p (l t) c", p=P))\
                    .then_inc(w_in_sem, 16)
                sp_e.dma_start(raw_w2[0:FCH[2][1], 2:3, :], W2[bass.ds(l, 1), 256:FF, :].rearrange("l p c -> p l c"))\
                    .then_inc(w_in_sem, 16)
            sp_e.wait_ge(at_out, DEPTH * GROUPS)
            sp_e.dma_start(xtok, x_in.rearrange("b (t p) c -> p (b t) c", p=P)).then_inc(s_in, 16)
            sp_e.dma_start(rotw[:, TOKENS:2 * TOKENS], s_dram[:, :]).then_inc(s_in, 16)
            ov = out.rearrange("b (t p) c -> p (b t) c", p=P)
            with sp_e.Fori(0, GROUPS) as g:
                sp_e.wait_ge(g_out, g + 1)
                sp_e.dma_start(ov[:, bass.ds(g * 4, 4), :], xtok[:, bass.ds(g * 4, 4), :]).then_inc(out_dma, 16)
            sp_e.wait_ge(out_dma, 16 * GROUPS)

        @block.tensor
        def _(pe):
            pe.wait_ge(consts_in, 16 * NCONST)
            pe.wait_ge(ln0_xn, 1)
            for t in range(TILES):
                if t >= 16 and t % 4 == 0:
                    pe.wait_ge(ln0_xT, t // 4 - 3)
                mm = pe.transpose(bank[t // 4 % 4][:, t % 4 * P:t % 4 * P + P], xtok[:, t, :], ident[:, :])
                if t % 4 == 3:
                    mm.then_inc(ln0_tr, 1)
            pe.wait_ge(ln0_xT, GROUPS)
            with pe.Fori(0, GROUPS) as g:
                pe.wait_ge(m_x, g + 1)
                pe.wait_ge(m_sout, g)
                pe.matmul(bank[0][:, :], w_in[:, 0:P], dtmp, start=True, stop=True).then_inc(m_proj, 1)
                pe.matmul(bank[1][:, :], w_in[:, P:2 * P], dtmp, start=True, stop=True).then_inc(m_proj, 1)
                pe.wait_ge(m_silu, g * 2 + 1)
                pe.matmul(bank[2][0:96, :], w_xdbl, u, start=True, stop=True).then_inc(m_xdbl, 1)
                pe.wait_ge(m_xd, g + 1)
                pe.matmul(bank[3][:, :], w_dt[0:DT_RANK, :], xd[0:DT_RANK, :], start=True, stop=True).then_inc(m_dt, 1)
                for n in range(D_STATE):
                    if n >= 2:
                        pe.wait_ge(m_dBu, g * D_STATE + n - 1)
                    pe.matmul(bank[4 + n % 2][:, :], statepick[64:96, n, :], xd[64:96, :], start=True, stop=True)\
                        .then_inc(m_B, 1)
                    if n >= 2:
                        pe.wait_ge(m_hC, g * D_STATE + n - 1)
                    pe.matmul(bank[6 + n % 2][:, :], statepick[64:96, D_STATE + n, :], xd[64:96, :],
                              start=True, stop=True).then_inc(m_C, 1)
                pe.wait_ge(m_y, g + 1)
                pe.wait_ge(m_silu, g * 2 + 2)
                pe.matmul(bank[2][:, :], w_out[:, 0:P], yy, start=True, stop=False)
                pe.matmul(bank[2][:, :], w_out[:, P:2 * P], z_act, start=False, stop=True).then_inc(m_s, 1)
            pe.wait_ge(consts_made, 1)
            pe.wait_ge(m_sout, GROUPS)
            with pe.Fori(0, DEPTH) as l:
                with pe.Fori(0, GROUPS) as g:
                    it = pe.snap(l * GROUPS + g)
                    it8 = pe.snap(it * 8)
                    it16 = pe.snap(it * 16)
                    pe.wait_ge(w_hi, l + 1)
                    pe.wait_ge(w_lo, l + 1)
                    pe.wait_ge(x_split, l * (GROUPS + 1) + (g + 1))
                    xhf = xh[:, :, :].rearrange("p b t -> p (b t)")
                    xlf = xl[:, :, :].rearrange("p b t -> p (b t)")

                    def square_sums(j):
                        p, isk = ORDER[j // 2], j % 2
                        t = 2 * isk + p // 4
                        return pe.matmul(bank[6][32 * t:32 * t + 32, :], headsum[:, p % 4, :], wide[:, j % 8, :],
                                         start=(p % 4 == 0), stop=(p % 4 == 3), skip_group_check=True)

                    for j in range(16):
                        p, isk = ORDER[j // 2], j % 2
                        slot = 2 * (j % 3)
                        if j >= 3:
                            pe.wait_ge(qk_mul, it16 + (j - 2))
                            pe.wait_ge(qk_sq, it16 + (j - 2))
                        for half in range(2):
                            blk = PAIRS * (2 * half + isk) + p
                            mm = three_pass(pe, bank[slot + half][:, :], wqk_h[:, blk, :], wqk_l[:, blk, :], xhf, xlf)
                        mm.then_inc(qk_proj, 1)
                        if j % 4 == 1 and j >= 5:
                            pe.wait_ge(qk_sq, it16 + (j - 1))
                            for i in range(j - 5, j - 1):
                                mm = square_sums(i)
                            mm.then_inc(sq_part, 1)
                    for v in range(8):
                        t, c = v // 2, v % 2
                        vb = (7, 2, 3)[v % 3]
                        if v == 0:
                            pe.wait_ge(at_add, it)
                        if v == 1:
                            pe.wait_ge(qk_mul, it16 + 14)
                            pe.wait_ge(qk_sq, it16 + 14)
                        if v >= 3:
                            pe.wait_ge(v_sb, it8 + (v - 2))
                        cols = slice(c * 512, c * 512 + 512)
                        b, tt = t // 2, t % 2
                        xa = xh[:, b, tt * P:tt * P + P]
                        three_pass(pe, bank[vb][:, :], xa, xl[:, b, tt * P:tt * P + P], wv_h[:, cols], wv_l[:, cols])\
                            .then_inc(v_proj, 1)
                        if v == 1:
                            pe.wait_ge(qk_sq, it16 + 16)
                            for i in range(12, 16):
                                mm = square_sums(i)
                            mm.then_inc(sq_part, 1)
                    pe.wait_ge(r_split, it + 1)
                    pe.wait_ge(qk_mul, it16 + 16)
                    pe.wait_ge(qk_sq, it16 + 16)
                    for p in range(PAIRS):
                        rb = (0, 1, 4, 5)[p % 4]
                        if p >= 4:
                            pe.wait_ge(k_norm, it8 + (p - 3))
                        pe.matmul(bank[rb][:, :], headpick[:, p, :], hh[:, 0, :], start=True, stop=False)
                        pe.matmul(bank[rb][:, :], headpick[:, p, :], hl[:, 0, :], start=False, stop=True)\
                            .then_inc(rk_bc, 1)
                        if p == 3:
                            pe.wait_ge(v_sb, it8 + 8)
                            for t in range(4):
                                mm = pe.transpose(bank[7][:, t * P:t * P + P], rsum[:, t * P:t * P + P], ident[:, :])
                            mm.then_inc(rq_T, 1)
                    pe.wait_ge(k_norm, it8 + 8)
                    pe.wait_ge(sq_clamp, it + 1)
                    for s in range(STEPS + 5):
                        if s < STEPS:
                            p, b = s // 2, s % 2
                            if s >= 2:
                                pe.wait_ge(sc_max, it16 + (s - 1))
                            for i in range(2):
                                o = bank[2 * (s % 2) + i]
                                rows = slice(64 * i, 64 * i + 64)
                                c0 = b * SEQ
                                pe.matmul(o[:, 0:P], rot[rows, p, c0:c0 + P], rot[rows, PAIRS + p, c0:c0 + P],
                                          start=True, stop=True)
                                mm = pe.matmul(o[:, P:UW], rot[rows, p, c0 + P:c0 + SEQ],
                                               rot[rows, PAIRS + p, c0 + P - WINDOW:c0 + SEQ], start=True, stop=True)
                            mm.then_inc(sc_ps, 1)
                        if 0 <= s - 3 < STEPS:
                            e = s - 3
                            pe.wait_ge(p_norm, it16 + (e + 1))
                            if e >= 2:
                                pe.wait_ge(p_Tsb, it16 + (e - 1))
                            for i in range(2):
                                o = bank[4 + e % 2]
                                pe.transpose(o[:, 256 * i:256 * i + P], pr[:, e % 4, i, 0:P], ident[:, :])
                                mm = pe.transpose(o[:, 256 * i + P:256 * i + 2 * P], pr[:, e % 4, i, P + WINDOW:UW],
                                                  ident[:, :])
                            mm.then_inc(p_T, 1)
                        if 0 <= s - 5 < STEPS:
                            e = s - 5
                            p, b = e // 2, e % 2
                            pe.wait_ge(p_Tsb, it16 + (e + 1))
                            if e >= 1:
                                pe.wait_ge(o_sb, it16 + e)
                            for i in range(2):
                                o = bank[6][64 * i:64 * i + 64, :]
                                ch = slice((2 * p + i) * DH, (2 * p + i) * DH + DH)
                                pe.matmul(o[:, 0:P], vtok[:, 2 * b, ch], pt[:, e % 3, i, 0:P], start=True, stop=True)
                                pe.matmul(o[:, P:2 * P], vtok[:, 2 * b + 1, ch], pt[:, e % 3, i, P:2 * P],
                                          start=True, stop=True)
                                mm = pe.matmul(o[:, P:P + WINDOW], vtok[96:128, 2 * b, ch], pp[96:128, e % 3, i, :],
                                               start=False, stop=True, skip_group_check=True)
                            mm.then_inc(o_ps, 1)
                    pe.wait_ge(o_sb, it16 + 16)
                    pe.wait_ge(rq_sb, it + 1)
                    for p in range(PAIRS):
                        mm = pe.matmul(bank[7][:, :], wo[:, p, :], wide[:, p, :], start=(p == 0), stop=(p == PAIRS - 1))
                    mm.then_inc(at_out, 1)
                with pe.Fori(0, GROUPS // 2) as g2:
                    i2 = pe.snap((l * (GROUPS // 2) + g2) * 2)
                    for k in range(2):
                        pe.wait_ge(l_sh, i2 + (k + 1))
                        pe.matmul(bank[k][:, :], mean_w[:, :], ab[:, k, 0, :], start=True, stop=True).then_inc(l_mean, 1)
                    for k in range(2):
                        pe.wait_ge(l_sq, i2 + (k + 1))
                        pe.matmul(bank[2 + k][:, :], mean_w[:, :], ab[:, k, 1, :], start=True, stop=True).then_inc(l_var, 1)
                with pe.Fori(0, GROUPS // 2) as g2:
                    i2 = pe.snap((l * (GROUPS // 2) + g2) * 2)
                    i6 = pe.snap(i2 * len(FCH))
                    for s in range(FFS + 2):
                        if s < FFS:
                            k, c = s // 3, s % 3
                            c0, cn = FCH[c]
                            if c == 0:
                                pe.wait_ge(f_split, i2 + (k + 1))
                            if s >= 3:
                                pe.wait_ge(f_h, i6 + (s - 2))
                            xhf = (xh, hh)[0][:, :, :].rearrange("p b t -> p (b t)")
                            xlf = xl[:, :, :].rearrange("p b t -> p (b t)")
                            o = 2 * (s % 3)
                            three_pass(pe, bank[o][0:cn, :], w1_h[:, c0:c0 + cn], w1_l[:, c0:c0 + cn], xhf, xlf)
                            three_pass(pe, bank[o + 1][0:cn, :], w1_h[:, FF + c0:FF + c0 + cn],
                                       w1_l[:, FF + c0:FF + c0 + cn], xhf, xlf).then_inc(f_up, 1)
                        if s >= 2:
                            e = s - 2
                            k, c = e // 3, e % 3
                            cn = FCH[c][1]
                            pe.wait_ge(f_hlo, i6 + (e + 1))
                            if c == 0:
                                pe.wait_ge(f_add, i2 if k == 0 else i2)
                            o = bank[6 + k][:, :]
                            pe.matmul(o, w2_h[0:cn, c, :], hh[0:cn, e % 2, :], start=(c == 0), stop=False)
                            pe.matmul(o, w2_l[0:cn, c, :], hh[0:cn, e % 2, :], start=False, stop=False)
                            mm = pe.matmul(o, w2_h[0:cn, c, :], hl[0:cn, e % 2, :], start=False, stop=(c == 2))
                            mm.then_inc(f_dn, 1)
            with pe.Fori(0, GROUPS) as g:
                pe.wait_ge(g_mul, g + 1)
                pe.wait_ge(g_out, g)
                for t in range(4):
                    mm = pe.transpose(bank[0][:, t * P:t * P + P], ab[:, 1, 0, t * P:t * P + P], ident[:, :])
                mm.then_inc(g_T, 1)

        @block.scalar
        def _(act):
            act.wait_ge(ln0_mean, 1)
            act.activation(xsq, xtok, ACT.Square).then_inc(ln0_sq, 1)
            act.wait_ge(ln0_var, 1)
            act.activation(st[:, 2, :], st[:, 1, :], ACT.Ln).then_inc(link["act"], 1)
            act.wait_ge(link["act"], 1)
            act.activation(st[:, 3, :], st[:, 2, :], ACT.Exp, scale=-0.5).then_inc(ln0_rstd, 1)
            act.wait_ge(consts_in, 16 * NCONST)
            act.wait_ge(consts_made, 1)
            with act.Fori(0, GROUPS) as g:
                for i, pad in enumerate((pad_x, pad_z)):
                    act.wait_ge(m_proj, g * 2 + (i + 1))
                    act.wait_ge(m_conv, g * 2)
                    act.activation(pad[:, :, 1:1 + SEQ], seqs(bank[i][:, :]), ACT.Copy).then_inc(m_pad, 1)
                for i, o in enumerate((u, z_act)):
                    act.wait_ge(m_conv, g * 2 + (i + 1))
                    act.wait_ge(m_s, g)
                    act.activation(o, ct[i], ACT.Silu).then_inc(m_silu, 1)
                act.wait_ge(m_dt, g + 1)
                act.activation(sp[0], bank[3][:, :], ACT.Abs, bias=mv[:, M_DT2:M_DT2 + 1]).then_inc(m_soft, 1)
                act.wait_ge(m_soft, g + 1)
                act.activation(sp[1], sp[0], ACT.Exp, scale=-1.0).then_inc(m_soft2, 1)
                act.wait_ge(m_soft2, g + 1)
                act.activation(sp[0], sp[1], ACT.Ln, bias=1.0).then_inc(m_softl, 1)
                act.wait_ge(m_delta, g + 1)
                for n in range(D_STATE):
                    if n >= 2:
                        act.wait_ge(m_scan, g * D_STATE + (n - 1))
                    act.activation(dA[n % 2], delta, ACT.Exp, scale=-float(n + 1)).then_inc(m_dA, 1)
                act.wait_ge(m_s, g + 1)
                act.wait_ge(m_sdma, g * 16)
                act.activation(s_out, bank[2][:, :], ACT.Identity, bias=mv[:, M_BO:M_BO + 1]).then_inc(m_sout, 1)
            with act.Fori(0, DEPTH) as l:
                act.wait_ge(w_in_sem, l * 80 + 80)
                act.wait_ge(f_dn, l * (GROUPS * 3))
                act.activation(wqk_h[:, 0:2 * PAIRS, :].rearrange("p a c -> p (a c)"), raw_qkv[:, 0:2 * INNER], ACT.Copy)
                for s in range(2):
                    dst = wqk_h[:, 2 * PAIRS:NBLK, :].rearrange("p a (h s i) -> p (a h) s i", s=2, i=32)[:, :, s, :]
                    src = raw_qkv[:, 0:2 * INNER].rearrange("p (h s i) -> p h s i", s=2, i=32)[:, :, 1 - s, :]
                    act.activation(dst, src, ACT.Copy)
                act.activation(wv_h[:, :], raw_qkv[:, 2 * INNER:3 * INNER], ACT.Copy)
                act.activation(w1_h[:, :], raw_w1, ACT.Copy)
                act.activation(w2_h[:, 0:2, :], raw_w2[:, 0:2, :], ACT.Copy)
                act.activation(w2_h[0:FCH[2][1], 2, :], raw_w2[0:FCH[2][1], 2, :], ACT.Copy)
                act.activation(wo[:, :, :], raw_wo, ACT.Copy).then_inc(w_hi, 1)
                act.wait_ge(w_lo, l + 1)
                with act.Fori(0, GROUPS) as g:
                    it = act.snap(l * GROUPS + g)
                    it8 = act.snap(it * 8)
                    it16 = act.snap(it * 16)
                    act.wait_ge(at_out, it)
                    for j in range(16):
                        act.wait_ge(qk_proj, it16 + (j + 1))
                        if j >= 8 and j % 4 == 0:
                            act.wait_ge(sq_part, it * 4 + (j // 4 - 1))
                        act.activation(wide[:, j % 8, :], bank[2 * (j % 3)][:, :], ACT.Square).then_inc(qk_sq, 1)
                    for v in range(8):
                        t, c = v // 2, v % 2
                        act.wait_ge(v_proj, it8 + (v + 1))
                        act.activation(vtok[:, t, c * 512:c * 512 + 512], bank[(7, 2, 3)[v % 3]][:, :], ACT.Copy)\
                            .then_inc(v_sb, 1)
                        if v == 4:
                            act.wait_ge(sq_clamp, it + 1)
                            act.activation(rsum[:, :], rsum[:, :], ACT.Ln, scale=float(2 ** R_LOG2)).then_inc(r_ln, 1)
                            act.wait_ge(r_ln, it + 1)
                            act.activation(rsum[:, :], rsum[:, :], ACT.Exp, scale=-0.5).then_inc(r_exp, 1)
                    for s in range(STEPS + 5):
                        if s < STEPS:
                            p, b = s // 2, s % 2
                            act.wait_ge(sc_bias, it16 + (s + 1))
                            if s >= 4:
                                act.wait_ge(p_T, it16 + (s - 3))
                                act.wait_ge(p_Tsb, it16 + (s - 3))
                            for i in range(2):
                                col = head_row(2 * p + i)
                                for t in range(2):
                                    cs = slice(0, P) if t == 0 else slice(P, UW)
                                    ins = act.activation(pr[:, s % 4, i, cs], sm[:, s % 2, i, cs], ACT.Exp,
                                                         bias=nb[:, s, t, i:i + 1], scale=rq[:, 2 * b + t, col:col + 1],
                                                         accum_out=den[:, s, t, i:i + 1])
                            ins.then_inc(p_exp, 1)
                        if s >= 5:
                            e = s - 5
                            p, b = e // 2, e % 2
                            act.wait_ge(o_ps, it16 + (e + 1))
                            act.activation(wide[:, p, b * SEQ:b * SEQ + SEQ], bank[6][:, 0:SEQ], ACT.Copy)\
                                .then_inc(o_sb, 1)
                with act.Fori(0, GROUPS // 2) as g2:
                    i2 = act.snap((l * (GROUPS // 2) + g2) * 2)
                    for k in range(2):
                        act.wait_ge(l_xc, i2 + (k + 1))
                        act.activation(ab[:, k, 1, :], ab[:, k, 0, :], ACT.Square).then_inc(l_sq, 1)
                    for k in range(2):
                        act.wait_ge(l_var, i2 + (k + 1))
                        act.activation(ab[:, k, 1, :], bank[2 + k][:, :], ACT.Ln, bias=eps[:, 0:1]).then_inc(l_ln, 1)
                        act.wait_ge(l_ln, i2 + (k + 1))
                        act.activation(ab[:, k, 1, :], ab[:, k, 1, :], ACT.Exp, scale=-0.5).then_inc(l_rstd, 1)
                with act.Fori(0, GROUPS // 2) as g2:
                    i2 = act.snap((l * (GROUPS // 2) + g2) * 2)
                    i6 = act.snap(i2 * len(FCH))
                    for s in range(FFS):
                        k, c = s // 3, s % 3
                        cn = FCH[c][1]
                        act.wait_ge(f_up, i6 + (s + 1))
                        act.wait_ge(f_h, i6 + max(s - 1, 0))
                        act.activation(ab[0:cn, s % 2, 0, :], bank[2 * (s % 3) + 1][0:cn, :], ACT.Gelu,
                                       bias=lv[0:cn, V_B1G + c:V_B1G + c + 1]).then_inc(f_gelu, 1)
                        act.wait_ge(f_h, i6 + (s + 1))
                        act.wait_ge(f_dn, i6 + max(s - 1, 0))
                        act.activation(hh[0:cn, s % 2, :], ab[0:cn, s % 2, 1, :], ACT.Copy).then_inc(f_hhi, 1)
            with act.Fori(0, GROUPS) as g:
                act.wait_ge(f_add, DEPTH * GROUPS)
                act.wait_ge(g_mul, g)
                act.activation(ab[:, 0, 0, :], xT[:, bass.ds(g * GT, GT)], ACT.Silu).then_inc(g_silu, 1)

        @block.gpsimd
        def _(pool):
            with pool.Fori(0, GROUPS) as g:
                for n in range(1, D_STATE):
                    pool.wait_ge(m_hC, g * D_STATE + (n + 1))
                    if n > 1:
                        pool.wait_ge(m_acc, g * (D_STATE - 1) + (n - 1))
                    pool.tensor_tensor(acc, hC[0] if n == 1 else acc, hC[n % 2], ALU.add).then_inc(m_acc, 1)
            with pool.Fori(0, DEPTH) as l:
                with pool.Fori(0, GROUPS) as g:
                    it16 = pool.snap((l * GROUPS + g) * 16)
                    for j in range(16):
                        p, isk = ORDER[j // 2], j % 2
                        pool.wait_ge(qk_mul, it16 + (j + 1))
                        pool.tensor_tensor(rot[:, PAIRS * isk + p, :], ab[:, j % 2, 0, :], ab[:, j % 2, 1, :], ALU.add)\
                            .then_inc(qk_rot, 1)
                    for s in range(STEPS):
                        settle(pool)
                        pool.wait_ge(p_rden, it16 + (s + 1))
                        for i in range(2):
                            for t in range(2):
                                cs = slice(0, P) if t == 0 else slice(P, UW)
                                ins = pool.tensor_scalar(pr[:, s % 4, i, cs], pr[:, s % 4, i, cs],
                                                         rden[:, s, t, i:i + 1], 1.0, ALU.mult, ALU.mult)
                        ins.then_inc(p_norm, 1)

        @block.vector
        def _(dve):
            chain = [0]

            def linked(ins):
                chain[0] += 1
                ins.then_inc(link["dve"], 1)
                dve.wait_ge(link["dve"], chain[0])

            dve.memset(mean_w[:, :], 1.0 / DIM)
            dve.memset(eps[:, :], 1e-5)
            dve.memset(xT[:, TOKENS:], 0.0)
            for pad in (pad_x, pad_z):
                dve.memset(pad[:, :, 0:1], 0.0)
                dve.memset(pad[:, :, 1 + SEQ:PADW], 0.0)
            dve.wait_ge(xtok_in, 16)
            linked(dve.tensor_reduce(st[:, 0, :], xtok, AX_X, ALU.add))
            linked(dve.tensor_scalar(st[:, 1, :], st[:, 0, :], 1.0 / DIM, None, ALU.mult))
            dve.tensor_tensor(xtok, xtok, st[:, 1, :].unsqueeze(2).to_broadcast([P, TILES, DIM]), ALU.subtract)\
                .then_inc(ln0_mean, 1)
            dve.wait_ge(ln0_sq, 1)
            linked(dve.tensor_reduce(st[:, 0, :], xsq, AX_X, ALU.add))
            dve.tensor_scalar(st[:, 1, :], st[:, 0, :], 1.0 / DIM, 1e-5, ALU.mult, ALU.add).then_inc(ln0_var, 1)
            dve.wait_ge(ln0_rstd, 1)
            dve.tensor_tensor(xtok, xtok, st[:, 3, :].unsqueeze(2).to_broadcast([P, TILES, DIM]), ALU.mult)\
                .then_inc(ln0_xn, 1)
            for q in range(GROUPS):
                dve.wait_ge(ln0_tr, q + 1)
                dve.tensor_copy(xT[:, q * GT:q * GT + GT], bank[q % 4][:, :]).then_inc(ln0_xT, 1)
            dve.wait_ge(consts_in, 16 * NCONST)
            dve.tensor_copy(headpick[:, :, :],
                            wide[:, 0:2, :].rearrange("p a n -> p (a n)").rearrange("p (t c) -> p t c", c=P))
            dve.tensor_scalar(mv[:, M_DT2:M_DT2 + 1], mv[:, M_DT2:M_DT2 + 1], 2.0, None, ALU.mult).then_inc(consts_made, 1)
            dve.wait_ge(consts_made, 1)
            dve.wait_ge(ln0_xT, GROUPS)
            with dve.Fori(0, GROUPS) as g:
                g16 = dve.snap(g * D_STATE)
                dve.wait_ge(m_s, g)
                dve.tensor_copy(dtmp, xT[:, bass.ds(g * GT, GT)]).then_inc(m_x, 1)
                for i, (pad, w0, b0) in enumerate(((pad_x, M_CXW, M_CXB), (pad_z, M_CZW, M_CZB))):
                    dve.wait_ge(m_pad, g * 2 + (i + 1))
                    dve.tensor_scalar(seqs(ct[2 + i]), pad[:, :, 0:SEQ], mv[:, w0:w0 + 1], mv[:, b0:b0 + 1],
                                      ALU.mult, ALU.add).then_inc(m_cv, 1)
                    for k in range(1, D_CONV):
                        src, dst = (ct[2 + i], ct[i]) if k % 2 else (ct[i], ct[2 + i])
                        dve.wait_ge(m_cv, g * 6 + (i * 3 + k))
                        ins = dve.scalar_tensor_tensor(seqs(dst), pad[:, :, k:k + SEQ], mv[:, w0 + k:w0 + k + 1],
                                                       seqs(src), ALU.mult, ALU.add)
                        ins.then_inc(m_cv if k < D_CONV - 1 else m_conv, 1)
                dve.wait_ge(m_xdbl, g + 1)
                dve.tensor_copy(xd[0:96, :], bank[2][0:96, :]).then_inc(m_xd, 1)
                dve.wait_ge(m_dt, g + 1)
                dve.wait_ge(m_soft, g + 1)
                dve.tensor_scalar(delta, bank[3][:, :], mv[:, M_DT2:M_DT2 + 1], 0.0, ALU.add, ALU.max).then_inc(m_rl, 1)
                dve.wait_ge(m_softl, g + 1)
                dve.wait_ge(m_rl, g + 1)
                dve.tensor_tensor(delta, delta, sp[0], ALU.add).then_inc(m_delta, 1)
                dve.wait_ge(m_delta, g + 1)
                dve.tensor_tensor(du, delta, u, ALU.mult).then_inc(m_du, 1)
                dve.wait_ge(m_du, g + 1)

                def emit(n):
                    dve.wait_ge(m_C, g16 + (n + 1))
                    dve.wait_ge(m_scan, g16 + (n + 1))
                    if n >= 2:
                        dve.wait_ge(m_acc, g * (D_STATE - 1) + max(1, n - 2))
                    dve.tensor_tensor(hC[n % 2], hst[n % 2], bank[6 + n % 2][:, :], ALU.mult).then_inc(m_hC, 1)

                for n in range(D_STATE):
                    dve.wait_ge(m_B, g16 + (n + 1))
                    if n >= 2:
                        dve.wait_ge(m_hC, g16 + (n - 1))
                    dve.tensor_tensor(dBu[n % 2], du, bank[4 + n % 2][:, :], ALU.mult).then_inc(m_dBu, 1)
                    if n >= 1:
                        emit(n - 1)
                    dve.wait_ge(m_dBu, g16 + (n + 1))
                    dve.wait_ge(m_dA, g16 + (n + 1))
                    for b in range(GB):
                        cs = slice(b * SEQ, b * SEQ + SEQ)
                        ins = dve.tensor_tensor_scan(hst[n % 2][:, cs], dA[n % 2][:, cs], dBu[n % 2][:, cs], 0.0,
                                                     ALU.mult, ALU.add)
                    ins.then_inc(m_scan, 1)
                emit(D_STATE - 1)
                dve.wait_ge(m_acc, (g + 1) * (D_STATE - 1))
                dve.scalar_tensor_tensor(yy, u, mv[:, M_D:M_D + 1], acc, ALU.mult, ALU.add).then_inc(m_y, 1)
            dve.wait_ge(m_sout, GROUPS)
            with dve.Fori(0, DEPTH) as l:
                dve.wait_ge(w_in_sem, l * 80 + 80)
                dve.wait_ge(w_hi, l + 1)
                dve.wait_ge(f_add, l * GROUPS)
                dve.tensor_tensor(wqk_l[:, 0:2 * PAIRS, :].rearrange("p a c -> p (a c)"), raw_qkv[:, 0:2 * INNER],
                                  wqk_h[:, 0:2 * PAIRS, :].rearrange("p a c -> p (a c)").bitcast(F32), ALU.subtract)
                for s in range(2):
                    def swapped(w):
                        return w[:, 2 * PAIRS:NBLK, :].rearrange("p a (h s i) -> p (a h) s i", s=2, i=32)[:, :, s, :]
                    src = raw_qkv[:, 0:2 * INNER].rearrange("p (h s i) -> p h s i", s=2, i=32)[:, :, 1 - s, :]
                    dve.tensor_tensor(swapped(wqk_l), src, swapped(wqk_h).bitcast(F32), ALU.subtract)
                dve.tensor_tensor(wv_l[:, :], raw_qkv[:, 2 * INNER:3 * INNER], wv_h[:, :].bitcast(F32), ALU.subtract)
                dve.tensor_tensor(w1_l[:, :], raw_w1, w1_h[:, :].bitcast(F32), ALU.subtract)
                n2 = FCH[2][1]
                dve.tensor_tensor(w2_l[:, 0:2, :], raw_w2[:, 0:2, :], w2_h[:, 0:2, :].bitcast(F32), ALU.subtract)
                dve.tensor_tensor(w2_l[0:n2, 2, :], raw_w2[0:n2, 2, :], w2_h[0:n2, 2, :].bitcast(F32), ALU.subtract)\
                    .then_inc(w_lo, 1)
                dve.tensor_copy(lv[:, :], lv_all[:, bass.ds(l * NVEC, NVEC)]).then_inc(lvec_ok, 1)
                dve.wait_ge(lvec_ok, l * 2 + 1)
                for i, c in enumerate((V_QS, V_QSW, V_KS, V_KSW)):
                    ins = dve.tensor_scalar(ltab[:, i, :], tab[:, i, :], lv[:, c:c + 1], None, ALU.mult)
                ins.then_inc(lvec_ok, 1)
                dve.wait_ge(lvec_ok, l * 2 + 2)

                def split_x(g, count):
                    xlo = seqs(xT[0:64, bass.ds(g * GT, GT)])
                    xhi = seqs(xT[64:128, bass.ds(g * GT, GT)])
                    dve.tensor_copy(xh[0:64, :, :], xlo)
                    dve.tensor_copy(xh[64:128, :, 1:SEQ], xhi[:, :, 0:SEQ - 1]).then_inc(x_hi, 1)
                    dve.wait_ge(x_hi, l * (GROUPS + 1) + count)
                    dve.tensor_tensor(xl[0:64, :, :], xlo, xh[0:64, :, :].bitcast(F32), ALU.subtract)
                    dve.tensor_tensor(xl[64:128, :, 1:SEQ], xhi[:, :, 0:SEQ - 1], xh[64:128, :, 1:SEQ].bitcast(F32),
                                      ALU.subtract).then_inc(x_split, 1)

                dve.memset(xh[64:128, :, 0:1].bitcast(F32), 0.0)
                dve.memset(xl[64:128, :, 0:1].bitcast(F32), 0.0)
                split_x(0, 1)
                with dve.Fori(0, GROUPS) as g:
                    it = dve.snap(l * GROUPS + g)
                    it8 = dve.snap(it * 8)
                    it16 = dve.snap(it * 16)

                    def group_x():
                        return xT[:, bass.ds(g * GT, GT)]

                    for j in range(16):
                        isk = j % 2
                        dve.wait_ge(qk_proj, it16 + (j + 1))
                        if j >= 2:
                            dve.wait_ge(qk_rot, it16 + (j - 1))
                        for half in (1, 0):
                            if half == 0:
                                dve.wait_ge(qk_sq, it16 + (j + 1))
                            tb = ltab[:, 2 * isk + half:2 * isk + half + 1, :].to_broadcast([P, GB, SEQ])
                            ins = dve.tensor_tensor(seqs(ab[:, j % 2, half, :]), seqs(bank[2 * (j % 3) + half][:, :]),
                                                    tb, ALU.mult)
                        ins.then_inc(qk_mul, 1)
                    dve.wait_ge(sq_part, it * 4 + 4)
                    dve.tensor_scalar(rsum[:, :], bank[6][:, :], 1e-24, None, ALU.max).then_inc(sq_clamp, 1)
                    dve.wait_ge(r_exp, it + 1)
                    dve.tensor_copy(hh[:, 0, :], rsum[:, :]).then_inc(r_hi, 1)
                    dve.wait_ge(r_hi, it + 1)
                    dve.tensor_tensor(hl[:, 0, :], rsum[:, :], hh[:, 0, :].bitcast(F32), ALU.subtract).then_inc(r_split, 1)
                    dve.wait_ge(qk_rot, it16 + 16)
                    for p in range(PAIRS):
                        dve.wait_ge(rk_bc, it8 + (p + 1))
                        rb = (0, 1, 4, 5)[p % 4]
                        dve.tensor_tensor(rot[:, PAIRS + p, :], rot[:, PAIRS + p, :], bank[rb][:, :], ALU.mult)\
                            .then_inc(k_norm, 1)
                    dve.wait_ge(rq_T, it + 1)
                    b7 = bank[7][:, :].rearrange("p (t r) -> p t r", t=4)[:, :, 0:64]
                    up = float(2 ** (R_LOG2 // 2)) * QK_SCALE
                    dve.tensor_scalar(rq[:, :, :], b7, up, None, ALU.mult)
                    dve.tensor_scalar(nrq[:, :, :], b7, -up, None, ALU.mult).then_inc(rq_sb, 1)
                    rq_n = dve.snap(it + 1)
                    settle(dve)
                    dve.wait_ge(rq_sb, rq_n)

                    for s in range(STEPS + 4):
                        if s < STEPS:
                            p, b = s // 2, s % 2
                            settle(dve)
                            dve.wait_ge(sc_ps, it16 + (s + 1))
                            if s >= 2:
                                dve.wait_ge(p_exp, it16 + (s - 1))
                            for i in range(2):
                                for t in range(2):
                                    cs = slice(0, P) if t == 0 else slice(P, UW)
                                    ins = dve.tensor_tensor_reduce(
                                        sm[:, s % 2, i, cs], bank[2 * (s % 2) + i][:, cs], mask[:, cs], 1.0, -3e38,
                                        ALU.add, ALU.max, mx[:, s, t, i:i + 1])
                            ins.then_inc(sc_max, 1)
                            dve.wait_ge(sc_max, it16 + (s + 1))
                            col = head_row(2 * p)
                            dve.tensor_tensor(nb[:, s, :, :], mx[:, s, :, :], nrq[:, 2 * b:2 * b + 2, col:col + 2],
                                              ALU.mult).then_inc(sc_bias, 1)
                        if 0 <= s - 2 < STEPS:
                            e = s - 2
                            dve.wait_ge(p_exp, it16 + (e + 1))
                            dve.reciprocal(rden[:, e, :, :], den[:, e, :, :]).then_inc(p_rden, 1)
                        if 0 <= s - 4 < STEPS:
                            e = s - 4
                            dve.wait_ge(p_T, it16 + (e + 1))
                            if e >= 3:
                                dve.wait_ge(o_ps, it16 + (e - 2))
                            dve.transpose(pp[96:128, e % 3, :, :], pr[0:32, e % 4, :, P:P + WINDOW])
                            dve.tensor_copy(pt[:, e % 3, :, :].rearrange("p i c -> p (i c)"), bank[4 + e % 2][:, :])\
                                .then_inc(p_Tsb, 1)
                    split_x(g + 1, g + 2)
                    dve.wait_ge(at_out, it + 1)
                    dve.tensor_tensor(group_x(), group_x(), bank[7][:, :], ALU.add).then_inc(at_add, 1)
                with dve.Fori(0, GROUPS // 2) as g2:
                    i2 = dve.snap((l * (GROUPS // 2) + g2) * 2)
                    for k in range(2):
                        xlo = seqs(xT[0:64, bass.ds((g2 * 2 + k) * GT, GT)])
                        xhi = seqs(xT[64:128, bass.ds((g2 * 2 + k) * GT, GT)])
                        a0 = ab[:, k, 0, :]
                        dve.wait_ge(at_add, (l + 1) * GROUPS)
                        dve.wait_ge(l_xn, i2)
                        dve.memset(seqs(a0)[64:128, :, 0:1], 0.0)
                        dve.tensor_copy(seqs(a0)[0:64, :, :], xlo)
                        dve.tensor_copy(seqs(a0)[64:128, :, 1:SEQ], xhi[:, :, 0:SEQ - 1]).then_inc(l_sh, 1)
                    for k in range(2):
                        dve.wait_ge(l_mean, i2 + (k + 1))
                        dve.wait_ge(l_sh, i2 + (k + 1))
                        dve.tensor_tensor(ab[:, k, 0, :], ab[:, k, 0, :], bank[k][:, :], ALU.subtract).then_inc(l_xc, 1)
                    for k in range(2):
                        dve.wait_ge(l_rstd, i2 + (k + 1))
                        dve.wait_ge(l_xc, i2 + (k + 1))
                        dve.tensor_tensor(ab[:, k, 0, :], ab[:, k, 0, :], ab[:, k, 1, :], ALU.mult).then_inc(l_mul, 1)
                    for k in range(2):
                        dve.wait_ge(l_mul, i2 + (k + 1))
                        dve.tensor_scalar(wide_f[:, bass.ds((g2 * 2 + k) * GT, GT)], ab[:, k, 0, :],
                                          lv[:, V_G:V_G + 1], lv[:, V_B:V_B + 1], ALU.mult, ALU.add).then_inc(l_xn, 1)
                with dve.Fori(0, GROUPS // 2) as g2:
                    i2 = dve.snap((l * (GROUPS // 2) + g2) * 2)
                    i6 = dve.snap(i2 * len(FCH))

                    def split(k):
                        src = wide_f[:, bass.ds((g2 * 2 + k) * GT, GT)]
                        dve.wait_ge(l_xn, (l + 1) * GROUPS)
                        dve.wait_ge(f_up, i6 + 3 * k)
                        dve.tensor_copy(xh[:, :, :], seqs(src)).then_inc(f_hi, 1)
                        dve.wait_ge(f_hi, i2 + (k + 1))
                        dve.tensor_tensor(xl[:, :, :], seqs(src), xh[:, :, :].bitcast(F32), ALU.subtract)\
                            .then_inc(f_split, 1)

                    def low(s):
                        cn = FCH[s % 3][1]
                        dve.wait_ge(f_hhi, i6 + (s + 1))
                        dve.tensor_tensor(hl[0:cn, s % 2, :], ab[0:cn, s % 2, 1, :], hh[0:cn, s % 2, :].bitcast(F32),
                                          ALU.subtract).then_inc(f_hlo, 1)

                    def residual(k):
                        dve.wait_ge(f_dn, i6 + (3 * k + 3))
                        dst = xT[:, bass.ds((g2 * 2 + k) * GT, GT)]
                        dve.scalar_tensor_tensor(dst, bank[6 + k][:, :], lv[:, V_B2:V_B2 + 1], dst, ALU.add, ALU.add)\
                            .then_inc(f_add, 1)

                    split(0)
                    for s in range(FFS):
                        c = s % 3
                        cn = FCH[c][1]
                        if s == 3:
                            split(1)
                        dve.wait_ge(f_gelu, i6 + (s + 1))
                        if s >= 2:
                            dve.wait_ge(f_hlo, i6 + (s - 1))
                        dve.scalar_tensor_tensor(ab[0:cn, s % 2, 1, :], bank[2 * (s % 3)][0:cn, :],
                                                 lv[0:cn, V_B1A + c:V_B1A + c + 1], ab[0:cn, s % 2, 0, :],
                                                 ALU.add, ALU.mult).then_inc(f_h, 1)
                        low(s)
                    residual(0)
                    residual(1)
            dve.wait_ge(s_in, 32)
            with dve.Fori(0, GROUPS) as g:
                dve.wait_ge(g_silu, g + 1)
                dve.wait_ge(g_T, g)
                dve.tensor_tensor(ab[:, 1, 0, :], ab[:, 0, 0, :], rotw[:, bass.ds(TOKENS + g * GT, GT)], ALU.mult)\
                    .then_inc(g_mul, 1)
                dve.wait_ge(g_T, g + 1)
                dst = rotw[:, bass.ds(g * GT, GT)]
                dve.tensor_tensor(dst, dst, bank[0][:, :], ALU.add).then_inc(g_out, 1)


def constants():
    half = np.arange(0, DH, 2, dtype=np.float32)
    inv_freq = (np.float32(1.0) / np.float32(10000.0) ** (half / np.float32(DH))).astype(np.float32)
    t = np.arange(SEQ, dtype=np.float32)
    freqs = t[:, None] * inv_freq[None, :]
    base = (half + np.float32(0.4 * DH)) / np.float32(1.4 * DH)
    power = (t - SEQ // 2) / np.float32(WINDOW // 2)
    scale = (base[None, :] ** power[:, None]).astype(np.float32)
    f = np.tile(freqs, (1, 4)).T
    s = np.tile(scale, (1, 4)).T
    sign = np.where(np.arange(P) % DH < DH // 2, -1.0, 1.0).astype(np.float32)[:, None]
    inv = (np.float32(1.0) / s).astype(np.float32)
    tabs = np.stack([np.cos(f) * s, np.sin(f) * s * sign, np.cos(f) * inv, np.sin(f) * inv * sign], 1)
    q = np.arange(P)[:, None]
    own = np.arange(P)[None, :]
    wide = np.arange(P + WINDOW)[None, :] - WINDOW

    def band(k):
        return np.where((k > q) | (k < q - WINDOW), MASKED, 0.0)

    mask = np.concatenate([band(own), band(wide)], 1)
    headsum = np.zeros((P, 4, 32))
    headpick = np.zeros((P, PAIRS, P))
    for p in range(4):
        for i in range(2):
            headsum[64 * i:64 * i + 64, p, 2 * p + i] = 1.0
    for p in range(PAIRS):
        for i in range(2):
            headpick[64 + head_row(2 * p + i), p, 64 * i:64 * i + 64] = 2.0 ** (R_LOG2 // 2)
    statepick = np.zeros((2 * D_STATE, 2 * D_STATE, P))
    for n in range(2 * D_STATE):
        statepick[n, n, :] = 1.0
    return {k: np.ascontiguousarray(v.astype(np.float32)) for k, v in dict(
        tabs_c=tabs, mask_c=mask, ident_c=np.eye(P), headsum_c=headsum, headpick_c=headpick,
        statepick_c=statepick).items()}


def columns(*vectors):
    cols = []
    for v in vectors:
        c = np.zeros((P,), np.float32)
        c[:v.shape[0]] = v
        cols.append(c)
    return np.stack(cols, 1)


def kernel(**inputs):
    import concourse.bacc as bacc
    from concourse.bass_utils import run_bass_kernel_spmd as run

    i = {k: np.asarray(v) for k, v in inputs.items()}
    A, F = "L0_attn_", "L0_ffn_"
    cxw, czw = i[A + "conv_x_w"][:, 0, :], i[A + "conv_z_w"][:, 0, :]
    mvec = columns(*[cxw[k] for k in range(D_CONV)], *[czw[k] for k in range(D_CONV)], i[A + "conv_x_b"],
                   i[A + "conv_z_b"], i[A + "inv_dt"], i[A + "D"], i[A + "b_out"])
    swap = np.r_[DH // 2:DH, 0:DH // 2]
    lay = []
    for l in range(DEPTH):
        qs, ks, b1 = i[F + "q_scale"][l], i[F + "k_scale"][l], i[F + "b1"][l]
        lay.append(columns(np.tile(qs, 2), np.tile(qs[swap], 2), np.tile(ks, 2), np.tile(ks[swap], 2),
                           i[F + "ln_g"][l], i[F + "ln_b"][l], i[F + "b2"][l],
                           *[b1[c0:c0 + cn] for c0, cn in FCH], *[b1[FF + c0:FF + c0 + cn] for c0, cn in FCH]))
    arrays = dict(x_in=i[A + "x"], W_in=i[A + "W_in"], W_xdbl=i[A + "W_xdbl"], W_dt=i[A + "W_dt"],
                  W_out=i[A + "W_out"], mvec=mvec, Wqkv=i[F + "Wqkv"], Wo=i[F + "Wo"], W1=i[F + "W1"],
                  W2=i[F + "W2"], lvec=np.concatenate(lay, 1), **constants())
    arrays = {k: np.ascontiguousarray(v) for k, v in arrays.items()}
    nc = bacc.Bacc("TRN2", target_bir_lowering=False, num_devices=1)
    aps = {n: nc.dram_tensor(n, a.shape, mybir.dt.from_np(a.dtype), kind="ExternalInput").ap()
           for n, a in arrays.items()}
    out = nc.dram_tensor("out", (BATCH, SEQ, DIM), F32, kind="ExternalOutput").ap()
    build(nc, **aps, out=out)
    r = run(nc, [arrays], core_ids=[0])
    return r.results[0]["out"]
```

```python
from contextlib import ExitStack

import numpy as np

import concourse.bass as bass
from concourse import mybir

ALU = mybir.AluOpType
ACT = mybir.ActivationFunctionType
AX_X = mybir.AxisListType.X
F32 = mybir.dt.float32
F32R = mybir.dt.float32r

P = 128
BATCH, SEQ, DIM = 16, 256, 128
TOKENS = BATCH * SEQ
GB = 2
GT = GB * SEQ
GROUPS = TOKENS // GT
TILES = TOKENS // P
DEPTH, HEADS, DH, WINDOW = 6, 16, 64, 32
INNER = HEADS * DH
PAIRS = HEADS // 2
FF = int(DIM * 4 * 2 / 3)
FCH = [(0, 128), (128, 128), (256, FF - 256)]
D_STATE, DT_RANK, D_CONV = 16, 64, 4
QK_SCALE = 8.0
MASKED = -1e30
R_LOG2 = 24
NBLK = 2 * PAIRS
STEPS = PAIRS * GB
UW = 2 * P + WINDOW
V_QS, V_KS, V_G, V_B, V_B2, V_B1A, V_B1G, NVEC = 0, 1, 2, 3, 4, 5, 8, 11
M_CXW, M_CZW, M_CXB, M_CZB, M_DT2, M_D, M_BO, NMV = 0, 4, 8, 9, 10, 11, 12, 13
CREDIT = 1
VCH = 4
VW = INNER // VCH
BANK_USES = [("qk", 0), ("qk", 1), ("qk", 2), ("qk", 3), ("qk", 4), ("qk", 5), ("qk", 6), ("v", 0), ("qk", 7),
             ("qk", 8), ("v", 1), ("qk", 9), ("qk", 10), ("v", 2), ("qk", 11), ("qk", 12), ("v", 3), ("rqT", 0),
             ("qk", 13), ("rk", 0), ("qk", 14), ("rk", 1), ("qk", 15), ("rk", 2), ("v", 4), ("rk", 3), ("v", 5),
             ("v", 6), ("v", 7), ("rqT", 1), ("rk", 4), ("rk", 5), ("rk", 6), ("rk", 7)]
TURN = 23
V_STEPS = (9, 11, 13, 15, 19, 20, 21, 22)


def build(nc, x_in, W_in, W_xdbl, W_dt, W_out, mvec, Wqkv, Wo, W1, W2, lvec, tabs_c, mask_c, ident_c,
          headsum_c, headpick_c, statepick_c, out):
    ctx = ExitStack()
    with ctx:
        def sb(name, shape, dt=F32):
            return ctx.enter_context(nc.sbuf_tensor(name, shape, dt))

        def sem(name):
            return ctx.enter_context(nc.semaphore(name))

        xT = sb("xT", [P, TOKENS + GT])
        rot = sb("rot", [P, 2 * PAIRS, GT])
        wide = sb("wide", [P, PAIRS, GT])
        sq = sb("sq", [P, 4, GT])
        vtok = sb("vtok", [P, 4, INNER])
        wqk_h = sb("wqk_h", [P, NBLK, P], F32R)
        wqk_l = sb("wqk_l", [P, NBLK, P], F32R)
        wv_h = sb("wv_h", [P, INNER], F32R)
        wv_l = sb("wv_l", [P, INNER], F32R)
        w1_h = sb("w1_h", [P, 2 * FF], F32R)
        w1_l = sb("w1_l", [P, 2 * FF], F32R)
        w2_h = sb("w2_h", [P, 3, P], F32R)
        w2_l = sb("w2_l", [P, 3, P], F32R)
        wo = sb("wo", [P, PAIRS, P])
        xh = sb("xh", [P, GB, SEQ], F32R)
        xl = sb("xl", [P, GB, SEQ], F32R)
        ab = sb("ab", [P, 3, 2, GT])
        swp = sb("swp", [P, 3, GT])
        hh = sb("hh", [P, 2, GT], F32R)
        hl = sb("hl", [P, 2, GT], F32R)
        sm = sb("sm", [P, 2, 2, UW])
        pr = sb("pr", [P, 4, 2, UW])
        pt = sb("pt", [P, 3, 2, 2 * P])
        pp = sb("pp", [P, 3, 2, WINDOW])
        nh = sb("nh", [P, GT], F32R)
        nl = sb("nl", [P, GT], F32R)
        tab = sb("tab", [P, 4, SEQ])
        ltab = sb("ltab", [P, 4, SEQ])
        mask = sb("mask", [P, UW])
        ident = sb("ident", [P, P])
        headsum = sb("headsum", [P, 4, 32])
        headpick = sb("headpick", [P, 4, P], F32R)
        mean_w = sb("mean_w", [P, P])
        rsum = sb("rsum", [P, GT])
        rq = sb("rq", [P, 2, 4, 8])
        nrq = sb("nrq", [P, 2, 4, 8])
        credit = sb("credit", [P, 64])
        mx = sb("mx", [P, STEPS, 2, 2])
        nb = sb("nb", [P, STEPS, 2, 2])
        den = sb("den", [P, STEPS, 2, 2])
        rden = sb("rden", [P, STEPS, 2, 2])
        lv_all = sb("lv_all", [P, DEPTH * NVEC])
        lv = sb("lv", [P, NVEC])
        mv = sb("mv", [P, NMV])
        st = sb("st", [P, 4, TILES])
        eps = sb("eps", [P, 1])
        bank = [ctx.enter_context(nc.psum_tensor(f"bank{i}", [P, GT], F32)) for i in range(8)]
        s_dram = nc.dram_tensor("s_scratch", (P, TOKENS), F32, kind="Internal").ap()

        rotw = rot[:, :, :].rearrange("p a n -> p (a n)")
        wide_f = wide[:, :, :].rearrange("p a n -> p (a n)")
        vt_f = vtok[:, :, :].rearrange("p a n -> p (a n)")
        xtok = rotw[:, 0:TOKENS].rearrange("p (t c) -> p t c", c=DIM)
        xsq = rotw[:, TOKENS:2 * TOKENS].rearrange("p (t c) -> p t c", c=DIM)
        statepick = vt_f[:, 0:32 * P].rearrange("p (n c) -> p n c", c=P)
        w_in = ab[:, 0, 0, 0:2 * P]
        w_xdbl = ab[:, 0, 1, 0:DT_RANK + 2 * D_STATE]
        w_dt = ab[:, 1, 0, 0:P]
        w_out = ab[:, 1, 1, 0:2 * P]
        PADW = SEQ + D_CONV - 1
        pad_x = sm[:, 0, :, 0:PADW]
        pad_z = sm[:, 1, :, 0:PADW]
        ct = [rot[:, i, :] for i in range(4)]
        u, z_act, xd, delta, du, acc, yy, dtmp = (rot[:, 4 + i, :] for i in range(8))
        dA = [rot[:, 12 + i, :] for i in range(2)]
        dBu = [rot[:, 14 + i, :] for i in range(2)]
        hst = [wide[:, i, :] for i in range(2)]
        hC = [wide[:, 2 + i, :] for i in range(2)]
        sp = [wide[:, 4 + i, :] for i in range(2)]
        s_out = wide[:, 6, :]
        raw_qkv = rotw[:, 0:3 * INNER]
        raw_wo = rotw[:, 3 * INNER:4 * INNER].rearrange("p (t c) -> p t c", c=P)
        raw_w1 = rotw[:, 4 * INNER:4 * INNER + 2 * FF]
        raw_w2 = rotw[:, 4 * INNER + 2 * FF:4 * INNER + 2 * FF + 3 * P].rearrange("p (t c) -> p t c", c=P)

        consts_in = sem("consts_in")
        xtok_in = sem("xtok_in")
        link = {e: sem(f"{e}_link") for e in ("dve", "act")}
        ln0_mean = sem("ln0_mean")
        ln0_sq = sem("ln0_sq")
        ln0_var = sem("ln0_var")
        ln0_rstd = sem("ln0_rstd")
        ln0_xn = sem("ln0_xn")
        ln0_tr = sem("ln0_tr")
        ln0_xT = sem("ln0_xT")
        consts_made = sem("consts_made")
        m_proj, m_pad, m_conv, m_silu, m_xdbl, m_xd = (sem(f"m_{n}") for n in ("proj", "pad", "conv", "silu", "xdbl", "xd"))
        m_dt, m_soft, m_soft2, m_softl, m_delta, m_B, m_C = (
            sem(f"m_{n}") for n in ("dt", "soft", "soft2", "softl", "delta", "B", "C"))
        m_dA, m_dBu, m_scan, m_hC, m_acc, m_y, m_s, m_sout, m_sdma = (
            sem(f"m_{n}") for n in ("dA", "dBu", "scan", "hC", "acc", "y", "s", "sout", "sdma"))
        m_x, m_cv, m_rl, m_du = (sem(f"m_{n}") for n in ("x", "cv", "rl", "du"))
        w_in_sem = sem("w_loaded")
        w_hi, w_lo = sem("w_hi"), sem("w_lo")
        lvec_ok = sem("lvec_ok")
        x_hi, x_split = sem("x_hi"), sem("x_split")
        swap_in = [sem(f"swap_in_{r}") for r in range(3)]
        qk_proj, qk_sq, qk_mul, qk_rot = sem("qk_proj"), sem("qk_sq"), sem("qk_mul"), sem("qk_rot")
        sq_part, sq_clamp, r_ln, r_exp, r_hi, r_split = (
            sem(n) for n in ("sq_part", "sq_clamp", "r_ln", "r_exp", "r_hi", "r_split"))
        v_proj, v_sb = sem("v_proj"), sem("v_sb")
        rq_T, rq_sb = sem("rq_T"), sem("rq_sb")
        rk_bc, k_norm = sem("rk_bc"), sem("k_norm")
        sc_ps, sc_max, sc_bias, p_exp, p_rden, p_norm, p_T, p_Tsb, o_ps, o_sb = (
            sem(n) for n in ("sc_ps", "sc_max", "sc_bias", "p_exp", "p_rden", "p_norm", "p_T", "p_Tsb", "o_ps", "o_sb"))
        at_out, at_add = sem("at_out"), sem("at_add")
        l_sh, l_mean, l_xc, l_sq, l_var, l_ln, l_rstd, l_mul, l_xn = (
            sem(n) for n in ("l_sh", "l_mean", "l_xc", "l_sq", "l_var", "l_ln", "l_rstd", "l_mul", "l_xn"))
        f_hi, f_split, f_up, f_gelu, f_h, f_hhi, f_hlo, f_dn, f_add = (
            sem(n) for n in ("f_hi", "f_split", "f_up", "f_gelu", "f_h", "f_hhi", "f_hlo", "f_dn", "f_add"))
        s_in = sem("s_in")
        g_silu, g_mul, g_T, g_out, out_dma = (sem(n) for n in ("g_silu", "g_mul", "g_T", "g_out", "out_dma"))

        NCONST = 12
        FFS = 2 * len(FCH)
        credited = [m_sout, m_conv, m_s, m_sdma, x_hi, x_split, qk_proj, qk_sq, qk_mul, qk_rot, sq_part, sq_clamp,
                    r_ln, r_exp, r_hi, r_split, v_proj, v_sb, rq_T, rq_sb, rk_bc, k_norm, sc_ps, sc_max, sc_bias,
                    p_exp, p_rden, p_norm, p_T, p_Tsb, o_ps, o_sb, at_out, at_add, l_sh, l_mean, l_xc, l_sq, l_var,
                    l_ln, l_rstd, l_mul, l_xn, f_hi, f_split, f_up, f_gelu, f_h, f_hhi, f_hlo, f_dn, f_add,
                    g_mul, g_T, g_out]
        block = ctx.enter_context(nc.Block())

        def held(eng, n):
            eng.to_reg(n)
            return n

        class Bases:
            def __init__(self, eng, it):
                self.n1 = eng.snap(it + CREDIT)
                self.n2 = eng.snap(it * 2 + CREDIT)
                self.n8 = eng.snap(it * 8 + CREDIT)
                self.n16 = eng.snap(it * 16 + CREDIT)
                self.n32 = eng.snap(it * 32 + CREDIT)

        def use_bank(kind, i):
            return bank[4 + BANK_USES.index((kind, i)) % 3]

        def head_scale(t, p, b):
            return t[:, p // 4, 2 * b:2 * b + 2, 2 * (p % 4):2 * (p % 4) + 2]

        def three_pass(eng, o, wh, wl, ah, al):
            eng.matmul(o, wh, ah, start=True, stop=False)
            eng.matmul(o, wl, ah, start=False, stop=False)
            return eng.matmul(o, wh, al, start=False, stop=True)

        def settle(eng):
            eng.wait_ge(consts_made, 1)

        def seqs(ap):
            return ap.rearrange("p (b t) -> p b t", b=GB)

        @block.sync
        def _(sp_e):
            sp_e.dma_start(xtok, x_in.rearrange("b (t p) c -> p (b t) c", p=P)).then_inc(xtok_in, 16)
            for dst, src in ((ident[:, :], ident_c), (w_in, W_in), (mv[:, :], mvec),
                             (w_xdbl, W_xdbl), (w_dt[0:DT_RANK, :], W_dt),
                             (w_out[:, :].rearrange("p (t c) -> p t c", t=2), W_out.rearrange("(t p) c -> p t c", p=P)),
                             (statepick[64:96, :, :], statepick_c), (lv_all[:, :], lvec),
                             (tab[:, :, :], tabs_c), (mask[:, :], mask_c), (headsum[:, :, :], headsum_c),
                             (wide[:, 0, :].rearrange("p (t c) -> p t c", c=P), headpick_c)):
                sp_e.dma_start(dst, src).then_inc(consts_in, 16)
            with sp_e.Fori(0, GROUPS) as g:
                sp_e.wait_ge(m_sout, g + 1 + CREDIT)
                sp_e.dma_start(s_dram[:, bass.ds(g * GT, GT)], s_out).then_inc(m_sdma, 16)
            sp_e.wait_ge(m_sdma, 16 * GROUPS + CREDIT)

            def swaps(n16, nxt):
                for j in range(16):
                    made = held(sp_e, n16 + (16 * nxt + j + 1))
                    used = held(sp_e, n16 + (16 * nxt + max(j - 2, 0)))
                    sp_e.wait_ge(qk_mul, made)
                    sp_e.wait_ge(qk_rot, used)
                    for r in range(0, P, 32):
                        src = r + 32 if r % 64 == 0 else r - 32
                        sp_e.dma_start(swp[r:r + 32, j % 3, :], ab[src:src + 32, j % 3, 1, :])\
                            .then_inc(swap_in[j % 3], 16)

            with sp_e.Fori(0, DEPTH) as l:
                sp_e.wait_ge(at_out, l * GROUPS + CREDIT)
                sp_e.dma_start(raw_qkv, Wqkv[bass.ds(l, 1), :, :].rearrange("l p n -> p (l n)")).then_inc(w_in_sem, 16)
                sp_e.dma_start(raw_wo, Wo[bass.ds(l, 1), :, :].rearrange("l (t p) c -> p (l t) c", p=P)).then_inc(w_in_sem, 16)
                sp_e.dma_start(raw_w1, W1[bass.ds(l, 1), :, :].rearrange("l p n -> p (l n)")).then_inc(w_in_sem, 16)
                sp_e.dma_start(raw_w2[:, 0:2, :], W2[bass.ds(l, 1), 0:256, :].rearrange("l (t p) c -> p (l t) c", p=P))\
                    .then_inc(w_in_sem, 16)
                sp_e.dma_start(raw_w2[0:FCH[2][1], 2:3, :], W2[bass.ds(l, 1), 256:FF, :].rearrange("l p c -> p l c"))\
                    .then_inc(w_in_sem, 16)
                swaps(sp_e.snap(l * (GROUPS * 16) + CREDIT), 0)
                with sp_e.Fori(0, GROUPS - 1) as g:
                    swaps(sp_e.snap((l * GROUPS + g) * 16 + CREDIT), 1)
            sp_e.wait_ge(at_out, DEPTH * GROUPS + CREDIT)
            sp_e.dma_start(xtok, x_in.rearrange("b (t p) c -> p (b t) c", p=P)).then_inc(s_in, 16)
            sp_e.dma_start(rotw[:, TOKENS:2 * TOKENS], s_dram[:, :]).then_inc(s_in, 16)
            ov = out.rearrange("b (t p) c -> p (b t) c", p=P)
            with sp_e.Fori(0, GROUPS) as g:
                sp_e.wait_ge(g_out, g + 1 + CREDIT)
                sp_e.dma_start(ov[:, bass.ds(g * 4, 4), :], xtok[:, bass.ds(g * 4, 4), :]).then_inc(out_dma, 16)
            sp_e.wait_ge(out_dma, 16 * GROUPS)

        @block.tensor
        def _(pe):
            pe.wait_ge(consts_in, 16 * NCONST)
            pe.wait_ge(ln0_xn, 1)
            for t in range(TILES):
                if t >= 16 and t % 4 == 0:
                    pe.wait_ge(ln0_xT, t // 4 - 3)
                mm = pe.transpose(bank[t // 4 % 4][:, t % 4 * P:t % 4 * P + P], xtok[:, t, :], ident[:, :])
                if t % 4 == 3:
                    mm.then_inc(ln0_tr, 1)
            pe.wait_ge(ln0_xT, GROUPS)
            with pe.Fori(0, GROUPS) as g:
                pe.wait_ge(m_x, g + 1)
                pe.wait_ge(m_sout, g + CREDIT)
                pe.matmul(bank[0][:, :], w_in[:, 0:P], dtmp, start=True, stop=True).then_inc(m_proj, 1)
                pe.matmul(bank[1][:, :], w_in[:, P:2 * P], dtmp, start=True, stop=True).then_inc(m_proj, 1)
                pe.wait_ge(m_silu, g * 2 + 1)
                pe.matmul(bank[2][0:96, :], w_xdbl, u, start=True, stop=True).then_inc(m_xdbl, 1)
                pe.wait_ge(m_xd, g + 1)
                pe.matmul(bank[3][:, :], w_dt[0:DT_RANK, :], xd[0:DT_RANK, :], start=True, stop=True).then_inc(m_dt, 1)
                for n in range(D_STATE):
                    if n >= 2:
                        pe.wait_ge(m_dBu, g * D_STATE + n - 1)
                    pe.matmul(bank[4 + n % 2][:, :], statepick[64:96, n, :], xd[64:96, :], start=True, stop=True)\
                        .then_inc(m_B, 1)
                    if n >= 2:
                        pe.wait_ge(m_hC, g * D_STATE + n - 1)
                    pe.matmul(bank[6 + n % 2][:, :], statepick[64:96, D_STATE + n, :], xd[64:96, :],
                              start=True, stop=True).then_inc(m_C, 1)
                pe.wait_ge(m_y, g + 1)
                pe.wait_ge(m_silu, g * 2 + 2)
                pe.matmul(bank[2][:, :], w_out[:, 0:P], yy, start=True, stop=False)
                pe.matmul(bank[2][:, :], w_out[:, P:2 * P], z_act, start=False, stop=True).then_inc(m_s, 1)
            pe.wait_ge(consts_made, 1)
            pe.wait_ge(m_sout, GROUPS + CREDIT)
            with pe.Fori(0, DEPTH) as l:
                xhf = xh[:, :, :].rearrange("p b t -> p (b t)")
                xlf = xl[:, :, :].rearrange("p b t -> p (b t)")

                def turn(n, cur, nxt, x_count):
                    def bank_for(kind, i, o):
                        k = BANK_USES.index((kind, i))
                        bk = use_bank(kind, i)
                        if k < 3:
                            pe.wait_ge(k_norm, n.n8 + 8 * o)
                        else:
                            kind, i = BANK_USES[k - 3]
                            if kind == "qk":
                                pe.wait_ge(qk_mul, n.n16 + (16 * o + i + 1))
                            elif kind == "v":
                                pe.wait_ge(v_sb, n.n8 + (8 * o + i + 1))
                            elif kind == "rk":
                                pe.wait_ge(k_norm, n.n8 + (8 * o + i + 1))
                            else:
                                pe.wait_ge(rq_sb, n.n2 + (2 * o + i + 1))
                        return bk

                    def q_norms(h, o):
                        bk = bank_for("rqT", h, o)
                        norms = held(pe, n.n2 + (2 * o + h + 1))
                        settle(pe)
                        pe.wait_ge(r_split, norms)
                        for t in range(4):
                            mm = pe.transpose(bk[:, 32 * t:32 * t + 32], rsum[64 * h:64 * h + 32, t * P:t * P + P],
                                              ident[64 * h:64 * h + 32, 64 * h:64 * h + 32])
                        mm.then_inc(rq_T, 1)

                    def k_norms(p, o):
                        bk = bank_for("rk", p, o)
                        rows = slice(64 * (p // 4), 64 * (p // 4) + 64)
                        pe.matmul(bk[:, :], headpick[rows, p % 4, :], nh[rows, :], start=True, stop=False)
                        pe.matmul(bk[:, :], headpick[rows, p % 4, :], nl[rows, :], start=False, stop=True)\
                            .then_inc(rk_bc, 1)

                    for s in range(TURN):
                        if cur and s < STEPS:
                            p, b = s // 2, s % 2
                            if s % 8 == 0:
                                pe.wait_ge(qk_rot, n.n16 + (8 if s == 0 else 16))
                                pe.wait_ge(k_norm, n.n8 + (4 if s == 0 else 8))
                            for i in range(2):
                                u = 2 * s + i
                                if u == 0:
                                    pe.wait_ge(sc_max, n.n32)
                                    pe.wait_ge(at_add, n.n1)
                                if u >= 2:
                                    pe.wait_ge(sc_max, n.n32 + (u - 1))
                                rows = slice(64 * i, 64 * i + 64)
                                c0 = b * SEQ
                                o = bank[i]
                                pe.matmul(o[:, 0:P], rot[rows, p, c0:c0 + P], rot[rows, PAIRS + p, c0:c0 + P],
                                          start=True, stop=True)
                                pe.matmul(o[:, P:UW], rot[rows, p, c0 + P:c0 + SEQ],
                                          rot[rows, PAIRS + p, c0 + P - WINDOW:c0 + SEQ], start=True, stop=True)\
                                    .then_inc(sc_ps, 1)
                        if cur and s == 0:
                            q_norms(1, 0)
                            k_norms(4, 0)
                        if cur and s == 1:
                            k_norms(5, 0)
                            k_norms(6, 0)
                        if cur and s == 2:
                            k_norms(7, 0)
                        if nxt is not None and s % 2 == 0 and 0 <= s - 6 < 16:
                            p = (s - 6) // 2
                            pe.wait_ge(qk_sq, n.n16 + (16 * nxt + 2 * p + 2))
                            if p == 0:
                                pe.wait_ge(sq_clamp, n.n2 + 2 * nxt)
                            for i in range(2):
                                t = 2 * (p // 4) + i
                                mm = pe.matmul(bank[7][32 * t:32 * t + 32, :], headsum[:, p % 4, :],
                                               sq[:, (2 * p + i) % 4, :], start=(p % 4 == 0), stop=(p % 4 == 3),
                                               skip_group_check=True)
                            mm.then_inc(sq_part, 1)
                        if cur and 0 <= s - 5 < STEPS:
                            e = s - 5
                            p, b = e // 2, e % 2
                            if e == 0:
                                pe.wait_ge(v_sb, n.n8 + 8)
                            pe.wait_ge(p_Tsb, n.n16 + (e + 1))
                            if e >= 1:
                                pe.wait_ge(o_sb, n.n16 + e)
                            o = [bank[3][64 * i:64 * i + 64, :] for i in range(2)]
                            ch = [slice((2 * p + i) * DH, (2 * p + i) * DH + DH) for i in range(2)]
                            for i in range(2):
                                pe.matmul(o[i][:, 0:P], vtok[:, 2 * b, ch[i]], pt[:, e % 3, i, 0:P],
                                          start=True, stop=True)
                            for i in range(2):
                                pe.matmul(o[i][:, P:2 * P], vtok[:, 2 * b + 1, ch[i]], pt[:, e % 3, i, P:2 * P],
                                          start=True, stop=True)
                            for i in range(2):
                                mm = pe.matmul(o[i][:, P:P + WINDOW], vtok[96:128, 2 * b, ch[i]],
                                               pp[96:128, e % 3, i, :], start=False, stop=True, skip_group_check=True)
                            mm.then_inc(o_ps, 1)
                        if nxt is not None and s == 16:
                            q_norms(0, nxt)
                        if nxt is not None and 17 <= s < 21:
                            k_norms(s - 17, nxt)
                        if nxt is not None and 0 <= s - 3 < 16:
                            j = s - 3
                            if j == 0:
                                pe.wait_ge(x_split, x_count)
                            bk = bank_for("qk", j, nxt)
                            blk = PAIRS * (j % 2) + j // 2
                            three_pass(pe, bk[:, :], wqk_h[:, blk, :], wqk_l[:, blk, :], xhf, xlf).then_inc(qk_proj, 1)
                        if nxt is not None and s in V_STEPS:
                            i = V_STEPS.index(s)
                            c, b = i // 2, i % 2
                            cols = slice(c * VW, c * VW + VW)
                            bk = bank_for("v", i, nxt)
                            for t in range(2):
                                mm = three_pass(pe, bk[:, t * VW:t * VW + VW], xh[:, b, t * P:t * P + P],
                                                xl[:, b, t * P:t * P + P], wv_h[:, cols], wv_l[:, cols])
                            mm.then_inc(v_proj, 1)
                        if cur and 0 <= s - 3 < STEPS:
                            e = s - 3
                            pe.wait_ge(p_norm, n.n16 + (e + 1))
                            if e >= 1:
                                pe.wait_ge(p_Tsb, n.n16 + e)
                            for i in range(2):
                                pe.transpose(bank[2][:, 256 * i:256 * i + P], pr[:, e % 4, i, 0:P], ident[:, :])
                                mm = pe.transpose(bank[2][:, 256 * i + P:256 * i + 2 * P],
                                                  pr[:, e % 4, i, P + WINDOW:UW], ident[:, :])
                            mm.then_inc(p_T, 1)
                        if cur and s == 21:
                            pe.wait_ge(o_sb, n.n16 + 16)
                            for p in range(PAIRS):
                                mm = pe.matmul(bank[2][:, :], wo[:, p, :], wide[:, p, :], start=(p == 0),
                                               stop=(p == PAIRS - 1))
                            mm.then_inc(at_out, 1)

                n0 = Bases(pe, pe.snap(l * GROUPS))
                x9 = pe.snap(l * (GROUPS + 1) + CREDIT)
                pe.wait_ge(w_hi, l + 1)
                pe.wait_ge(w_lo, l + 1)
                turn(n0, False, 0, x9 + 1)
                with pe.Fori(0, GROUPS - 1) as g:
                    n = Bases(pe, pe.snap(l * GROUPS + g))
                    xg = pe.snap(l * (GROUPS + 1) + g + CREDIT)
                    turn(n, True, 1, xg + 2)
                turn(Bases(pe, pe.snap(l * GROUPS + (GROUPS - 1))), True, None, None)
                with pe.Fori(0, GROUPS // 2) as g2:
                    i2 = pe.snap((l * (GROUPS // 2) + g2) * 2 + CREDIT)
                    for k in range(2):
                        pe.wait_ge(l_sh, i2 + (k + 1))
                        pe.matmul(bank[k][:, :], mean_w[:, :], ab[:, k, 0, :], start=True, stop=True).then_inc(l_mean, 1)
                    for k in range(2):
                        pe.wait_ge(l_sq, i2 + (k + 1))
                        pe.matmul(bank[2 + k][:, :], mean_w[:, :], ab[:, k, 1, :], start=True, stop=True).then_inc(l_var, 1)
                with pe.Fori(0, GROUPS // 2) as g2:
                    i2 = pe.snap((l * (GROUPS // 2) + g2) * 2 + CREDIT)
                    i6 = pe.snap((l * (GROUPS // 2) + g2) * (2 * len(FCH)) + CREDIT)
                    for s in range(FFS + 2):
                        if s < FFS:
                            k, c = s // 3, s % 3
                            c0, cn = FCH[c]
                            if c == 0:
                                pe.wait_ge(f_split, i2 + (k + 1))
                            if s >= 3:
                                pe.wait_ge(f_h, i6 + (s - 2))
                            xhf = (xh, hh)[0][:, :, :].rearrange("p b t -> p (b t)")
                            xlf = xl[:, :, :].rearrange("p b t -> p (b t)")
                            o = 2 * (s % 3)
                            three_pass(pe, bank[o][0:cn, :], w1_h[:, c0:c0 + cn], w1_l[:, c0:c0 + cn], xhf, xlf)
                            three_pass(pe, bank[o + 1][0:cn, :], w1_h[:, FF + c0:FF + c0 + cn],
                                       w1_l[:, FF + c0:FF + c0 + cn], xhf, xlf).then_inc(f_up, 1)
                        if s >= 2:
                            e = s - 2
                            k, c = e // 3, e % 3
                            cn = FCH[c][1]
                            pe.wait_ge(f_hlo, i6 + (e + 1))
                            if c == 0:
                                pe.wait_ge(f_add, i2 if k == 0 else i2)
                            o = bank[6 + k][:, :]
                            pe.matmul(o, w2_h[0:cn, c, :], hh[0:cn, e % 2, :], start=(c == 0), stop=False)
                            pe.matmul(o, w2_l[0:cn, c, :], hh[0:cn, e % 2, :], start=False, stop=False)
                            mm = pe.matmul(o, w2_h[0:cn, c, :], hl[0:cn, e % 2, :], start=False, stop=(c == 2))
                            mm.then_inc(f_dn, 1)
            with pe.Fori(0, GROUPS) as g:
                pe.wait_ge(g_mul, g + 1 + CREDIT)
                pe.wait_ge(g_out, g + CREDIT)
                for t in range(4):
                    mm = pe.transpose(bank[0][:, t * P:t * P + P], ab[:, 1, 0, t * P:t * P + P], ident[:, :])
                mm.then_inc(g_T, 1)

        @block.scalar
        def _(act):
            act.wait_ge(ln0_mean, 1)
            act.activation(xsq, xtok, ACT.Square).then_inc(ln0_sq, 1)
            act.wait_ge(ln0_var, 1)
            act.activation(st[:, 2, :], st[:, 1, :], ACT.Ln).then_inc(link["act"], 1)
            act.wait_ge(link["act"], 1)
            act.activation(st[:, 3, :], st[:, 2, :], ACT.Exp, scale=-0.5).then_inc(ln0_rstd, 1)
            act.wait_ge(consts_in, 16 * NCONST)
            act.wait_ge(consts_made, 1)
            with act.Fori(0, GROUPS) as g:
                for i, pad in enumerate((pad_x, pad_z)):
                    act.wait_ge(m_proj, g * 2 + (i + 1))
                    act.wait_ge(m_conv, g * 2 + CREDIT)
                    act.activation(pad[:, :, 1:1 + SEQ], seqs(bank[i][:, :]), ACT.Copy).then_inc(m_pad, 1)
                for i, o in enumerate((u, z_act)):
                    act.wait_ge(m_conv, g * 2 + (i + 1) + CREDIT)
                    act.wait_ge(m_s, g + CREDIT)
                    act.activation(o, ct[i], ACT.Silu).then_inc(m_silu, 1)
                act.wait_ge(m_dt, g + 1)
                act.activation(sp[0], bank[3][:, :], ACT.Abs, bias=mv[:, M_DT2:M_DT2 + 1]).then_inc(m_soft, 1)
                act.wait_ge(m_soft, g + 1)
                act.activation(sp[1], sp[0], ACT.Exp, scale=-1.0).then_inc(m_soft2, 1)
                act.wait_ge(m_soft2, g + 1)
                act.activation(sp[0], sp[1], ACT.Ln, bias=1.0).then_inc(m_softl, 1)
                act.wait_ge(m_delta, g + 1)
                for n in range(D_STATE):
                    if n >= 2:
                        act.wait_ge(m_scan, g * D_STATE + (n - 1))
                    act.activation(dA[n % 2], delta, ACT.Exp, scale=-float(n + 1)).then_inc(m_dA, 1)
                act.wait_ge(m_s, g + 1 + CREDIT)
                act.wait_ge(m_sdma, g * 16 + CREDIT)
                act.activation(s_out, bank[2][:, :], ACT.Identity, bias=mv[:, M_BO:M_BO + 1]).then_inc(m_sout, 1)
            with act.Fori(0, DEPTH) as l:
                act.wait_ge(w_in_sem, l * 80 + 80)
                act.wait_ge(f_dn, l * (GROUPS * 3) + CREDIT)
                act.activation(wqk_h[:, 0:2 * PAIRS, :].rearrange("p a c -> p (a c)"), raw_qkv[:, 0:2 * INNER], ACT.Copy)
                act.activation(wv_h[:, :], raw_qkv[:, 2 * INNER:3 * INNER], ACT.Copy)
                act.activation(w1_h[:, :], raw_w1, ACT.Copy)
                act.activation(w2_h[:, 0:2, :], raw_w2[:, 0:2, :], ACT.Copy)
                act.activation(w2_h[0:FCH[2][1], 2, :], raw_w2[0:FCH[2][1], 2, :], ACT.Copy)
                act.activation(wo[:, :, :], raw_wo, ACT.Copy).then_inc(w_hi, 1)
                act.wait_ge(w_lo, l + 1)

                def turn(n, cur, nxt):
                    for s in range(TURN):
                        if nxt is not None and 0 <= s - 4 < 16:
                            j = s - 4
                            act.wait_ge(qk_proj, n.n16 + (16 * nxt + j + 1))
                            act.wait_ge(sq_part, n.n8 + (8 * nxt + max((j - 2) // 2, 0)))
                            bk = use_bank("qk", j)
                            act.activation(sq[:, j % 4, :], bk[:, :], ACT.Square).then_inc(qk_sq, 1)
                        if cur and s < STEPS:
                            p, b = s // 2, s % 2
                            act.wait_ge(sc_bias, n.n16 + (s + 1))
                            if s >= 4:
                                act.wait_ge(p_T, n.n16 + (s - 3))
                                act.wait_ge(p_Tsb, n.n16 + (s - 3))
                            for i in range(2):
                                for t in range(2):
                                    cs = slice(0, P) if t == 0 else slice(P, UW)
                                    ins = act.activation(pr[:, s % 4, i, cs], sm[:, s % 2, i, cs], ACT.Exp,
                                                         bias=nb[:, s, t, i:i + 1],
                                                         scale=head_scale(rq, p, b)[:, t, i:i + 1],
                                                         accum_out=den[:, s, t, i:i + 1])
                            ins.then_inc(p_exp, 1)
                        if cur and 0 <= s - 5 < STEPS:
                            e = s - 5
                            p, b = e // 2, e % 2
                            act.wait_ge(o_ps, n.n16 + (e + 1))
                            if e == 0:
                                act.wait_ge(at_out, n.n1)
                            act.activation(wide[:, p, b * SEQ:b * SEQ + SEQ], bank[3][:, 0:SEQ], ACT.Copy)\
                                .then_inc(o_sb, 1)
                        if nxt is not None and s in V_STEPS:
                            i = V_STEPS.index(s)
                            c, b = i // 2, i % 2
                            act.wait_ge(v_proj, n.n8 + (8 * nxt + i + 1))
                            bk = use_bank("v", i)
                            act.activation(vtok[:, 2 * b:2 * b + 2, c * VW:c * VW + VW],
                                           bk[:, :].rearrange("p (t c) -> p t c", t=2), ACT.Copy).then_inc(v_sb, 1)
                        if nxt is not None and s in (13, 21):
                            h = (13, 21).index(s)
                            rows = slice(64 * h, 64 * h + 64)
                            act.wait_ge(sq_clamp, n.n2 + (2 * nxt + h + 1))
                            act.activation(rsum[rows, :], rsum[rows, :], ACT.Ln, scale=float(2 ** R_LOG2))\
                                .then_inc(r_ln, 1)
                            act.wait_ge(r_ln, n.n2 + (2 * nxt + h + 1))
                            act.activation(rsum[rows, :], rsum[rows, :], ACT.Exp, scale=-0.5).then_inc(r_exp, 1)

                turn(Bases(act, act.snap(l * GROUPS)), False, 0)
                with act.Fori(0, GROUPS - 1) as g:
                    turn(Bases(act, act.snap(l * GROUPS + g)), True, 1)
                turn(Bases(act, act.snap(l * GROUPS + (GROUPS - 1))), True, None)
                with act.Fori(0, GROUPS // 2) as g2:
                    i2 = act.snap((l * (GROUPS // 2) + g2) * 2 + CREDIT)
                    for k in range(2):
                        act.wait_ge(l_xc, i2 + (k + 1))
                        act.activation(ab[:, k, 1, :], ab[:, k, 0, :], ACT.Square).then_inc(l_sq, 1)
                    for k in range(2):
                        act.wait_ge(l_var, i2 + (k + 1))
                        act.activation(ab[:, k, 1, :], bank[2 + k][:, :], ACT.Ln, bias=eps[:, 0:1]).then_inc(l_ln, 1)
                        act.wait_ge(l_ln, i2 + (k + 1))
                        act.activation(ab[:, k, 1, :], ab[:, k, 1, :], ACT.Exp, scale=-0.5).then_inc(l_rstd, 1)
                with act.Fori(0, GROUPS // 2) as g2:
                    i2 = act.snap((l * (GROUPS // 2) + g2) * 2 + CREDIT)
                    i6 = act.snap((l * (GROUPS // 2) + g2) * (2 * len(FCH)) + CREDIT)
                    for s in range(FFS):
                        k, c = s // 3, s % 3
                        cn = FCH[c][1]
                        act.wait_ge(f_up, i6 + (s + 1))
                        act.wait_ge(f_h, i6 + max(s - 1, 0))
                        act.activation(ab[0:cn, s % 2, 0, :], bank[2 * (s % 3) + 1][0:cn, :], ACT.Gelu,
                                       bias=lv[0:cn, V_B1G + c:V_B1G + c + 1]).then_inc(f_gelu, 1)
                        act.wait_ge(f_h, i6 + (s + 1))
                        act.wait_ge(f_dn, i6 + max(s - 1, 0))
                        act.activation(hh[0:cn, s % 2, :], ab[0:cn, s % 2, 1, :], ACT.Copy).then_inc(f_hhi, 1)
            with act.Fori(0, GROUPS) as g:
                act.wait_ge(f_add, DEPTH * GROUPS + CREDIT)
                act.wait_ge(g_mul, g + CREDIT)
                act.activation(ab[:, 0, 0, :], xT[:, bass.ds(g * GT, GT)], ACT.Silu).then_inc(g_silu, 1)

        @block.gpsimd
        def _(pool):
            for i, c in enumerate(credited):
                pool.memset(credit[:, i:i + 1], 0.0).then_inc(c, CREDIT)
            with pool.Fori(0, GROUPS) as g:
                for n in range(1, D_STATE):
                    pool.wait_ge(m_hC, g * D_STATE + (n + 1))
                    if n > 1:
                        pool.wait_ge(m_acc, g * (D_STATE - 1) + (n - 1))
                    pool.tensor_tensor(acc, hC[0] if n == 1 else acc, hC[n % 2], ALU.add).then_inc(m_acc, 1)
            with pool.Fori(0, DEPTH) as l:
                SWAPS = [len(range(r, 16, 3)) for r in range(3)]

                def swap_bases(it):
                    return [pool.snap(it * (64 * c)) for c in SWAPS]

                def turn(n, ns, cur, nxt):
                    for s in range(TURN):
                        if cur and 0 <= s - 2 < STEPS:
                            e = s - 2
                            count = held(pool, n.n16 + (e + 1))
                            settle(pool)
                            pool.wait_ge(p_rden, count)
                            for i in range(2):
                                for t in range(2):
                                    cs = slice(0, P) if t == 0 else slice(P, UW)
                                    ins = pool.tensor_scalar(pr[:, e % 4, i, cs], pr[:, e % 4, i, cs],
                                                             rden[:, e, t, i:i + 1], 1.0, ALU.mult, ALU.mult)
                            ins.then_inc(p_norm, 1)
                        if nxt is not None and 0 <= s - 6 < 16:
                            j = s - 6
                            pool.wait_ge(swap_in[j % 3], ns[j % 3] + (64 * (SWAPS[j % 3] * nxt + j // 3 + 1)))
                            pool.wait_ge(qk_mul, n.n16 + (16 * nxt + j + 1))
                            pool.tensor_tensor(rot[:, PAIRS * (j % 2) + j // 2, :], ab[:, j % 3, 0, :], swp[:, j % 3, :],
                                               ALU.add).then_inc(qk_rot, 1)

                turn(Bases(pool, pool.snap(l * GROUPS)), swap_bases(pool.snap(l * GROUPS)), False, 0)
                with pool.Fori(0, GROUPS - 1) as g:
                    turn(Bases(pool, pool.snap(l * GROUPS + g)), swap_bases(pool.snap(l * GROUPS + g)), True, 1)
                turn(Bases(pool, pool.snap(l * GROUPS + (GROUPS - 1))), None, True, None)

        @block.vector
        def _(dve):
            chain = [0]

            def linked(ins):
                chain[0] += 1
                ins.then_inc(link["dve"], 1)
                dve.wait_ge(link["dve"], chain[0])

            dve.memset(mean_w[:, :], 1.0 / DIM)
            dve.memset(eps[:, :], 1e-5)
            dve.memset(xT[:, TOKENS:], 0.0)
            for pad in (pad_x, pad_z):
                dve.memset(pad[:, :, 0:1], 0.0)
                dve.memset(pad[:, :, 1 + SEQ:PADW], 0.0)
            dve.wait_ge(xtok_in, 16)
            linked(dve.tensor_reduce(st[:, 0, :], xtok, AX_X, ALU.add))
            linked(dve.tensor_scalar(st[:, 1, :], st[:, 0, :], 1.0 / DIM, None, ALU.mult))
            dve.tensor_tensor(xtok, xtok, st[:, 1, :].unsqueeze(2).to_broadcast([P, TILES, DIM]), ALU.subtract)\
                .then_inc(ln0_mean, 1)
            dve.wait_ge(ln0_sq, 1)
            linked(dve.tensor_reduce(st[:, 0, :], xsq, AX_X, ALU.add))
            dve.tensor_scalar(st[:, 1, :], st[:, 0, :], 1.0 / DIM, 1e-5, ALU.mult, ALU.add).then_inc(ln0_var, 1)
            dve.wait_ge(ln0_rstd, 1)
            dve.tensor_tensor(xtok, xtok, st[:, 3, :].unsqueeze(2).to_broadcast([P, TILES, DIM]), ALU.mult)\
                .then_inc(ln0_xn, 1)
            for q in range(GROUPS):
                dve.wait_ge(ln0_tr, q + 1)
                dve.tensor_copy(xT[:, q * GT:q * GT + GT], bank[q % 4][:, :]).then_inc(ln0_xT, 1)
            dve.wait_ge(consts_in, 16 * NCONST)
            dve.tensor_copy(headpick[:, :, :], wide[:, 0, :].rearrange("p (t c) -> p t c", c=P))
            dve.tensor_scalar(mv[:, M_DT2:M_DT2 + 1], mv[:, M_DT2:M_DT2 + 1], 2.0, None, ALU.mult).then_inc(consts_made, 1)
            dve.wait_ge(consts_made, 1)
            dve.wait_ge(ln0_xT, GROUPS)
            with dve.Fori(0, GROUPS) as g:
                g16 = dve.snap(g * D_STATE)
                dve.wait_ge(m_s, g + CREDIT)
                dve.tensor_copy(dtmp, xT[:, bass.ds(g * GT, GT)]).then_inc(m_x, 1)
                for i, (pad, w0, b0) in enumerate(((pad_x, M_CXW, M_CXB), (pad_z, M_CZW, M_CZB))):
                    dve.wait_ge(m_pad, g * 2 + (i + 1))
                    dve.tensor_scalar(seqs(ct[2 + i]), pad[:, :, 0:SEQ], mv[:, w0:w0 + 1], mv[:, b0:b0 + 1],
                                      ALU.mult, ALU.add).then_inc(m_cv, 1)
                    for k in range(1, D_CONV):
                        src, dst = (ct[2 + i], ct[i]) if k % 2 else (ct[i], ct[2 + i])
                        dve.wait_ge(m_cv, g * 6 + (i * 3 + k))
                        ins = dve.scalar_tensor_tensor(seqs(dst), pad[:, :, k:k + SEQ], mv[:, w0 + k:w0 + k + 1],
                                                       seqs(src), ALU.mult, ALU.add)
                        ins.then_inc(m_cv if k < D_CONV - 1 else m_conv, 1)
                dve.wait_ge(m_xdbl, g + 1)
                dve.tensor_copy(xd[0:96, :], bank[2][0:96, :]).then_inc(m_xd, 1)
                dve.wait_ge(m_dt, g + 1)
                dve.wait_ge(m_soft, g + 1)
                dve.tensor_scalar(delta, bank[3][:, :], mv[:, M_DT2:M_DT2 + 1], 0.0, ALU.add, ALU.max).then_inc(m_rl, 1)
                dve.wait_ge(m_softl, g + 1)
                dve.wait_ge(m_rl, g + 1)
                dve.tensor_tensor(delta, delta, sp[0], ALU.add).then_inc(m_delta, 1)
                dve.wait_ge(m_delta, g + 1)
                dve.tensor_tensor(du, delta, u, ALU.mult).then_inc(m_du, 1)
                dve.wait_ge(m_du, g + 1)

                def emit(n):
                    dve.wait_ge(m_C, g16 + (n + 1))
                    dve.wait_ge(m_scan, g16 + (n + 1))
                    if n >= 2:
                        dve.wait_ge(m_acc, g * (D_STATE - 1) + max(1, n - 2))
                    dve.tensor_tensor(hC[n % 2], hst[n % 2], bank[6 + n % 2][:, :], ALU.mult).then_inc(m_hC, 1)

                for n in range(D_STATE):
                    dve.wait_ge(m_B, g16 + (n + 1))
                    if n >= 2:
                        dve.wait_ge(m_hC, g16 + (n - 1))
                    dve.tensor_tensor(dBu[n % 2], du, bank[4 + n % 2][:, :], ALU.mult).then_inc(m_dBu, 1)
                    if n >= 1:
                        emit(n - 1)
                    dve.wait_ge(m_dBu, g16 + (n + 1))
                    dve.wait_ge(m_dA, g16 + (n + 1))
                    for b in range(GB):
                        cs = slice(b * SEQ, b * SEQ + SEQ)
                        ins = dve.tensor_tensor_scan(hst[n % 2][:, cs], dA[n % 2][:, cs], dBu[n % 2][:, cs], 0.0,
                                                     ALU.mult, ALU.add)
                    ins.then_inc(m_scan, 1)
                emit(D_STATE - 1)
                dve.wait_ge(m_acc, (g + 1) * (D_STATE - 1))
                dve.scalar_tensor_tensor(yy, u, mv[:, M_D:M_D + 1], acc, ALU.mult, ALU.add).then_inc(m_y, 1)
            dve.wait_ge(m_sout, GROUPS + CREDIT)
            with dve.Fori(0, DEPTH) as l:
                dve.wait_ge(w_in_sem, l * 80 + 80)
                dve.wait_ge(w_hi, l + 1)
                dve.wait_ge(f_add, l * GROUPS + CREDIT)
                dve.tensor_tensor(wqk_l[:, 0:2 * PAIRS, :].rearrange("p a c -> p (a c)"), raw_qkv[:, 0:2 * INNER],
                                  wqk_h[:, 0:2 * PAIRS, :].rearrange("p a c -> p (a c)").bitcast(F32), ALU.subtract)
                dve.tensor_tensor(wv_l[:, :], raw_qkv[:, 2 * INNER:3 * INNER], wv_h[:, :].bitcast(F32), ALU.subtract)
                dve.tensor_tensor(w1_l[:, :], raw_w1, w1_h[:, :].bitcast(F32), ALU.subtract)
                n2 = FCH[2][1]
                dve.tensor_tensor(w2_l[:, 0:2, :], raw_w2[:, 0:2, :], w2_h[:, 0:2, :].bitcast(F32), ALU.subtract)
                dve.tensor_tensor(w2_l[0:n2, 2, :], raw_w2[0:n2, 2, :], w2_h[0:n2, 2, :].bitcast(F32), ALU.subtract)\
                    .then_inc(w_lo, 1)
                dve.tensor_copy(lv[:, :], lv_all[:, bass.ds(l * NVEC, NVEC)]).then_inc(lvec_ok, 1)
                dve.wait_ge(lvec_ok, l * 2 + 1)
                for i, c in enumerate((V_QS, V_QS, V_KS, V_KS)):
                    ins = dve.tensor_scalar(ltab[:, i, :], tab[:, i, :], lv[:, c:c + 1], None, ALU.mult)
                ins.then_inc(lvec_ok, 1)
                dve.wait_ge(lvec_ok, l * 2 + 2)

                def split_x(g, count):
                    xlo = seqs(xT[0:64, bass.ds(g * GT, GT)])
                    xhi = seqs(xT[64:128, bass.ds(g * GT, GT)])
                    dve.tensor_copy(xh[0:64, :, :], xlo)
                    dve.tensor_copy(xh[64:128, :, 1:SEQ], xhi[:, :, 0:SEQ - 1]).then_inc(x_hi, 1)
                    dve.wait_ge(x_hi, count)
                    dve.tensor_tensor(xl[0:64, :, :], xlo, xh[0:64, :, :].bitcast(F32), ALU.subtract)
                    dve.tensor_tensor(xl[64:128, :, 1:SEQ], xhi[:, :, 0:SEQ - 1], xh[64:128, :, 1:SEQ].bitcast(F32),
                                      ALU.subtract).then_inc(x_split, 1)

                dve.memset(xh[64:128, :, 0:1].bitcast(F32), 0.0)
                dve.memset(xl[64:128, :, 0:1].bitcast(F32), 0.0)
                x9 = dve.snap(l * (GROUPS + 1) + (CREDIT + 1))
                split_x(0, x9)

                def turn(n, cur, nxt, g, x_count):
                    def scale_k(p, o):
                        dve.wait_ge(qk_rot, n.n16 + (16 * o + 2 * p + 2))
                        dve.wait_ge(rk_bc, n.n8 + (8 * o + p + 1))
                        bk = use_bank("rk", p)
                        dve.tensor_tensor(rot[:, PAIRS + p, :], rot[:, PAIRS + p, :], bk[:, :], ALU.mult)\
                            .then_inc(k_norm, 1)

                    def scale_q(h, o):
                        dve.wait_ge(rq_T, n.n2 + (2 * o + h + 1))
                        bk = use_bank("rqT", h)
                        src = bk[:, 0:P].rearrange("p (t r) -> p t r", t=4)[:, :, 0:8]
                        up = float(2 ** (R_LOG2 // 2)) * QK_SCALE
                        dve.tensor_scalar(rq[:, h, :, :], src, up, None, ALU.mult)
                        dve.tensor_scalar(nrq[:, h, :, :], src, -up, None, ALU.mult).then_inc(rq_sb, 1)

                    for s in range(TURN):
                        if cur and 0 <= s - 2 < STEPS:
                            e = s - 2
                            dve.wait_ge(p_exp, n.n16 + (e + 1))
                            dve.reciprocal(rden[:, e, :, :], den[:, e, :, :]).then_inc(p_rden, 1)
                        if cur and s == 1:
                            scale_q(1, 0)
                            scale_k(4, 0)
                        if cur and s == 2:
                            scale_k(5, 0)
                            scale_k(6, 0)
                        if cur and s == 3:
                            scale_k(7, 0)
                        if nxt is not None and s == 17:
                            scale_q(0, nxt)
                        if nxt is not None and 18 <= s < 22:
                            scale_k(s - 18, nxt)
                        if nxt is not None and 0 <= s - 5 < 16:
                            j = s - 5
                            dve.wait_ge(qk_sq, n.n16 + (16 * nxt + j + 1))
                            dve.wait_ge(qk_rot, n.n16 + (16 * nxt + max(j - 2, 0)))
                            bk = use_bank("qk", j)
                            for i in range(2):
                                ins = dve.tensor_tensor(seqs(ab[:, j % 3, i, :]), seqs(bk[:, :]),
                                                        ltab[:, 2 * (j % 2) + i:2 * (j % 2) + i + 1, :]
                                                        .to_broadcast([P, GB, SEQ]), ALU.mult)
                            ins.then_inc(qk_mul, 1)
                        if cur and 0 <= s - 4 < STEPS:
                            e = s - 4
                            dve.wait_ge(p_T, n.n16 + (e + 1))
                            if e >= 3:
                                dve.wait_ge(o_ps, n.n16 + (e - 2))
                            dve.transpose(pp[96:128, e % 3, :, :], pr[0:32, e % 4, :, P:P + WINDOW])
                            dve.tensor_copy(pt[:, e % 3, :, :].rearrange("p i c -> p (i c)"), bank[2][:, :])\
                                .then_inc(p_Tsb, 1)
                        if cur and s < STEPS:
                            p, b = s // 2, s % 2
                            for i in range(2):
                                u = 2 * s + i
                                scores = held(dve, n.n32 + (u + 1))
                                used = held(dve, n.n16 + max(s - 1, 0))
                                settle(dve)
                                dve.wait_ge(sc_ps, scores)
                                if i == 0:
                                    dve.wait_ge(p_exp, used)
                                for t in range(2):
                                    cs = slice(0, P) if t == 0 else slice(P, UW)
                                    ins = dve.tensor_tensor_reduce(sm[:, s % 2, i, cs], bank[i][:, cs], mask[:, cs],
                                                                   1.0, -3e38, ALU.add, ALU.max, mx[:, s, t, i:i + 1])
                                ins.then_inc(sc_max, 1)
                            dve.wait_ge(sc_max, n.n32 + (2 * s + 2))
                            if s == 0:
                                dve.wait_ge(rq_sb, n.n2 + 1)
                            if s == 8:
                                dve.wait_ge(rq_sb, n.n2 + 2)
                            dve.tensor_tensor(nb[:, s, :, :], mx[:, s, :, :], head_scale(nrq, p, b), ALU.mult)\
                                .then_inc(sc_bias, 1)
                        if nxt is not None and s in (13, 21):
                            h = (13, 21).index(s)
                            rows = slice(64 * h, 64 * h + 64)
                            dve.wait_ge(sq_part, n.n8 + (8 * nxt + 4 * h + 4))
                            dve.tensor_scalar(rsum[rows, :], bank[7][rows, :], 1e-24, None, ALU.max)\
                                .then_inc(sq_clamp, 1)
                        if nxt is not None and s in (14, 22):
                            h = (14, 22).index(s)
                            rows = slice(64 * h, 64 * h + 64)
                            dve.wait_ge(r_exp, n.n2 + (2 * nxt + h + 1))
                            dve.tensor_copy(nh[rows, :], rsum[rows, :]).then_inc(r_hi, 1)
                            dve.wait_ge(r_hi, n.n2 + (2 * nxt + h + 1))
                            dve.tensor_tensor(nl[rows, :], rsum[rows, :], nh[rows, :].bitcast(F32), ALU.subtract)\
                                .then_inc(r_split, 1)
                    if nxt is not None:
                        dve.wait_ge(v_proj, n.n8 + (8 * nxt + 8))
                        split_x(g + (nxt + 1), x_count)
                    if cur:
                        dve.wait_ge(at_out, n.n1 + 1)
                        dst = xT[:, bass.ds(g * GT, GT)]
                        dve.tensor_tensor(dst, dst, bank[2][:, :], ALU.add).then_inc(at_add, 1)

                turn(Bases(dve, dve.snap(l * GROUPS)), False, 0, 0, x9 + 1)
                with dve.Fori(0, GROUPS - 1) as g:
                    xg = dve.snap(l * (GROUPS + 1) + g + (CREDIT + 3))
                    turn(Bases(dve, dve.snap(l * GROUPS + g)), True, 1, g, xg)
                turn(Bases(dve, dve.snap(l * GROUPS + (GROUPS - 1))), True, None, GROUPS - 1, None)
                with dve.Fori(0, GROUPS // 2) as g2:
                    i2 = dve.snap((l * (GROUPS // 2) + g2) * 2 + CREDIT)
                    for k in range(2):
                        xlo = seqs(xT[0:64, bass.ds((g2 * 2 + k) * GT, GT)])
                        xhi = seqs(xT[64:128, bass.ds((g2 * 2 + k) * GT, GT)])
                        a0 = ab[:, k, 0, :]
                        dve.wait_ge(at_add, (l + 1) * GROUPS + CREDIT)
                        dve.wait_ge(l_xn, i2)
                        dve.memset(seqs(a0)[64:128, :, 0:1], 0.0)
                        dve.tensor_copy(seqs(a0)[0:64, :, :], xlo)
                        dve.tensor_copy(seqs(a0)[64:128, :, 1:SEQ], xhi[:, :, 0:SEQ - 1]).then_inc(l_sh, 1)
                    for k in range(2):
                        dve.wait_ge(l_mean, i2 + (k + 1))
                        dve.wait_ge(l_sh, i2 + (k + 1))
                        dve.tensor_tensor(ab[:, k, 0, :], ab[:, k, 0, :], bank[k][:, :], ALU.subtract).then_inc(l_xc, 1)
                    for k in range(2):
                        dve.wait_ge(l_rstd, i2 + (k + 1))
                        dve.wait_ge(l_xc, i2 + (k + 1))
                        dve.tensor_tensor(ab[:, k, 0, :], ab[:, k, 0, :], ab[:, k, 1, :], ALU.mult).then_inc(l_mul, 1)
                    for k in range(2):
                        dve.wait_ge(l_mul, i2 + (k + 1))
                        dve.tensor_scalar(wide_f[:, bass.ds((g2 * 2 + k) * GT, GT)], ab[:, k, 0, :],
                                          lv[:, V_G:V_G + 1], lv[:, V_B:V_B + 1], ALU.mult, ALU.add).then_inc(l_xn, 1)
                with dve.Fori(0, GROUPS // 2) as g2:
                    i2 = dve.snap((l * (GROUPS // 2) + g2) * 2 + CREDIT)
                    i6 = dve.snap((l * (GROUPS // 2) + g2) * (2 * len(FCH)) + CREDIT)

                    def split(k):
                        src = wide_f[:, bass.ds((g2 * 2 + k) * GT, GT)]
                        dve.wait_ge(l_xn, (l + 1) * GROUPS + CREDIT)
                        dve.wait_ge(f_up, i6 + 3 * k)
                        dve.tensor_copy(xh[:, :, :], seqs(src)).then_inc(f_hi, 1)
                        dve.wait_ge(f_hi, i2 + (k + 1))
                        dve.tensor_tensor(xl[:, :, :], seqs(src), xh[:, :, :].bitcast(F32), ALU.subtract)\
                            .then_inc(f_split, 1)

                    def low(s):
                        cn = FCH[s % 3][1]
                        dve.wait_ge(f_hhi, i6 + (s + 1))
                        dve.tensor_tensor(hl[0:cn, s % 2, :], ab[0:cn, s % 2, 1, :], hh[0:cn, s % 2, :].bitcast(F32),
                                          ALU.subtract).then_inc(f_hlo, 1)

                    def residual(k):
                        dve.wait_ge(f_dn, i6 + (3 * k + 3))
                        dst = xT[:, bass.ds((g2 * 2 + k) * GT, GT)]
                        dve.scalar_tensor_tensor(dst, bank[6 + k][:, :], lv[:, V_B2:V_B2 + 1], dst, ALU.add, ALU.add)\
                            .then_inc(f_add, 1)

                    split(0)
                    for s in range(FFS):
                        c = s % 3
                        cn = FCH[c][1]
                        if s == 3:
                            split(1)
                        dve.wait_ge(f_gelu, i6 + (s + 1))
                        if s >= 2:
                            dve.wait_ge(f_hlo, i6 + (s - 1))
                        dve.scalar_tensor_tensor(ab[0:cn, s % 2, 1, :], bank[2 * (s % 3)][0:cn, :],
                                                 lv[0:cn, V_B1A + c:V_B1A + c + 1], ab[0:cn, s % 2, 0, :],
                                                 ALU.add, ALU.mult).then_inc(f_h, 1)
                        low(s)
                    residual(0)
                    residual(1)
            dve.wait_ge(s_in, 32)
            with dve.Fori(0, GROUPS) as g:
                dve.wait_ge(g_silu, g + 1)
                dve.wait_ge(g_T, g + CREDIT)
                dve.tensor_tensor(ab[:, 1, 0, :], ab[:, 0, 0, :], rotw[:, bass.ds(TOKENS + g * GT, GT)], ALU.mult)\
                    .then_inc(g_mul, 1)
                dve.wait_ge(g_T, g + 1 + CREDIT)
                dst = rotw[:, bass.ds(g * GT, GT)]
                dve.tensor_tensor(dst, dst, bank[0][:, :], ALU.add).then_inc(g_out, 1)


def constants():
    half = np.arange(0, DH, 2, dtype=np.float32)
    inv_freq = (np.float32(1.0) / np.float32(10000.0) ** (half / np.float32(DH))).astype(np.float32)
    t = np.arange(SEQ, dtype=np.float32)
    freqs = t[:, None] * inv_freq[None, :]
    base = (half + np.float32(0.4 * DH)) / np.float32(1.4 * DH)
    power = (t - SEQ // 2) / np.float32(WINDOW // 2)
    scale = (base[None, :] ** power[:, None]).astype(np.float32)
    f = np.tile(freqs, (1, 4)).T
    s = np.tile(scale, (1, 4)).T
    sign = np.where(np.arange(P) % DH < DH // 2, -1.0, 1.0).astype(np.float32)[:, None]
    inv = (np.float32(1.0) / s).astype(np.float32)
    tabs = np.stack([np.cos(f) * s, -np.sin(f) * s * sign, np.cos(f) * inv, -np.sin(f) * inv * sign], 1)
    q = np.arange(P)[:, None]
    own = np.arange(P)[None, :]
    wide = np.arange(P + WINDOW)[None, :] - WINDOW

    def band(k):
        return np.where((k > q) | (k < q - WINDOW), MASKED, 0.0)

    mask = np.concatenate([band(own), band(wide)], 1)
    headsum = np.zeros((P, 4, 32))
    headpick = np.zeros((P, 4, P))
    for p in range(4):
        for i in range(2):
            headsum[64 * i:64 * i + 64, p, 2 * p + i] = 1.0
    for p in range(4):
        for i in range(2):
            for half in range(2):
                headpick[64 * half + 32 + 2 * p + i, p, 64 * i:64 * i + 64] = 2.0 ** (R_LOG2 // 2)
    statepick = np.zeros((2 * D_STATE, 2 * D_STATE, P))
    for n in range(2 * D_STATE):
        statepick[n, n, :] = 1.0
    return {k: np.ascontiguousarray(v.astype(np.float32)) for k, v in dict(
        tabs_c=tabs, mask_c=mask, ident_c=np.eye(P), headsum_c=headsum, headpick_c=headpick,
        statepick_c=statepick).items()}


def columns(*vectors):
    cols = []
    for v in vectors:
        c = np.zeros((P,), np.float32)
        c[:v.shape[0]] = v
        cols.append(c)
    return np.stack(cols, 1)


def kernel(**inputs):
    import concourse.bacc as bacc
    from concourse.bass_utils import run_bass_kernel_spmd as run

    i = {k: np.asarray(v) for k, v in inputs.items()}
    A, F = "L0_attn_", "L0_ffn_"
    cxw, czw = i[A + "conv_x_w"][:, 0, :], i[A + "conv_z_w"][:, 0, :]
    mvec = columns(*[cxw[k] for k in range(D_CONV)], *[czw[k] for k in range(D_CONV)], i[A + "conv_x_b"],
                   i[A + "conv_z_b"], i[A + "inv_dt"], i[A + "D"], i[A + "b_out"])
    lay = []
    for l in range(DEPTH):
        qs, ks, b1 = i[F + "q_scale"][l], i[F + "k_scale"][l], i[F + "b1"][l]
        lay.append(columns(np.tile(qs, 2), np.tile(ks, 2),
                           i[F + "ln_g"][l], i[F + "ln_b"][l], i[F + "b2"][l],
                           *[b1[c0:c0 + cn] for c0, cn in FCH], *[b1[FF + c0:FF + c0 + cn] for c0, cn in FCH]))
    arrays = dict(x_in=i[A + "x"], W_in=i[A + "W_in"], W_xdbl=i[A + "W_xdbl"], W_dt=i[A + "W_dt"],
                  W_out=i[A + "W_out"], mvec=mvec, Wqkv=i[F + "Wqkv"], Wo=i[F + "Wo"], W1=i[F + "W1"],
                  W2=i[F + "W2"], lvec=np.concatenate(lay, 1), **constants())
    arrays = {k: np.ascontiguousarray(v) for k, v in arrays.items()}
    nc = bacc.Bacc("TRN2", target_bir_lowering=False, num_devices=1)
    aps = {n: nc.dram_tensor(n, a.shape, mybir.dt.from_np(a.dtype), kind="ExternalInput").ap()
           for n, a in arrays.items()}
    out = nc.dram_tensor("out", (BATCH, SEQ, DIM), F32, kind="ExternalOutput").ap()
    build(nc, **aps, out=out)
    r = run(nc, [arrays], core_ids=[0])
    return r.results[0]["out"]
```

```python
from contextlib import ExitStack

import numpy as np

import concourse.bass as bass
from concourse import mybir

ALU = mybir.AluOpType
ACT = mybir.ActivationFunctionType
AX_X = mybir.AxisListType.X
F32 = mybir.dt.float32
F32R = mybir.dt.float32r

P = 128
BATCH, SEQ, DIM = 16, 256, 128
TOKENS = BATCH * SEQ
GB = 2
GT = GB * SEQ
GROUPS = TOKENS // GT
TILES = TOKENS // P
DEPTH, HEADS, DH, WINDOW = 6, 16, 64, 32
INNER = HEADS * DH
PAIRS = HEADS // 2
FF = int(DIM * 4 * 2 / 3)
FCH = [(0, 128), (128, 128), (256, FF - 256)]
D_STATE, DT_RANK, D_CONV = 16, 64, 4
QK_SCALE = 8.0
MASKED = -1e30
R_LOG2 = 24
NBLK = 2 * PAIRS
STEPS = PAIRS * GB
UW = 2 * P + WINDOW
V_QS, V_KS, V_G, V_B, V_B2, V_B1A, V_B1G, NVEC = 0, 1, 2, 3, 4, 5, 8, 11
M_CXW, M_CZW, M_CXB, M_CZB, M_DT2, M_D, M_BO, NMV = 0, 4, 8, 9, 10, 11, 12, 13
FFG = 4
LNG = 4
CREDIT = 1
VCH = 4
VW = INNER // VCH
BANK_STEPS = [[("next", "qk", 0)],
              [("next", "qk", 1), ("cur", "v", 4)],
              [("next", "qk", 2), ("cur", "v", 5)],
              [("next", "qk", 3), ("cur", "rqT", 1)],
              [("next", "qk", 4), ("cur", "rk", 4), ("prev", "wo", 0)],
              [("next", "qk", 5), ("cur", "rk", 5), ("prev", "wo", 1)],
              [("next", "qk", 6), ("cur", "rk", 6), ("cur", "rk", 7)],
              [("next", "qk", 7), ("cur", "v", 6)],
              [("next", "qk", 8), ("cur", "v", 7)],
              [("next", "qk", 9), ("next", "v", 0)],
              [("next", "qk", 10), ("next", "v", 1)],
              [("next", "qk", 11), ("next", "rqT", 0)],
              [("next", "qk", 12), ("next", "rk", 0), ("next", "rk", 1)],
              [("next", "qk", 13), ("next", "rk", 2), ("next", "rk", 3)],
              [("next", "qk", 14), ("next", "v", 2)],
              [("next", "qk", 15), ("next", "v", 3)]]
BANK_USES = [use for step in BANK_STEPS for use in step]
BANK_OF = {use[1:]: k % 3 for k, use in enumerate(BANK_USES)}
DRAIN = 7


def build(nc, x_in, W_in, W_xdbl, W_dt, W_out, mvec, Wqkv, Wo, W1, W2, lvec, tabs_c, mask_c, ident_c,
          headsum_c, headpick_c, statepick_c, out):
    ctx = ExitStack()
    with ctx:
        def sb(name, shape, dt=F32):
            return ctx.enter_context(nc.sbuf_tensor(name, shape, dt))

        def sem(name):
            return ctx.enter_context(nc.semaphore(name))

        xT = sb("xT", [P, TOKENS + GT])
        rot = sb("rot", [P, 2 * PAIRS, GT])
        wide = sb("wide", [P, PAIRS, GT])
        sq = sb("sq", [P, 4, GT])
        vtok = sb("vtok", [P, 4, INNER])
        wqk_h = sb("wqk_h", [P, NBLK, P], F32R)
        wqk_l = sb("wqk_l", [P, NBLK, P], F32R)
        wv_h = sb("wv_h", [P, INNER], F32R)
        wv_l = sb("wv_l", [P, INNER], F32R)
        w1_h = sb("w1_h", [P, 2 * FF], F32R)
        w1_l = sb("w1_l", [P, 2 * FF], F32R)
        w2_h = sb("w2_h", [P, 3, P], F32R)
        w2_l = sb("w2_l", [P, 3, P], F32R)
        wo = sb("wo", [P, PAIRS, P])
        xh = sb("xh", [P, 2, GB, SEQ], F32R)
        xl = sb("xl", [P, 2, GB, SEQ], F32R)
        ab = sb("ab", [P, 2, 2, GT])
        swp = sb("swp", [P, 2, GT])
        hh = sb("hh", [P, 2, GT], F32R)
        hl = sb("hl", [P, 2, GT], F32R)
        sm = sb("sm", [P, 2, 2, UW])
        pr = sb("pr", [P, 4, 2, UW])
        pt = sb("pt", [P, 2, 2, 2 * P])
        pp = sb("pp", [P, 2, 2, WINDOW])
        nh = sb("nh", [P, GT], F32R)
        nl = sb("nl", [P, GT], F32R)
        tab = sb("tab", [P, 4, SEQ])
        ltab = sb("ltab", [P, 4, SEQ])
        mask = sb("mask", [P, UW])
        ident = sb("ident", [P, P])
        headsum = sb("headsum", [P, 4, 32])
        headpick = sb("headpick", [P, PAIRS, P], F32R)
        mean_w = sb("mean_w", [P, P])
        rsum = sb("rsum", [P, GT])
        rq = sb("rq", [P, 2, 4, 8])
        nrq = sb("nrq", [P, 2, 4, 8])
        credit = sb("credit", [P, 64])
        mx = sb("mx", [P, STEPS, 2, 2])
        nb = sb("nb", [P, STEPS, 2, 2])
        den = sb("den", [P, STEPS, 2, 2])
        rden = sb("rden", [P, STEPS, 2, 2])
        lv_all = sb("lv_all", [P, DEPTH * NVEC])
        lv = sb("lv", [P, NVEC])
        mv = sb("mv", [P, NMV])
        st = sb("st", [P, 4, TILES])
        eps = sb("eps", [P, 1])
        bank = [ctx.enter_context(nc.psum_tensor(f"bank{i}", [P, GT], F32)) for i in range(8)]
        s_dram = nc.dram_tensor("s_scratch", (P, TOKENS), F32, kind="Internal").ap()

        rotw = rot[:, :, :].rearrange("p a n -> p (a n)")
        wide_f = wide[:, :, :].rearrange("p a n -> p (a n)")
        vt_f = vtok[:, :, :].rearrange("p a n -> p (a n)")
        xtok = rotw[:, 0:TOKENS].rearrange("p (t c) -> p t c", c=DIM)
        xsq = rotw[:, TOKENS:2 * TOKENS].rearrange("p (t c) -> p t c", c=DIM)
        statepick = vt_f[:, 0:32 * P].rearrange("p (n c) -> p n c", c=P)
        pick_B, pick_C = wqk_h, wqk_l
        xd_h, xd_l = hh[0:96, 0, :], hl[0:96, 0, :]
        w_in = ab[:, 0, 0, 0:2 * P]
        w_xdbl = ab[:, 0, 1, 0:DT_RANK + 2 * D_STATE]
        w_dt = ab[:, 1, 0, 0:P]
        w_out = ab[:, 1, 1, 0:2 * P]
        PADW = SEQ + D_CONV - 1
        pad_x = sm[:, 0, :, 0:PADW]
        pad_z = sm[:, 1, :, 0:PADW]
        ct = [rot[:, i, :] for i in range(4)]
        u, z_act, xd, delta, du, acc, yy, dtmp = (rot[:, 4 + i, :] for i in range(8))
        dA = [rot[:, 12 + i, :] for i in range(2)]
        dBu = [rot[:, 14 + i, :] for i in range(2)]
        hst = [wide[:, i, :] for i in range(2)]
        hC = [wide[:, 2 + i, :] for i in range(2)]
        sp = [wide[:, 4 + i, :] for i in range(2)]
        s_out = wide[:, 6, :]
        lnx = [vt_f[:, k * GT:(k + 1) * GT] for k in range(LNG)]
        lny = [vt_f[:, (LNG + k) * GT:(LNG + k + 1) * GT] for k in range(LNG)]
        raw_qkv = rotw[:, 0:3 * INNER]
        raw_wo = rotw[:, 3 * INNER:4 * INNER].rearrange("p (t c) -> p t c", c=P)
        raw_w1 = rotw[:, 4 * INNER:4 * INNER + 2 * FF]
        raw_w2 = rotw[:, 4 * INNER + 2 * FF:4 * INNER + 2 * FF + 3 * P].rearrange("p (t c) -> p t c", c=P)

        consts_in = sem("consts_in")
        xtok_in = sem("xtok_in")
        link = {e: sem(f"{e}_link") for e in ("dve", "act")}
        ln0_mean = sem("ln0_mean")
        ln0_sq = sem("ln0_sq")
        ln0_var = sem("ln0_var")
        ln0_rstd = sem("ln0_rstd")
        ln0_xn = sem("ln0_xn")
        ln0_tr = sem("ln0_tr")
        ln0_xT = sem("ln0_xT")
        consts_made = sem("consts_made")
        m_proj, m_pad, m_conv, m_silu, m_xdbl, m_xd = (sem(f"m_{n}") for n in ("proj", "pad", "conv", "silu", "xdbl", "xd"))
        m_dt, m_soft, m_soft2, m_softl, m_delta, m_B, m_C = (
            sem(f"m_{n}") for n in ("dt", "soft", "soft2", "softl", "delta", "B", "C"))
        m_dA, m_dBu, m_scan, m_hC, m_acc, m_y, m_s, m_sout, m_sdma = (
            sem(f"m_{n}") for n in ("dA", "dBu", "scan", "hC", "acc", "y", "s", "sout", "sdma"))
        m_x, m_cv, m_rl, m_du = (sem(f"m_{n}") for n in ("x", "cv", "rl", "du"))
        m_xh, m_xsplit = sem("m_xh"), sem("m_xsplit")
        w_in_sem = sem("w_loaded")
        w_hi, w_lo = sem("w_hi"), sem("w_lo")
        lvec_ok = sem("lvec_ok")
        x_hi, x_split = sem("x_hi"), sem("x_split")
        swap_in = [sem(f"swap_in_{r}") for r in range(2)]
        qk_proj, qk_sq, qk_mul, qk_rot = sem("qk_proj"), sem("qk_sq"), sem("qk_mul"), sem("qk_rot")
        sq_part, sq_clamp, r_ln, r_exp, r_hi, r_split = (
            sem(n) for n in ("sq_part", "sq_clamp", "r_ln", "r_exp", "r_hi", "r_split"))
        v_proj, v_sb = sem("v_proj"), sem("v_sb")
        rq_T, rq_sb = sem("rq_T"), sem("rq_sb")
        rk_bc, k_norm = sem("rk_bc"), sem("k_norm")
        sc_ps, sc_max, sc_bias, p_exp, p_rden, p_norm, p_T, p_Tsb, o_ps, o_sb = (
            sem(n) for n in ("sc_ps", "sc_max", "sc_bias", "p_exp", "p_rden", "p_norm", "p_T", "p_Tsb", "o_ps", "o_sb"))
        at_out, at_add = sem("at_out"), sem("at_add")
        l_sh, l_mean, l_xc, l_sq, l_var, l_ln, l_rstd, l_mul, l_xn = (
            sem(n) for n in ("l_sh", "l_mean", "l_xc", "l_sq", "l_var", "l_ln", "l_rstd", "l_mul", "l_xn"))
        f_hi, f_split, f_up, f_gelu, f_h, f_hhi, f_hlo, f_dn, f_add = (
            sem(n) for n in ("f_hi", "f_split", "f_up", "f_gelu", "f_h", "f_hhi", "f_hlo", "f_dn", "f_add"))
        s_in = sem("s_in")
        g_silu, g_mul, g_T, g_out, out_dma = (sem(n) for n in ("g_silu", "g_mul", "g_T", "g_out", "out_dma"))

        NCONST = 12
        FFS = FFG * len(FCH)
        credited = [m_sout, m_conv, m_s, m_sdma, x_hi, x_split, qk_proj, qk_sq, qk_mul, qk_rot, sq_part, sq_clamp,
                    r_ln, r_exp, r_hi, r_split, v_proj, v_sb, rq_T, rq_sb, rk_bc, k_norm, sc_ps, sc_max, sc_bias,
                    p_exp, p_rden, p_norm, p_T, p_Tsb, o_ps, o_sb, at_out, at_add, l_sh, l_mean, l_xc, l_sq, l_var,
                    l_ln, l_rstd, l_mul, l_xn, f_hi, f_split, f_up, f_gelu, f_h, f_hhi, f_hlo, f_dn, f_add,
                    g_mul, g_T, g_out]
        block = ctx.enter_context(nc.Block())

        def held(eng, n):
            eng.to_reg(n)
            return n

        class Bases:
            def __init__(self, eng, it):
                self.n1 = eng.snap(it + CREDIT)
                self.n2 = eng.snap(it * 2 + CREDIT)
                self.n8 = eng.snap(it * 8 + CREDIT)
                self.n16 = eng.snap(it * 16 + CREDIT)
                self.n32 = eng.snap(it * 32 + CREDIT)

        def use_bank(kind, i):
            return bank[4 + BANK_OF[kind, i]]

        def group_of(role, o):
            return o[("prev", "cur", "next").index(role)]

        def layer_turns(eng, l, turn):
            x_base = eng.snap(l * (GROUPS + 1) + CREDIT)
            turn(Bases(eng, eng.snap(l * GROUPS)), (None, None, 0), 0, 0, x_base)
            turn(Bases(eng, eng.snap(l * GROUPS)), (None, 0, 1), 0, 0, x_base)
            with eng.Fori(0, (GROUPS - 2) // 2) as h:
                for k in range(2):
                    g = eng.snap(h * 2 + (1 + k))
                    turn(Bases(eng, eng.snap(l * GROUPS + g)), (-1, 0, 1), 1 - k, g,
                         eng.snap(l * (GROUPS + 1) + g + CREDIT))
            turn(Bases(eng, eng.snap(l * GROUPS + (GROUPS - 1))), (-1, 0, None), 1, GROUPS - 1, None)
            turn(Bases(eng, eng.snap(l * GROUPS + (GROUPS - 1))), (0, None, None), 1, GROUPS - 1, None)

        def head_scale(t, p, b):
            return t[:, p // 4, 2 * b:2 * b + 2, 2 * (p % 4):2 * (p % 4) + 2]

        def three_pass(eng, o, wh, wl, ah, al):
            eng.matmul(o, wh, ah, start=True, stop=False)
            eng.matmul(o, wl, ah, start=False, stop=False)
            return eng.matmul(o, wh, al, start=False, stop=True)

        def settle(eng):
            eng.wait_ge(consts_made, 1)

        def seqs(ap):
            return ap.rearrange("p (b t) -> p b t", b=GB)

        @block.sync
        def _(sp_e):
            sp_e.dma_start(xtok, x_in.rearrange("b (t p) c -> p (b t) c", p=P)).then_inc(xtok_in, 16)
            for dst, src in ((ident[:, :], ident_c), (w_in, W_in), (mv[:, :], mvec),
                             (w_xdbl, W_xdbl), (w_dt[0:DT_RANK, :], W_dt),
                             (w_out[:, :].rearrange("p (t c) -> p t c", t=2), W_out.rearrange("(t p) c -> p t c", p=P)),
                             (statepick[0:96, :, :], statepick_c), (lv_all[:, :], lvec),
                             (tab[:, :, :], tabs_c), (mask[:, :], mask_c), (headsum[:, :, :], headsum_c),
                             (wide[:, 0:2, :].rearrange("p a n -> p (a n)").rearrange("p (t c) -> p t c", c=P), headpick_c)):
                sp_e.dma_start(dst, src).then_inc(consts_in, 16)
            with sp_e.Fori(0, GROUPS) as g:
                sp_e.wait_ge(m_sout, g + 1 + CREDIT)
                sp_e.dma_start(s_dram[:, bass.ds(g * GT, GT)], s_out).then_inc(m_sdma, 16)
            sp_e.wait_ge(m_sdma, 16 * GROUPS + CREDIT)

            def swaps(n16, o):
                for j in range(16):
                    made = held(sp_e, n16 + (16 * o + j + 1))
                    sp_e.wait_ge(qk_mul, made)
                    for r in range(0, P, 32):
                        src = r + 32 if r % 64 == 0 else r - 32
                        sp_e.dma_start(swp[r:r + 32, j % 2, :], ab[src:src + 32, j % 2, 1, :])\
                            .then_inc(swap_in[j % 2], 16)

            with sp_e.Fori(0, DEPTH) as l:
                sp_e.wait_ge(at_out, l * (2 * GROUPS) + CREDIT)
                sp_e.dma_start(raw_qkv, Wqkv[bass.ds(l, 1), :, :].rearrange("l p n -> p (l n)")).then_inc(w_in_sem, 16)
                sp_e.dma_start(raw_wo, Wo[bass.ds(l, 1), :, :].rearrange("l (t p) c -> p (l t) c", p=P)).then_inc(w_in_sem, 16)
                sp_e.dma_start(raw_w1, W1[bass.ds(l, 1), :, :].rearrange("l p n -> p (l n)")).then_inc(w_in_sem, 16)
                sp_e.dma_start(raw_w2[:, 0:2, :], W2[bass.ds(l, 1), 0:256, :].rearrange("l (t p) c -> p (l t) c", p=P))\
                    .then_inc(w_in_sem, 16)
                sp_e.dma_start(raw_w2[0:FCH[2][1], 2:3, :], W2[bass.ds(l, 1), 256:FF, :].rearrange("l p c -> p l c"))\
                    .then_inc(w_in_sem, 16)
                swaps(sp_e.snap(l * (GROUPS * 16) + CREDIT), 0)
                with sp_e.Fori(0, GROUPS - 1) as g:
                    swaps(sp_e.snap((l * GROUPS + g) * 16 + CREDIT), 1)
            sp_e.wait_ge(at_out, DEPTH * 2 * GROUPS + CREDIT)
            sp_e.dma_start(xtok, x_in.rearrange("b (t p) c -> p (b t) c", p=P)).then_inc(s_in, 16)
            sp_e.dma_start(rotw[:, TOKENS:2 * TOKENS], s_dram[:, :]).then_inc(s_in, 16)
            ov = out.rearrange("b (t p) c -> p (b t) c", p=P)
            with sp_e.Fori(0, GROUPS) as g:
                sp_e.wait_ge(g_out, g + 1 + CREDIT)
                sp_e.dma_start(ov[:, bass.ds(g * 4, 4), :], xtok[:, bass.ds(g * 4, 4), :]).then_inc(out_dma, 16)
            sp_e.wait_ge(out_dma, 16 * GROUPS)

        @block.tensor
        def _(pe):
            pe.wait_ge(consts_in, 16 * NCONST)
            pe.wait_ge(ln0_xn, 1)
            for t in range(TILES):
                if t >= 16 and t % 4 == 0:
                    pe.wait_ge(ln0_xT, t // 4 - 3)
                mm = pe.transpose(bank[t // 4 % 4][:, t % 4 * P:t % 4 * P + P], xtok[:, t, :], ident[:, :])
                if t % 4 == 3:
                    mm.then_inc(ln0_tr, 1)
            pe.wait_ge(ln0_xT, GROUPS)
            with pe.Fori(0, GROUPS) as g:
                pe.wait_ge(m_x, g + 1)
                pe.wait_ge(m_sout, g + CREDIT)
                pe.matmul(bank[0][:, :], w_in[:, 0:P], dtmp, start=True, stop=True).then_inc(m_proj, 1)
                pe.matmul(bank[1][:, :], w_in[:, P:2 * P], dtmp, start=True, stop=True).then_inc(m_proj, 1)
                pe.wait_ge(m_silu, g * 2 + 1)
                pe.matmul(bank[2][0:96, :], w_xdbl, u, start=True, stop=True).then_inc(m_xdbl, 1)
                pe.wait_ge(m_xd, g + 1)
                pe.matmul(bank[3][:, :], w_dt[0:DT_RANK, :], xd[0:DT_RANK, :], start=True, stop=True).then_inc(m_dt, 1)
                pe.wait_ge(m_xsplit, g + 1)
                for n in range(D_STATE):
                    if n >= 2:
                        pe.wait_ge(m_dBu, g * D_STATE + n - 1)
                    pe.matmul(bank[4 + n % 2][:, :], pick_B[0:96, n, :], xd_h, start=True, stop=False)
                    pe.matmul(bank[4 + n % 2][:, :], pick_B[0:96, n, :], xd_l, start=False, stop=True).then_inc(m_B, 1)
                    if n >= 2:
                        pe.wait_ge(m_hC, g * D_STATE + n - 1)
                    pe.matmul(bank[6 + n % 2][:, :], pick_C[0:96, n, :], xd_h, start=True, stop=False)
                    pe.matmul(bank[6 + n % 2][:, :], pick_C[0:96, n, :], xd_l, start=False, stop=True).then_inc(m_C, 1)
                pe.wait_ge(m_y, g + 1)
                pe.wait_ge(m_silu, g * 2 + 2)
                pe.matmul(bank[2][:, :], w_out[:, 0:P], yy, start=True, stop=False)
                pe.matmul(bank[2][:, :], w_out[:, P:2 * P], z_act, start=False, stop=True).then_inc(m_s, 1)
            pe.wait_ge(consts_made, 1)
            pe.wait_ge(m_sout, GROUPS + CREDIT)
            with pe.Fori(0, DEPTH) as l:
                def turn(n, o, par, g, x_base):
                    prev, cur, nxt = o

                    def at(kind, i, q):
                        return {"qk": (qk_sq, n.n16, 16), "v": (v_sb, n.n8, 8), "rk": (k_norm, n.n8, 8),
                                "rqT": (rq_sb, n.n2, 2), "wo": (at_add, n.n2, 2)}[kind], i, q

                    def free_bank(k):
                        for b in range(k - 3, -len(BANK_USES) - 1, -3):
                            role, kind, i = BANK_USES[b]
                            q = group_of(role, o)
                            if b < 0:
                                q = {"next": cur, "cur": prev, "prev": None if prev is None else prev - 1}[role]
                            if q is not None:
                                (read, base, per), i, q = at(kind, i, q)
                                if q * per + i + 1 >= 0 or prev is not None:
                                    pe.wait_ge(read, base + (q * per + i + 1))
                                return

                    def q_norms(h, q, bk):
                        norms = held(pe, n.n2 + (2 * q + h + 1))
                        settle(pe)
                        pe.wait_ge(r_split, norms)
                        for t in range(4):
                            mm = pe.transpose(bk[:, 32 * t:32 * t + 32], rsum[64 * h:64 * h + 32, t * P:t * P + P],
                                              ident[64 * h:64 * h + 32, 64 * h:64 * h + 32])
                        mm.then_inc(rq_T, 1)

                    def k_norms(p, bk):
                        pe.matmul(bk[:, :], headpick[:, p, :], nh[:, :], start=True, stop=False)
                        pe.matmul(bk[:, :], headpick[:, p, :], nl[:, :], start=False, stop=True).then_inc(rk_bc, 1)

                    def project(j, q, bk):
                        if j == 0:
                            pe.wait_ge(x_split, x_base + (q + 1))
                        xb = par if cur is None else 1 - par
                        blk = PAIRS * (j % 2) + j // 2
                        three_pass(pe, bk[:, :], wqk_h[:, blk, :], wqk_l[:, blk, :],
                                   xh[:, xb, :, :].rearrange("p b t -> p (b t)"),
                                   xl[:, xb, :, :].rearrange("p b t -> p (b t)")).then_inc(qk_proj, 1)

                    def make_v(i, role, bk):
                        xb = 1 - par if role == "next" and cur is not None else par
                        c, b = i // 2, i % 2
                        cols = slice(c * VW, c * VW + VW)
                        for t in range(2):
                            mm = three_pass(pe, bk[:, t * VW:t * VW + VW], xh[:, xb, b, t * P:t * P + P],
                                            xl[:, xb, b, t * P:t * P + P], wv_h[:, cols], wv_l[:, cols])
                        mm.then_inc(v_proj, 1)

                    def square_sums(p, q):
                        pe.wait_ge(qk_sq, n.n16 + (16 * q + 2 * p + 2))
                        if p % 4 == 0 and (2 * q + p // 4 > 0 or prev is not None):
                            pe.wait_ge(sq_clamp, n.n2 + (2 * q + p // 4 - 1))
                        for i in range(2):
                            t = 2 * (p // 4) + i
                            mm = pe.matmul(bank[7][32 * t:32 * t + 32, :], headsum[:, p % 4, :],
                                           sq[:, (2 * p + i) % 4, :], start=(p % 4 == 0), stop=(p % 4 == 3),
                                           skip_group_check=True)
                        mm.then_inc(sq_part, 1)

                    def scores(s):
                        p, b = s // 2, s % 2
                        if s % 8 == 0:
                            pe.wait_ge(qk_rot, n.n16 + (8 if s == 0 else 16))
                            pe.wait_ge(k_norm, n.n8 + (4 if s == 0 else 8))
                        for i in range(2):
                            u = 2 * s + i
                            if u >= 2 or prev is not None:
                                pe.wait_ge(sc_max, n.n32 + (u - 1))
                            rows = slice(64 * i, 64 * i + 64)
                            c0 = b * SEQ
                            pe.matmul(bank[i][:, 0:P], rot[rows, p, c0:c0 + P], rot[rows, PAIRS + p, c0:c0 + P],
                                      start=True, stop=True)
                            pe.matmul(bank[i][:, P:UW], rot[rows, p, c0 + P:c0 + SEQ],
                                      rot[rows, PAIRS + p, c0 + P - WINDOW:c0 + SEQ], start=True, stop=True)\
                                .then_inc(sc_ps, 1)

                    def transpose_probs(e, q):
                        pe.wait_ge(p_norm, n.n16 + (16 * q + e + 1))
                        if 16 * q + e >= 0 or prev is not None:
                            pe.wait_ge(p_Tsb, n.n16 + (16 * q + e))
                        for i in range(2):
                            pe.transpose(bank[2][:, 256 * i:256 * i + P], pr[:, e % 4, i, 0:P], ident[:, :])
                            mm = pe.transpose(bank[2][:, 256 * i + P:256 * i + 2 * P],
                                              pr[:, e % 4, i, P + WINDOW:UW], ident[:, :])
                        mm.then_inc(p_T, 1)

                    def outputs(e, q):
                        p, b = e // 2, e % 2
                        if e % 4 == 0:
                            pe.wait_ge(v_sb, n.n8 + (8 * q + e // 2 + 2))
                        pe.wait_ge(p_Tsb, n.n16 + (16 * q + e + 1))
                        pe.wait_ge(o_sb, n.n16 + (16 * q + e))
                        out_i = [bank[3][64 * i:64 * i + 64, :] for i in range(2)]
                        ch = [slice((2 * p + i) * DH, (2 * p + i) * DH + DH) for i in range(2)]
                        for i in range(2):
                            pe.matmul(out_i[i][:, 0:P], vtok[:, 2 * b, ch[i]], pt[:, e % 2, i, 0:P],
                                      start=True, stop=True)
                        for i in range(2):
                            pe.matmul(out_i[i][:, P:2 * P], vtok[:, 2 * b + 1, ch[i]], pt[:, e % 2, i, P:2 * P],
                                      start=True, stop=True)
                        for i in range(2):
                            mm = pe.matmul(out_i[i][:, P:P + WINDOW], vtok[96:128, 2 * b, ch[i]],
                                           pp[96:128, e % 2, i, :], start=False, stop=True, skip_group_check=True)
                        mm.then_inc(o_ps, 1)

                    def project_out(b, q, bk):
                        pe.wait_ge(o_sb, n.n16 + (16 * q + 15 + b))
                        for p in range(PAIRS):
                            mm = pe.matmul(bk[:, 0:SEQ], wo[:, p, :], wide[:, p, b * SEQ:b * SEQ + SEQ],
                                           start=(p == 0), stop=(p == PAIRS - 1))
                        mm.then_inc(at_out, 1)

                    k = 0
                    for s in range(16):
                        if cur is not None:
                            scores(s)
                        if s < 5 and prev is not None:
                            outputs(s + 11, prev)
                        if s >= 5 and cur is not None:
                            outputs(s - 5, cur)
                        if s == 1 and cur is not None:
                            square_sums(7, cur)
                        if s >= 3 and s % 2 == 1 and nxt is not None:
                            square_sums((s - 3) // 2, nxt)
                        if s < 3 and prev is not None:
                            transpose_probs(s + 13, prev)
                        if s >= 3 and cur is not None:
                            transpose_probs(s - 3, cur)
                        for role, kind, i in BANK_STEPS[s]:
                            q = group_of(role, o)
                            if q is not None:
                                free_bank(k)
                                bk = use_bank(kind, i)
                                if kind == "qk":
                                    project(i, q, bk)
                                elif kind == "v":
                                    make_v(i, role, bk)
                                elif kind == "rqT":
                                    q_norms(i, q, bk)
                                elif kind == "rk":
                                    pe.wait_ge(r_split, n.n2 + (2 * q + i // 4 + 1))
                                    k_norms(i, bk)
                                else:
                                    project_out(i, q, bk)
                            k += 1

                pe.wait_ge(w_hi, l + 1)
                pe.wait_ge(w_lo, l + 1)
                layer_turns(pe, l, turn)
                with pe.Fori(0, GROUPS // LNG) as g2:
                    i4 = pe.snap((l * (GROUPS // LNG) + g2) * LNG + CREDIT)
                    for k in range(LNG):
                        pe.wait_ge(l_sh, i4 + (k + 1))
                        pe.matmul(bank[k][:, :], mean_w[:, :], lnx[k], start=True, stop=True).then_inc(l_mean, 1)
                    for k in range(LNG):
                        pe.wait_ge(l_sq, i4 + (k + 1))
                        pe.matmul(bank[4 + k][:, :], mean_w[:, :], lny[k], start=True, stop=True).then_inc(l_var, 1)
                with pe.Fori(0, GROUPS // FFG) as g2:
                    i4 = pe.snap((l * (GROUPS // FFG) + g2) * FFG + CREDIT)
                    i12 = pe.snap((l * (GROUPS // FFG) + g2) * FFS + CREDIT)
                    for s in range(FFS + 2):
                        if s < FFS:
                            k, c = s // 3, s % 3
                            c0, cn = FCH[c]
                            if c == 0:
                                pe.wait_ge(f_split, i4 + (k + 1))
                            if s >= 3:
                                pe.wait_ge(f_h, i12 + (s - 2))
                            xhf = xh[:, k % 2, :, :].rearrange("p b t -> p (b t)")
                            xlf = xl[:, k % 2, :, :].rearrange("p b t -> p (b t)")
                            o = 2 * (s % 3)
                            three_pass(pe, bank[o][0:cn, :], w1_h[:, c0:c0 + cn], w1_l[:, c0:c0 + cn], xhf, xlf)
                            three_pass(pe, bank[o + 1][0:cn, :], w1_h[:, FF + c0:FF + c0 + cn],
                                       w1_l[:, FF + c0:FF + c0 + cn], xhf, xlf).then_inc(f_up, 1)
                        if s >= 2:
                            e = s - 2
                            k, c = e // 3, e % 3
                            cn = FCH[c][1]
                            pe.wait_ge(f_hlo, i12 + (e + 1))
                            if c == 0:
                                pe.wait_ge(f_add, i4 + max(k - 1, 0))
                            o = bank[6 + k % 2][:, :]
                            pe.matmul(o, w2_h[0:cn, c, :], hh[0:cn, e % 2, :], start=(c == 0), stop=False)
                            pe.matmul(o, w2_l[0:cn, c, :], hh[0:cn, e % 2, :], start=False, stop=False)
                            mm = pe.matmul(o, w2_h[0:cn, c, :], hl[0:cn, e % 2, :], start=False, stop=(c == 2))
                            mm.then_inc(f_dn, 1)
            with pe.Fori(0, GROUPS) as g:
                pe.wait_ge(g_mul, g + 1 + CREDIT)
                pe.wait_ge(g_out, g + CREDIT)
                for t in range(4):
                    mm = pe.transpose(bank[0][:, t * P:t * P + P], ab[:, 1, 0, t * P:t * P + P], ident[:, :])
                mm.then_inc(g_T, 1)

        @block.scalar
        def _(act):
            act.wait_ge(ln0_mean, 1)
            act.activation(xsq, xtok, ACT.Square).then_inc(ln0_sq, 1)
            act.wait_ge(ln0_var, 1)
            act.activation(st[:, 2, :], st[:, 1, :], ACT.Ln).then_inc(link["act"], 1)
            act.wait_ge(link["act"], 1)
            act.activation(st[:, 3, :], st[:, 2, :], ACT.Exp, scale=-0.5).then_inc(ln0_rstd, 1)
            act.wait_ge(consts_in, 16 * NCONST)
            act.wait_ge(consts_made, 1)
            with act.Fori(0, GROUPS) as g:
                for i, pad in enumerate((pad_x, pad_z)):
                    act.wait_ge(m_proj, g * 2 + (i + 1))
                    act.wait_ge(m_conv, g * 2 + CREDIT)
                    act.activation(pad[:, :, 1:1 + SEQ], seqs(bank[i][:, :]), ACT.Copy).then_inc(m_pad, 1)
                for i, o in enumerate((u, z_act)):
                    act.wait_ge(m_conv, g * 2 + (i + 1) + CREDIT)
                    act.wait_ge(m_s, g + CREDIT)
                    act.activation(o, ct[i], ACT.Silu).then_inc(m_silu, 1)
                act.wait_ge(m_dt, g + 1)
                act.activation(sp[0], bank[3][:, :], ACT.Abs, bias=mv[:, M_DT2:M_DT2 + 1]).then_inc(m_soft, 1)
                act.wait_ge(m_soft, g + 1)
                act.activation(sp[1], sp[0], ACT.Exp, scale=-1.0).then_inc(m_soft2, 1)
                act.wait_ge(m_soft2, g + 1)
                act.activation(sp[0], sp[1], ACT.Ln, bias=1.0).then_inc(m_softl, 1)
                act.wait_ge(m_delta, g + 1)
                for n in range(D_STATE):
                    if n >= 2:
                        act.wait_ge(m_scan, g * D_STATE + (n - 1))
                    act.activation(dA[n % 2], delta, ACT.Exp, scale=-float(n + 1)).then_inc(m_dA, 1)
                act.wait_ge(m_s, g + 1 + CREDIT)
                act.wait_ge(m_sdma, g * 16 + CREDIT)
                act.activation(s_out, bank[2][:, :], ACT.Identity, bias=mv[:, M_BO:M_BO + 1]).then_inc(m_sout, 1)
            with act.Fori(0, DEPTH) as l:
                act.wait_ge(w_in_sem, l * 80 + 80)
                act.wait_ge(f_dn, l * (GROUPS * 3) + CREDIT)
                act.activation(wqk_h[:, 0:2 * PAIRS, :].rearrange("p a c -> p (a c)"), raw_qkv[:, 0:2 * INNER], ACT.Copy)
                act.activation(wv_h[:, :], raw_qkv[:, 2 * INNER:3 * INNER], ACT.Copy)
                act.activation(w1_h[:, :], raw_w1, ACT.Copy)
                act.activation(w2_h[:, 0:2, :], raw_w2[:, 0:2, :], ACT.Copy)
                act.activation(w2_h[0:FCH[2][1], 2, :], raw_w2[0:FCH[2][1], 2, :], ACT.Copy)
                act.activation(wo[:, :, :], raw_wo, ACT.Copy).then_inc(w_hi, 1)
                act.wait_ge(w_lo, l + 1)

                def turn(n, o, par, g, x_base):
                    prev, cur, nxt = o

                    def square(j, q):
                        act.wait_ge(qk_mul, n.n16 + (16 * q + j + 1))
                        if 8 * q + j // 2 - 1 >= 0 or prev is not None:
                            act.wait_ge(sq_part, n.n8 + (8 * q + j // 2 - 1))
                        act.activation(sq[:, j % 4, :], use_bank("qk", j)[:, :], ACT.Square).then_inc(qk_sq, 1)

                    def probabilities(s):
                        p, b = s // 2, s % 2
                        act.wait_ge(sc_bias, n.n16 + (s + 1))
                        if s >= 4 or prev is not None:
                            act.wait_ge(p_T, n.n16 + (s - 3))
                            act.wait_ge(p_Tsb, n.n16 + (s - 3))
                        for i in range(2):
                            for t in range(2):
                                cs = slice(0, P) if t == 0 else slice(P, UW)
                                ins = act.activation(pr[:, s % 4, i, cs], sm[:, s % 2, i, cs], ACT.Exp,
                                                     bias=nb[:, s, t, i:i + 1], scale=head_scale(rq, p, b)[:, t, i:i + 1],
                                                     accum_out=den[:, s, t, i:i + 1])
                        ins.then_inc(p_exp, 1)

                    def copy_outputs(e, q):
                        p, b = e // 2, e % 2
                        act.wait_ge(o_ps, n.n16 + (16 * q + e + 1))
                        if e < 2 and (2 * q + e - 1 >= 0 or prev is not None):
                            act.wait_ge(at_out, n.n2 + (2 * q + e - 1))
                        act.activation(wide[:, p, b * SEQ:b * SEQ + SEQ], bank[3][:, 0:SEQ], ACT.Copy).then_inc(o_sb, 1)

                    def copy_v(i, q):
                        c, b = i // 2, i % 2
                        act.wait_ge(v_proj, n.n8 + (8 * q + i + 1))
                        act.activation(vtok[:, 2 * b:2 * b + 2, c * VW:c * VW + VW],
                                       use_bank("v", i)[:, :].rearrange("p (t c) -> p t c", t=2), ACT.Copy)\
                            .then_inc(v_sb, 1)

                    def norms(h, q):
                        rows = slice(64 * h, 64 * h + 64)
                        act.wait_ge(sq_clamp, n.n2 + (2 * q + h + 1))
                        act.activation(rsum[rows, :], rsum[rows, :], ACT.Ln, scale=float(2 ** R_LOG2)).then_inc(r_ln, 1)
                        act.wait_ge(r_ln, n.n2 + (2 * q + h + 1))
                        act.activation(rsum[rows, :], rsum[rows, :], ACT.Exp, scale=-0.5).then_inc(r_exp, 1)

                    for s in range(16):
                        if cur is not None:
                            probabilities(s)
                        if s < 5 and prev is not None:
                            copy_outputs(s + 11, prev)
                        if s >= 5 and cur is not None:
                            copy_outputs(s - 5, cur)
                        for role, kind, i in BANK_STEPS[s]:
                            if kind == "v" and group_of(role, o) is not None:
                                copy_v(i, group_of(role, o))
                        if nxt is not None:
                            square(s, nxt)
                        if s == 1 and cur is not None:
                            norms(1, cur)
                        if s == 9 and nxt is not None:
                            norms(0, nxt)

                layer_turns(act, l, turn)
                with act.Fori(0, GROUPS // LNG) as g2:
                    i4 = act.snap((l * (GROUPS // LNG) + g2) * LNG + CREDIT)
                    for k in range(LNG):
                        act.wait_ge(l_xc, i4 + (k + 1))
                        act.activation(lny[k], lnx[k], ACT.Square).then_inc(l_sq, 1)
                    for k in range(LNG):
                        act.wait_ge(l_var, i4 + (k + 1))
                        act.activation(lny[k], bank[4 + k][:, :], ACT.Ln, bias=eps[:, 0:1]).then_inc(l_ln, 1)
                    for k in range(LNG):
                        act.wait_ge(l_ln, i4 + (k + 1))
                        act.activation(lny[k], lny[k], ACT.Exp, scale=-0.5).then_inc(l_rstd, 1)
                with act.Fori(0, GROUPS // FFG) as g2:
                    i12 = act.snap((l * (GROUPS // FFG) + g2) * FFS + CREDIT)
                    for s in range(FFS):
                        k, c = s // 3, s % 3
                        cn = FCH[c][1]
                        act.wait_ge(f_up, i12 + (s + 1))
                        act.wait_ge(f_h, i12 + max(s - 1, 0))
                        act.activation(ab[0:cn, s % 2, 0, :], bank[2 * (s % 3) + 1][0:cn, :], ACT.Gelu,
                                       bias=lv[0:cn, V_B1G + c:V_B1G + c + 1]).then_inc(f_gelu, 1)
                        act.wait_ge(f_h, i12 + (s + 1))
                        act.wait_ge(f_dn, i12 + max(s - 1, 0))
                        act.activation(hh[0:cn, s % 2, :], ab[0:cn, s % 2, 1, :], ACT.Copy).then_inc(f_hhi, 1)
            with act.Fori(0, GROUPS) as g:
                act.wait_ge(f_add, DEPTH * GROUPS + CREDIT)
                act.wait_ge(g_mul, g + CREDIT)
                act.activation(ab[:, 0, 0, :], xT[:, bass.ds(g * GT, GT)], ACT.Silu).then_inc(g_silu, 1)

        @block.gpsimd
        def _(pool):
            for i, c in enumerate(credited):
                pool.memset(credit[:, i:i + 1], 0.0).then_inc(c, CREDIT)
            with pool.Fori(0, GROUPS) as g:
                for n in range(1, D_STATE):
                    pool.wait_ge(m_hC, g * D_STATE + (n + 1))
                    if n > 1:
                        pool.wait_ge(m_acc, g * (D_STATE - 1) + (n - 1))
                    pool.tensor_tensor(acc, hC[0] if n == 1 else acc, hC[n % 2], ALU.add).then_inc(m_acc, 1)
            with pool.Fori(0, DEPTH) as l:
                def turn(n, o, par, g, x_base):
                    prev, cur, nxt = o
                    swaps = pool.snap((n.n1 - CREDIT) * 512)

                    def normalise(e, q):
                        count = held(pool, n.n16 + (16 * q + e + 1))
                        settle(pool)
                        pool.wait_ge(p_rden, count)
                        for i in range(2):
                            for t in range(2):
                                cs = slice(0, P) if t == 0 else slice(P, UW)
                                ins = pool.tensor_scalar(pr[:, e % 4, i, cs], pr[:, e % 4, i, cs],
                                                         rden[:, e, t, i:i + 1], 1.0, ALU.mult, ALU.mult)
                        ins.then_inc(p_norm, 1)

                    def rotate(j, q):
                        pool.wait_ge(swap_in[j % 2], swaps + (512 * q + 64 * (j // 2) + 64))
                        pool.wait_ge(qk_mul, n.n16 + (16 * q + j + 1))
                        pool.tensor_tensor(rot[:, PAIRS * (j % 2) + j // 2, :], ab[:, j % 2, 0, :], swp[:, j % 2, :],
                                           ALU.add).then_inc(qk_rot, 1)

                    for s in range(16):
                        if s < 2 and prev is not None:
                            normalise(s + 14, prev)
                        if s >= 2 and cur is not None:
                            normalise(s - 2, cur)
                        if s < 2 and cur is not None:
                            rotate(s + 14, cur)
                        if s >= 2 and nxt is not None:
                            rotate(s - 2, nxt)

                layer_turns(pool, l, turn)

        @block.vector
        def _(dve):
            chain = [0]

            def linked(ins):
                chain[0] += 1
                ins.then_inc(link["dve"], 1)
                dve.wait_ge(link["dve"], chain[0])

            dve.memset(mean_w[:, :], 1.0 / DIM)
            dve.memset(eps[:, :], 1e-5)
            dve.memset(nh[:, :].bitcast(F32), 0.0)
            dve.memset(nl[:, :].bitcast(F32), 0.0)
            dve.memset(xT[:, TOKENS:], 0.0)
            for pad in (pad_x, pad_z):
                dve.memset(pad[:, :, 0:1], 0.0)
                dve.memset(pad[:, :, 1 + SEQ:PADW], 0.0)
            dve.wait_ge(xtok_in, 16)
            linked(dve.tensor_reduce(st[:, 0, :], xtok, AX_X, ALU.add))
            linked(dve.tensor_scalar(st[:, 1, :], st[:, 0, :], 1.0 / DIM, None, ALU.mult))
            dve.tensor_tensor(xtok, xtok, st[:, 1, :].unsqueeze(2).to_broadcast([P, TILES, DIM]), ALU.subtract)\
                .then_inc(ln0_mean, 1)
            dve.wait_ge(ln0_sq, 1)
            linked(dve.tensor_reduce(st[:, 0, :], xsq, AX_X, ALU.add))
            dve.tensor_scalar(st[:, 1, :], st[:, 0, :], 1.0 / DIM, 1e-5, ALU.mult, ALU.add).then_inc(ln0_var, 1)
            dve.wait_ge(ln0_rstd, 1)
            dve.tensor_tensor(xtok, xtok, st[:, 3, :].unsqueeze(2).to_broadcast([P, TILES, DIM]), ALU.mult)\
                .then_inc(ln0_xn, 1)
            for q in range(GROUPS):
                dve.wait_ge(ln0_tr, q + 1)
                dve.tensor_copy(xT[:, q * GT:q * GT + GT], bank[q % 4][:, :]).then_inc(ln0_xT, 1)
            dve.wait_ge(consts_in, 16 * NCONST)
            dve.tensor_copy(headpick[:, :, :],
                            wide[:, 0:2, :].rearrange("p a n -> p (a n)").rearrange("p (t c) -> p t c", c=P))
            dve.tensor_copy(pick_B[0:96, :, :], statepick[0:96, 0:D_STATE, :])
            dve.tensor_copy(pick_C[0:96, :, :], statepick[0:96, D_STATE:2 * D_STATE, :])
            dve.tensor_scalar(mv[:, M_DT2:M_DT2 + 1], mv[:, M_DT2:M_DT2 + 1], 2.0, None, ALU.mult).then_inc(consts_made, 1)
            dve.wait_ge(consts_made, 1)
            dve.wait_ge(ln0_xT, GROUPS)
            with dve.Fori(0, GROUPS) as g:
                g16 = dve.snap(g * D_STATE)
                dve.wait_ge(m_s, g + CREDIT)
                dve.tensor_copy(dtmp, xT[:, bass.ds(g * GT, GT)]).then_inc(m_x, 1)
                for i, (pad, w0, b0) in enumerate(((pad_x, M_CXW, M_CXB), (pad_z, M_CZW, M_CZB))):
                    dve.wait_ge(m_pad, g * 2 + (i + 1))
                    dve.tensor_scalar(seqs(ct[2 + i]), pad[:, :, 0:SEQ], mv[:, w0:w0 + 1], mv[:, b0:b0 + 1],
                                      ALU.mult, ALU.add).then_inc(m_cv, 1)
                    for k in range(1, D_CONV):
                        src, dst = (ct[2 + i], ct[i]) if k % 2 else (ct[i], ct[2 + i])
                        dve.wait_ge(m_cv, g * 6 + (i * 3 + k))
                        ins = dve.scalar_tensor_tensor(seqs(dst), pad[:, :, k:k + SEQ], mv[:, w0 + k:w0 + k + 1],
                                                       seqs(src), ALU.mult, ALU.add)
                        ins.then_inc(m_cv if k < D_CONV - 1 else m_conv, 1)
                dve.wait_ge(m_xdbl, g + 1)
                dve.tensor_copy(xd[0:96, :], bank[2][0:96, :]).then_inc(m_xd, 1)
                dve.wait_ge(m_xd, g + 1)
                dve.tensor_copy(xd_h, xd[0:96, :]).then_inc(m_xh, 1)
                dve.wait_ge(m_xh, g + 1)
                dve.tensor_tensor(xd_l, xd[0:96, :], xd_h.bitcast(F32), ALU.subtract).then_inc(m_xsplit, 1)
                dve.wait_ge(m_dt, g + 1)
                dve.wait_ge(m_soft, g + 1)
                dve.tensor_scalar(delta, bank[3][:, :], mv[:, M_DT2:M_DT2 + 1], 0.0, ALU.add, ALU.max).then_inc(m_rl, 1)
                dve.wait_ge(m_softl, g + 1)
                dve.wait_ge(m_rl, g + 1)
                dve.tensor_tensor(delta, delta, sp[0], ALU.add).then_inc(m_delta, 1)
                dve.wait_ge(m_delta, g + 1)
                dve.tensor_tensor(du, delta, u, ALU.mult).then_inc(m_du, 1)
                dve.wait_ge(m_du, g + 1)

                def emit(n):
                    dve.wait_ge(m_C, g16 + (n + 1))
                    dve.wait_ge(m_scan, g16 + (n + 1))
                    if n >= 2:
                        dve.wait_ge(m_acc, g * (D_STATE - 1) + max(1, n - 2))
                    dve.tensor_tensor(hC[n % 2], hst[n % 2], bank[6 + n % 2][:, :], ALU.mult).then_inc(m_hC, 1)

                for n in range(D_STATE):
                    dve.wait_ge(m_B, g16 + (n + 1))
                    if n >= 2:
                        dve.wait_ge(m_hC, g16 + (n - 1))
                    dve.tensor_tensor(dBu[n % 2], du, bank[4 + n % 2][:, :], ALU.mult).then_inc(m_dBu, 1)
                    if n >= 1:
                        emit(n - 1)
                    dve.wait_ge(m_dBu, g16 + (n + 1))
                    dve.wait_ge(m_dA, g16 + (n + 1))
                    for b in range(GB):
                        cs = slice(b * SEQ, b * SEQ + SEQ)
                        ins = dve.tensor_tensor_scan(hst[n % 2][:, cs], dA[n % 2][:, cs], dBu[n % 2][:, cs], 0.0,
                                                     ALU.mult, ALU.add)
                    ins.then_inc(m_scan, 1)
                emit(D_STATE - 1)
                dve.wait_ge(m_acc, (g + 1) * (D_STATE - 1))
                dve.scalar_tensor_tensor(yy, u, mv[:, M_D:M_D + 1], acc, ALU.mult, ALU.add).then_inc(m_y, 1)
            dve.wait_ge(m_sout, GROUPS + CREDIT)
            with dve.Fori(0, DEPTH) as l:
                dve.wait_ge(w_in_sem, l * 80 + 80)
                dve.wait_ge(w_hi, l + 1)
                dve.wait_ge(f_add, l * GROUPS + CREDIT)
                dve.tensor_tensor(wqk_l[:, 0:2 * PAIRS, :].rearrange("p a c -> p (a c)"), raw_qkv[:, 0:2 * INNER],
                                  wqk_h[:, 0:2 * PAIRS, :].rearrange("p a c -> p (a c)").bitcast(F32), ALU.subtract)
                dve.tensor_tensor(wv_l[:, :], raw_qkv[:, 2 * INNER:3 * INNER], wv_h[:, :].bitcast(F32), ALU.subtract)
                dve.tensor_tensor(w1_l[:, :], raw_w1, w1_h[:, :].bitcast(F32), ALU.subtract)
                n2 = FCH[2][1]
                dve.tensor_tensor(w2_l[:, 0:2, :], raw_w2[:, 0:2, :], w2_h[:, 0:2, :].bitcast(F32), ALU.subtract)
                dve.tensor_tensor(w2_l[0:n2, 2, :], raw_w2[0:n2, 2, :], w2_h[0:n2, 2, :].bitcast(F32), ALU.subtract)\
                    .then_inc(w_lo, 1)
                dve.tensor_copy(lv[:, :], lv_all[:, bass.ds(l * NVEC, NVEC)]).then_inc(lvec_ok, 1)
                dve.wait_ge(lvec_ok, l * 2 + 1)
                for i, c in enumerate((V_QS, V_QS, V_KS, V_KS)):
                    ins = dve.tensor_scalar(ltab[:, i, :], tab[:, i, :], lv[:, c:c + 1], None, ALU.mult)
                ins.then_inc(lvec_ok, 1)
                dve.wait_ge(lvec_ok, l * 2 + 2)

                def split_x(g, buf, count):
                    xlo = seqs(xT[0:64, bass.ds(g * GT, GT)])
                    xhi = seqs(xT[64:128, bass.ds(g * GT, GT)])
                    hi, lo = xh[:, buf, :, :], xl[:, buf, :, :]
                    dve.tensor_copy(hi[0:64], xlo)
                    dve.tensor_copy(hi[64:128, :, 1:SEQ], xhi[:, :, 0:SEQ - 1]).then_inc(x_hi, 1)
                    dve.wait_ge(x_hi, count)
                    dve.tensor_tensor(lo[0:64], xlo, hi[0:64].bitcast(F32), ALU.subtract)
                    dve.tensor_tensor(lo[64:128, :, 1:SEQ], xhi[:, :, 0:SEQ - 1], hi[64:128, :, 1:SEQ].bitcast(F32),
                                      ALU.subtract).then_inc(x_split, 1)

                dve.memset(xh[64:128, :, :, 0:1].bitcast(F32), 0.0)
                dve.memset(xl[64:128, :, :, 0:1].bitcast(F32), 0.0)
                split_x(0, 0, dve.snap(l * (GROUPS + 1) + (CREDIT + 1)))

                def turn(n, o, par, g, x_base):
                    prev, cur, nxt = o

                    def products(j, q):
                        dve.wait_ge(qk_proj, n.n16 + (16 * q + j + 1))
                        if 16 * q + j - 1 >= 0 or prev is not None:
                            dve.wait_ge(qk_rot, n.n16 + (16 * q + j - 1))
                        for i in range(2):
                            ins = dve.tensor_tensor(seqs(ab[:, j % 2, i, :]), seqs(use_bank("qk", j)[:, :]),
                                                    ltab[:, 2 * (j % 2) + i:2 * (j % 2) + i + 1, :]
                                                    .to_broadcast([P, GB, SEQ]), ALU.mult)
                        ins.then_inc(qk_mul, 1)

                    def scale_k(p, q):
                        dve.wait_ge(qk_rot, n.n16 + (16 * q + 2 * p + 2))
                        dve.wait_ge(rk_bc, n.n8 + (8 * q + p + 1))
                        dve.tensor_tensor(rot[:, PAIRS + p, :], rot[:, PAIRS + p, :], use_bank("rk", p)[:, :], ALU.mult)\
                            .then_inc(k_norm, 1)

                    def scale_q(h, q):
                        dve.wait_ge(rq_T, n.n2 + (2 * q + h + 1))
                        src = use_bank("rqT", h)[:, 0:P].rearrange("p (t r) -> p t r", t=4)[:, :, 0:8]
                        up = float(2 ** (R_LOG2 // 2)) * QK_SCALE
                        dve.tensor_scalar(rq[:, h, :, :], src, up, None, ALU.mult)
                        dve.tensor_scalar(nrq[:, h, :, :], src, -up, None, ALU.mult).then_inc(rq_sb, 1)

                    def residual(b, q):
                        dve.wait_ge(at_out, n.n2 + (2 * q + b + 1))
                        dst = xT[:, bass.ds((g + q) * GT + b * SEQ, SEQ)]
                        dve.tensor_tensor(dst, dst, use_bank("wo", b)[:, 0:SEQ], ALU.add).then_inc(at_add, 1)

                    def denominators(e, q):
                        dve.wait_ge(p_exp, n.n16 + (16 * q + e + 1))
                        dve.reciprocal(rden[:, e, :, :], den[:, e, :, :]).then_inc(p_rden, 1)

                    def copy_probs(e, q):
                        dve.wait_ge(p_T, n.n16 + (16 * q + e + 1))
                        if 16 * q + e - 1 >= 0 or prev is not None:
                            dve.wait_ge(o_ps, n.n16 + (16 * q + e - 1))
                        dve.transpose(pp[96:128, e % 2, :, :], pr[0:32, e % 4, :, P:P + WINDOW])
                        dve.tensor_copy(pt[:, e % 2, :, :].rearrange("p i c -> p (i c)"), bank[2][:, :])\
                            .then_inc(p_Tsb, 1)

                    def maxima(s):
                        p, b = s // 2, s % 2
                        for i in range(2):
                            u = 2 * s + i
                            scores = held(dve, n.n32 + (u + 1))
                            used = held(dve, n.n16 + (s - 1 if s >= 2 or prev is not None else 0))
                            settle(dve)
                            dve.wait_ge(sc_ps, scores)
                            if i == 0:
                                dve.wait_ge(p_exp, used)
                            for t in range(2):
                                cs = slice(0, P) if t == 0 else slice(P, UW)
                                ins = dve.tensor_tensor_reduce(sm[:, s % 2, i, cs], bank[i][:, cs], mask[:, cs],
                                                               1.0, -3e38, ALU.add, ALU.max, mx[:, s, t, i:i + 1])
                            ins.then_inc(sc_max, 1)
                        dve.wait_ge(sc_max, n.n32 + (2 * s + 2))
                        if s % 8 == 0:
                            dve.wait_ge(rq_sb, n.n2 + (s // 8 + 1))
                        dve.tensor_tensor(nb[:, s, :, :], mx[:, s, :, :], head_scale(nrq, p, b), ALU.mult)\
                            .then_inc(sc_bias, 1)

                    def clamp(h, q):
                        rows = slice(64 * h, 64 * h + 64)
                        dve.wait_ge(sq_part, n.n8 + (8 * q + 4 * h + 4))
                        dve.tensor_scalar(rsum[rows, :], bank[7][rows, :], 1e-24, None, ALU.max).then_inc(sq_clamp, 1)

                    def split_norms(h, q):
                        rows = slice(64 * h, 64 * h + 64)
                        dve.wait_ge(r_exp, n.n2 + (2 * q + h + 1))
                        dve.tensor_copy(nh[rows, :], rsum[rows, :]).then_inc(r_hi, 1)
                        dve.wait_ge(r_hi, n.n2 + (2 * q + h + 1))
                        dve.tensor_tensor(nl[rows, :], rsum[rows, :], nh[rows, :].bitcast(F32), ALU.subtract)\
                            .then_inc(r_split, 1)

                    for s in range(DRAIN if cur is None and nxt is None else 16):
                        if s < 2 and prev is not None:
                            denominators(s + 14, prev)
                        if s >= 2 and cur is not None:
                            denominators(s - 2, cur)
                        if s < 4 and prev is not None:
                            copy_probs(s + 12, prev)
                        if s >= 4 and cur is not None:
                            copy_probs(s - 4, cur)
                        if s == 0 and cur is not None:
                            products(15, cur)
                        if s >= 1 and nxt is not None:
                            products(s - 1, nxt)
                        for role, kind, i in BANK_STEPS[s - 1] if s else ():
                            q = group_of(role, o)
                            if q is not None and kind == "rqT":
                                scale_q(i, q)
                            if q is not None and kind == "rk":
                                scale_k(i, q)
                            if q is not None and kind == "wo":
                                residual(i, q)
                        if cur is not None:
                            maxima(s)
                        if s == 1 and cur is not None:
                            clamp(1, cur)
                        if s == 2 and cur is not None:
                            split_norms(1, cur)
                        if s == 9 and nxt is not None:
                            clamp(0, nxt)
                        if s == 10 and nxt is not None:
                            split_norms(0, nxt)
                            if cur is not None:
                                dve.wait_ge(v_proj, n.n8 + 8)
                                split_x(g + 2, par, x_base + 3)
                            else:
                                split_x(1, 1, x_base + 2)

                layer_turns(dve, l, turn)
                with dve.Fori(0, GROUPS // LNG) as g2:
                    i4 = dve.snap((l * (GROUPS // LNG) + g2) * LNG + CREDIT)
                    for k in range(LNG):
                        xlo = seqs(xT[0:64, bass.ds((g2 * LNG + k) * GT, GT)])
                        xhi = seqs(xT[64:128, bass.ds((g2 * LNG + k) * GT, GT)])
                        dve.wait_ge(at_add, (l + 1) * (2 * GROUPS) + CREDIT)
                        dve.wait_ge(l_xn, i4)
                        dve.memset(seqs(lnx[k])[64:128, :, 0:1], 0.0)
                        dve.tensor_copy(seqs(lnx[k])[0:64, :, :], xlo)
                        dve.tensor_copy(seqs(lnx[k])[64:128, :, 1:SEQ], xhi[:, :, 0:SEQ - 1]).then_inc(l_sh, 1)
                    for k in range(LNG):
                        dve.wait_ge(l_mean, i4 + (k + 1))
                        dve.wait_ge(l_sh, i4 + (k + 1))
                        dve.tensor_tensor(lnx[k], lnx[k], bank[k][:, :], ALU.subtract).then_inc(l_xc, 1)
                    for k in range(LNG):
                        dve.wait_ge(l_rstd, i4 + (k + 1))
                        dve.wait_ge(l_xc, i4 + (k + 1))
                        dve.tensor_tensor(lnx[k], lnx[k], lny[k], ALU.mult).then_inc(l_mul, 1)
                    for k in range(LNG):
                        dve.wait_ge(l_mul, i4 + (k + 1))
                        dve.tensor_scalar(wide_f[:, bass.ds((g2 * LNG + k) * GT, GT)], lnx[k],
                                          lv[:, V_G:V_G + 1], lv[:, V_B:V_B + 1], ALU.mult, ALU.add).then_inc(l_xn, 1)
                with dve.Fori(0, GROUPS // FFG) as g2:
                    i4 = dve.snap((l * (GROUPS // FFG) + g2) * FFG + CREDIT)
                    i12 = dve.snap((l * (GROUPS // FFG) + g2) * FFS + CREDIT)

                    def split(k):
                        src = wide_f[:, bass.ds((g2 * FFG + k) * GT, GT)]
                        dve.wait_ge(l_xn, (l + 1) * GROUPS + CREDIT)
                        dve.wait_ge(f_up, i12 + 3 * max(k - 1, 0))
                        dve.tensor_copy(xh[:, k % 2, :, :], seqs(src)).then_inc(f_hi, 1)
                        dve.wait_ge(f_hi, i4 + (k + 1))
                        dve.tensor_tensor(xl[:, k % 2, :, :], seqs(src), xh[:, k % 2, :, :].bitcast(F32), ALU.subtract)\
                            .then_inc(f_split, 1)

                    def low(s):
                        cn = FCH[s % 3][1]
                        dve.wait_ge(f_hhi, i12 + (s + 1))
                        dve.tensor_tensor(hl[0:cn, s % 2, :], ab[0:cn, s % 2, 1, :], hh[0:cn, s % 2, :].bitcast(F32),
                                          ALU.subtract).then_inc(f_hlo, 1)

                    def residual(k):
                        dve.wait_ge(f_dn, i12 + (3 * k + 3))
                        dst = xT[:, bass.ds((g2 * FFG + k) * GT, GT)]
                        dve.scalar_tensor_tensor(dst, bank[6 + k % 2][:, :], lv[:, V_B2:V_B2 + 1], dst, ALU.add, ALU.add)\
                            .then_inc(f_add, 1)

                    split(0)
                    for s in range(FFS):
                        c = s % 3
                        cn = FCH[c][1]
                        if s % 3 == 1 and s // 3 + 1 < FFG:
                            split(s // 3 + 1)
                        dve.wait_ge(f_gelu, i12 + (s + 1))
                        if s >= 2:
                            dve.wait_ge(f_hlo, i12 + (s - 1))
                        dve.scalar_tensor_tensor(ab[0:cn, s % 2, 1, :], bank[2 * (s % 3)][0:cn, :],
                                                 lv[0:cn, V_B1A + c:V_B1A + c + 1], ab[0:cn, s % 2, 0, :],
                                                 ALU.add, ALU.mult).then_inc(f_h, 1)
                        low(s)
                        if s % 3 == 0 and s >= 3:
                            residual(s // 3 - 1)
                    residual(FFG - 1)
            dve.wait_ge(s_in, 32)
            with dve.Fori(0, GROUPS) as g:
                dve.wait_ge(g_silu, g + 1)
                dve.wait_ge(g_T, g + CREDIT)
                dve.tensor_tensor(ab[:, 1, 0, :], ab[:, 0, 0, :], rotw[:, bass.ds(TOKENS + g * GT, GT)], ALU.mult)\
                    .then_inc(g_mul, 1)
                dve.wait_ge(g_T, g + 1 + CREDIT)
                dst = rotw[:, bass.ds(g * GT, GT)]
                dve.tensor_tensor(dst, dst, bank[0][:, :], ALU.add).then_inc(g_out, 1)


def constants():
    half = np.arange(0, DH, 2, dtype=np.float32)
    inv_freq = (np.float32(1.0) / np.float32(10000.0) ** (half / np.float32(DH))).astype(np.float32)
    t = np.arange(SEQ, dtype=np.float32)
    freqs = t[:, None] * inv_freq[None, :]
    base = (half + np.float32(0.4 * DH)) / np.float32(1.4 * DH)
    power = (t - SEQ // 2) / np.float32(WINDOW // 2)
    scale = (base[None, :] ** power[:, None]).astype(np.float32)
    f = np.tile(freqs, (1, 4)).T
    s = np.tile(scale, (1, 4)).T
    sign = np.where(np.arange(P) % DH < DH // 2, -1.0, 1.0).astype(np.float32)[:, None]
    inv = (np.float32(1.0) / s).astype(np.float32)
    tabs = np.stack([np.cos(f) * s, -np.sin(f) * s * sign, np.cos(f) * inv, -np.sin(f) * inv * sign], 1)
    q = np.arange(P)[:, None]
    own = np.arange(P)[None, :]
    wide = np.arange(P + WINDOW)[None, :] - WINDOW

    def band(k):
        return np.where((k > q) | (k < q - WINDOW), MASKED, 0.0)

    mask = np.concatenate([band(own), band(wide)], 1)
    headsum = np.zeros((P, 4, 32))
    headpick = np.zeros((P, PAIRS, P))
    for p in range(4):
        for i in range(2):
            headsum[64 * i:64 * i + 64, p, 2 * p + i] = 1.0
    for p in range(4):
        for i in range(2):
            for half in range(2):
                headpick[64 * half + 32 + 2 * p + i, 4 * half + p, 64 * i:64 * i + 64] = 2.0 ** (R_LOG2 // 2)
    statepick = np.zeros((DT_RANK + 2 * D_STATE, 2 * D_STATE, P))
    for n in range(2 * D_STATE):
        statepick[DT_RANK + n, n, :] = 1.0
    return {k: np.ascontiguousarray(v.astype(np.float32)) for k, v in dict(
        tabs_c=tabs, mask_c=mask, ident_c=np.eye(P), headsum_c=headsum, headpick_c=headpick,
        statepick_c=statepick).items()}


def columns(*vectors):
    cols = []
    for v in vectors:
        c = np.zeros((P,), np.float32)
        c[:v.shape[0]] = v
        cols.append(c)
    return np.stack(cols, 1)


def kernel(**inputs):
    import concourse.bacc as bacc
    from concourse.bass_utils import run_bass_kernel_spmd as run

    i = {k: np.asarray(v) for k, v in inputs.items()}
    A, F = "L0_attn_", "L0_ffn_"
    cxw, czw = i[A + "conv_x_w"][:, 0, :], i[A + "conv_z_w"][:, 0, :]
    mvec = columns(*[cxw[k] for k in range(D_CONV)], *[czw[k] for k in range(D_CONV)], i[A + "conv_x_b"],
                   i[A + "conv_z_b"], i[A + "inv_dt"], i[A + "D"], i[A + "b_out"])
    lay = []
    for l in range(DEPTH):
        qs, ks, b1 = i[F + "q_scale"][l], i[F + "k_scale"][l], i[F + "b1"][l]
        lay.append(columns(np.tile(qs, 2), np.tile(ks, 2),
                           i[F + "ln_g"][l], i[F + "ln_b"][l], i[F + "b2"][l],
                           *[b1[c0:c0 + cn] for c0, cn in FCH], *[b1[FF + c0:FF + c0 + cn] for c0, cn in FCH]))
    arrays = dict(x_in=i[A + "x"], W_in=i[A + "W_in"], W_xdbl=i[A + "W_xdbl"], W_dt=i[A + "W_dt"],
                  W_out=i[A + "W_out"], mvec=mvec, Wqkv=i[F + "Wqkv"], Wo=i[F + "Wo"], W1=i[F + "W1"],
                  W2=i[F + "W2"], lvec=np.concatenate(lay, 1), **constants())
    arrays = {k: np.ascontiguousarray(v) for k, v in arrays.items()}
    nc = bacc.Bacc("TRN2", target_bir_lowering=False, num_devices=1)
    aps = {n: nc.dram_tensor(n, a.shape, mybir.dt.from_np(a.dtype), kind="ExternalInput").ap()
           for n, a in arrays.items()}
    out = nc.dram_tensor("out", (BATCH, SEQ, DIM), F32, kind="ExternalOutput").ap()
    build(nc, **aps, out=out)
    r = run(nc, [arrays], core_ids=[0])
    return r.results[0]["out"]
```
